# Optimizing a Trainium2 kernel written in Bass

```python
import numpy as np
import jax
import jax.numpy as jnp

def _softmax(x, axis=-1):
    return jax.nn.softmax(x, axis=axis)

def _gelu(x):
    return jax.nn.gelu(x, approximate=True)

def _silu(x):
    return jax.nn.silu(x)

def _sigmoid(x):
    return jax.nn.sigmoid(x)

def _layernorm(x, axis=-1, eps=1e-05):
    m = jnp.mean(x, axis=axis, keepdims=True)
    v = jnp.var(x, axis=axis, keepdims=True)
    return (x - m) / jnp.sqrt(v + eps)

def _scatter_add(tgt, idx, src, axis=0):
    return tgt.at[idx].add(src)

def _segment_sum(src, seg, n):
    return jax.ops.segment_sum(src, seg, n)
kernel_name = 'mk_hybrid_d1_jaxref_r8_059fbd'

def setup_inputs(seed: int=0):
    np.random.seed(seed)
    _w = jnp.asarray

    def _L0_attn_a_setup():
        import jax, jax.numpy as jnp
        import numpy as np
        D_MODEL = 128
        NUM_HEADS = 16
        MAX_LEN = 64
        BATCH = 2
        SEQ_LEN = 256

        def _mha(x, w_in, b_in, w_out, b_out, num_heads):
            *batch, S, d = x.shape
            hd = d // num_heads
            qkv = x @ w_in.T + b_in
            q, k, v = jnp.split(qkv, 3, axis=-1)

            def heads(t):
                return t.reshape(*batch, S, num_heads, hd)
            q, k, v = (heads(q), heads(k), heads(v))
            scale = 1.0 / np.sqrt(hd).astype(np.float32)
            scores = jnp.einsum('...qhd,...khd->...hqk', q, k) * scale
            attn = jax.nn.softmax(scores, axis=-1)
            o = jnp.einsum('...hqk,...khd->...qhd', attn, v).reshape(*batch, S, d)
            return o @ w_out.T + b_out
        key = jax.random.key(seed)
        ks = jax.random.split(key, 5)
        d = D_MODEL
        s = 0.02
        return {'x': jax.random.normal(ks[0], (BATCH, SEQ_LEN, d), dtype=jnp.float32), 'w_in_l': jax.random.normal(ks[1], (3 * d, d), dtype=jnp.float32) * s, 'b_in_l': jnp.zeros((3 * d,), jnp.float32), 'w_out_l': jax.random.normal(ks[2], (d, d), dtype=jnp.float32) * s, 'b_out_l': jnp.zeros((d,), jnp.float32), 'w_in_g': jax.random.normal(ks[3], (3 * d, d), dtype=jnp.float32) * s, 'b_in_g': jnp.zeros((3 * d,), jnp.float32), 'w_out_g': jax.random.normal(ks[4], (d, d), dtype=jnp.float32) * s, 'b_out_g': jnp.zeros((d,), jnp.float32)}
    _L0_attn_a_in = _L0_attn_a_setup()

    def _L0_attn_b_setup():
        import jax, jax.numpy as jnp
        import numpy as np
        D_MODEL = 128
        D_STATE = 128
        D_CONV = 4
        EXPAND = 2
        HEAD_DIM = 128
        NGROUPS = 1
        CHUNK = 32
        D_INNER = EXPAND * D_MODEL
        HEADS = D_INNER // HEAD_DIM
        D_IN_PROJ = 2 * D_INNER + 2 * NGROUPS * D_STATE + HEADS
        CONV_DIM = D_INNER + 2 * NGROUPS * D_STATE
        EPS = 1e-05

        def _segsum_exp(a):
            T = a.shape[-1]
            ac = jnp.cumsum(a, axis=-1)
            diff = ac[..., :, None] - ac[..., None, :]
            mask = jnp.tril(jnp.ones((T, T), dtype=bool))
            return jnp.where(mask, jnp.exp(jnp.where(mask, diff, 0.0)), 0.0)

        def _ssd(xdt, dA, Bmat, Cmat):
            b, L, h, p = xdt.shape
            nc, cs = (L // CHUNK, CHUNK)
            x_c = xdt.reshape(b, nc, cs, h, p)
            B_c = Bmat.reshape(b, nc, cs, -1)
            C_c = Cmat.reshape(b, nc, cs, -1)
            A_r = dA.reshape(b, nc, cs, h).transpose(0, 3, 1, 2)
            Lmat = _segsum_exp(A_r)
            Y_diag = jnp.einsum('bcin,bcjn,bhcij,bcjhp->bcihp', C_c, B_c, Lmat, x_c)
            A_cum = jnp.cumsum(A_r, axis=-1)
            decay_states = jnp.exp(A_cum[..., -1:] - A_cum)
            states = jnp.einsum('bcin,bhci,bcihp->bchpn', B_c, decay_states, x_c)
            chunk_decay = jnp.exp(A_cum[..., -1])

            def step(prev, inp):
                s, dec = inp
                new = prev * dec[..., None, None] + s
                return (new, prev)
            init = jnp.zeros((b, h, p, states.shape[-1]), dtype=xdt.dtype)
            _, prior = jax.lax.scan(step, init, (states.transpose(1, 0, 2, 3, 4), chunk_decay.transpose(2, 0, 1)))
            prior = prior.transpose(1, 0, 2, 3, 4)
            state_decay_out = jnp.exp(A_cum)
            Y_off = jnp.einsum('bcin,bchpn,bhci->bcihp', C_c, prior, state_decay_out)
            return (Y_diag + Y_off).reshape(b, L, h, p)
        key = jax.random.key(seed)
        ks = jax.random.split(key, 10)
        B, L = (2, 256)
        u = jax.random.normal(ks[0], (B, L, D_MODEL), dtype=jnp.float32)
        in_proj_w = jax.random.normal(ks[1], (D_IN_PROJ, D_MODEL), dtype=jnp.float32) * 0.02
        conv_w = jax.random.normal(ks[2], (CONV_DIM, 1, D_CONV), dtype=jnp.float32) * 0.2
        conv_b = jnp.zeros((CONV_DIM,), dtype=jnp.float32)
        dt = jnp.exp(jax.random.uniform(ks[3], (HEADS,)) * (np.log(0.1) - np.log(0.001)) + np.log(0.001))
        dt = jnp.clip(dt, 0.0001, None)
        dt_bias = (dt + jnp.log(-jnp.expm1(-dt))).astype(jnp.float32)
        A_log = jax.random.uniform(ks[4], (HEADS,), minval=np.log(0.001), maxval=np.log(0.999)).astype(jnp.float32)
        D_param = jax.random.uniform(ks[5], (HEADS,), minval=-0.5, maxval=0.5).astype(jnp.float32)
        norm_w = jnp.ones((D_INNER,), dtype=jnp.float32)
        out_proj_w = jax.random.normal(ks[6], (D_MODEL, D_INNER), dtype=jnp.float32) * 0.02
        out_proj_b = jnp.zeros((D_MODEL,), dtype=jnp.float32)
        return {'u': u, 'in_proj_w': in_proj_w, 'conv_w': conv_w, 'conv_b': conv_b, 'dt_bias': dt_bias, 'A_log': A_log, 'D_param': D_param, 'norm_w': norm_w, 'out_proj_w': out_proj_w, 'out_proj_b': out_proj_b}
    _L0_attn_b_in = _L0_attn_b_setup()

    def _L0_ffn_setup():
        import jax, jax.numpy as jnp
        import numpy as np
        key = jax.random.key(seed)
        ks = jax.random.split(key, 5)
        B, T, D, E = (4, 256, 128, 8)
        inputs = jax.random.normal(ks[0], (B, T, D), dtype=jnp.float32)
        Wr = jax.random.normal(ks[1], (D, E), dtype=jnp.float32) * 0.02
        br = jnp.zeros((E,), dtype=jnp.float32)
        W1 = jax.random.normal(ks[2], (E, D, D), dtype=jnp.float32) * 0.02
        b1 = jnp.zeros((E, D), dtype=jnp.float32)
        W2 = jax.random.normal(ks[3], (E, D, D), dtype=jnp.float32) * 0.02
        b2 = jnp.zeros((E, D), dtype=jnp.float32)
        return {'inputs': inputs, 'Wr': Wr, 'br': br, 'W1': W1, 'b1': b1, 'W2': W2, 'b2': b2}
    _L0_ffn_in = _L0_ffn_setup()
    _d = {'L0_attn_a_x': _L0_attn_a_in['x'], 'L0_attn_a_w_in_l': _L0_attn_a_in['w_in_l'], 'L0_attn_a_b_in_l': _L0_attn_a_in['b_in_l'], 'L0_attn_a_w_out_l': _L0_attn_a_in['w_out_l'], 'L0_attn_a_b_out_l': _L0_attn_a_in['b_out_l'], 'L0_attn_a_w_in_g': _L0_attn_a_in['w_in_g'], 'L0_attn_a_b_in_g': _L0_attn_a_in['b_in_g'], 'L0_attn_a_w_out_g': _L0_attn_a_in['w_out_g'], 'L0_attn_a_b_out_g': _L0_attn_a_in['b_out_g'], 'L0_attn_b_in_proj_w': _L0_attn_b_in['in_proj_w'], 'L0_attn_b_conv_w': _L0_attn_b_in['conv_w'], 'L0_attn_b_conv_b': _L0_attn_b_in['conv_b'], 'L0_attn_b_dt_bias': _L0_attn_b_in['dt_bias'], 'L0_attn_b_A_log': _L0_attn_b_in['A_log'], 'L0_attn_b_D_param': _L0_attn_b_in['D_param'], 'L0_attn_b_norm_w': _L0_attn_b_in['norm_w'], 'L0_attn_b_out_proj_w': _L0_attn_b_in['out_proj_w'], 'L0_attn_b_out_proj_b': _L0_attn_b_in['out_proj_b'], 'L0_ffn_Wr': _L0_ffn_in['Wr'], 'L0_ffn_br': _L0_ffn_in['br'], 'L0_ffn_W1': _L0_ffn_in['W1'], 'L0_ffn_b1': _L0_ffn_in['b1'], 'L0_ffn_W2': _L0_ffn_in['W2'], 'L0_ffn_b2': _L0_ffn_in['b2']}
    _x0 = _d['L0_attn_a_x']
    _d['L0_attn_a_x'] = jax.random.normal(jax.random.fold_in(jax.random.key(seed), 1), (8, 512, 128), dtype=_x0.dtype)
    del _x0
    return _d

def reference(L0_attn_a_x, L0_attn_a_w_in_l, L0_attn_a_b_in_l, L0_attn_a_w_out_l, L0_attn_a_b_out_l, L0_attn_a_w_in_g, L0_attn_a_b_in_g, L0_attn_a_w_out_g, L0_attn_a_b_out_g, L0_attn_b_in_proj_w, L0_attn_b_conv_w, L0_attn_b_conv_b, L0_attn_b_dt_bias, L0_attn_b_A_log, L0_attn_b_D_param, L0_attn_b_norm_w, L0_attn_b_out_proj_w, L0_attn_b_out_proj_b, L0_ffn_Wr, L0_ffn_br, L0_ffn_W1, L0_ffn_b1, L0_ffn_W2, L0_ffn_b2):

    def _L0_attn_a_ref(x, w_in_l, b_in_l, w_out_l, b_out_l, w_in_g, b_in_g, w_out_g, b_out_g):
        import jax, jax.numpy as jnp
        import numpy as np
        D_MODEL = 128
        NUM_HEADS = 16
        MAX_LEN = 64
        BATCH = 2
        SEQ_LEN = 256

        def _mha(x, w_in, b_in, w_out, b_out, num_heads):
            *batch, S, d = x.shape
            hd = d // num_heads
            qkv = x @ w_in.T + b_in
            q, k, v = jnp.split(qkv, 3, axis=-1)

            def heads(t):
                return t.reshape(*batch, S, num_heads, hd)
            q, k, v = (heads(q), heads(k), heads(v))
            scale = 1.0 / np.sqrt(hd).astype(np.float32)
            scores = jnp.einsum('...qhd,...khd->...hqk', q, k) * scale
            attn = jax.nn.softmax(scores, axis=-1)
            o = jnp.einsum('...hqk,...khd->...qhd', attn, v).reshape(*batch, S, d)
            return o @ w_out.T + b_out
        B, S, d = x.shape
        cs = MAX_LEN
        nc = S // cs
        xc = x.reshape(B, nc, cs, d).transpose(0, 2, 1, 3)
        loc = _mha(xc, w_in_l, b_in_l, w_out_l, b_out_l, NUM_HEADS)
        loc = loc.transpose(2, 0, 1, 3).reshape(B, S, d)
        return _mha(loc, w_in_g, b_in_g, w_out_g, b_out_g, NUM_HEADS)

    def _L0_attn_b_ref(u, in_proj_w, conv_w, conv_b, dt_bias, A_log, D_param, norm_w, out_proj_w, out_proj_b):
        import jax, jax.numpy as jnp
        import numpy as np
        D_MODEL = 128
        D_STATE = 128
        D_CONV = 4
        EXPAND = 2
        HEAD_DIM = 128
        NGROUPS = 1
        CHUNK = 32
        D_INNER = EXPAND * D_MODEL
        HEADS = D_INNER // HEAD_DIM
        D_IN_PROJ = 2 * D_INNER + 2 * NGROUPS * D_STATE + HEADS
        CONV_DIM = D_INNER + 2 * NGROUPS * D_STATE
        EPS = 1e-05

        def _segsum_exp(a):
            T = a.shape[-1]
            ac = jnp.cumsum(a, axis=-1)
            diff = ac[..., :, None] - ac[..., None, :]
            mask = jnp.tril(jnp.ones((T, T), dtype=bool))
            return jnp.where(mask, jnp.exp(jnp.where(mask, diff, 0.0)), 0.0)

        def _ssd(xdt, dA, Bmat, Cmat):
            b, L, h, p = xdt.shape
            nc, cs = (L // CHUNK, CHUNK)
            x_c = xdt.reshape(b, nc, cs, h, p)
            B_c = Bmat.reshape(b, nc, cs, -1)
            C_c = Cmat.reshape(b, nc, cs, -1)
            A_r = dA.reshape(b, nc, cs, h).transpose(0, 3, 1, 2)
            Lmat = _segsum_exp(A_r)
            Y_diag = jnp.einsum('bcin,bcjn,bhcij,bcjhp->bcihp', C_c, B_c, Lmat, x_c)
            A_cum = jnp.cumsum(A_r, axis=-1)
            decay_states = jnp.exp(A_cum[..., -1:] - A_cum)
            states = jnp.einsum('bcin,bhci,bcihp->bchpn', B_c, decay_states, x_c)
            chunk_decay = jnp.exp(A_cum[..., -1])

            def step(prev, inp):
                s, dec = inp
                new = prev * dec[..., None, None] + s
                return (new, prev)
            init = jnp.zeros((b, h, p, states.shape[-1]), dtype=xdt.dtype)
            _, prior = jax.lax.scan(step, init, (states.transpose(1, 0, 2, 3, 4), chunk_decay.transpose(2, 0, 1)))
            prior = prior.transpose(1, 0, 2, 3, 4)
            state_decay_out = jnp.exp(A_cum)
            Y_off = jnp.einsum('bcin,bchpn,bhci->bcihp', C_c, prior, state_decay_out)
            return (Y_diag + Y_off).reshape(b, L, h, p)
        b, L, _ = u.shape
        zxbcdt = u @ in_proj_w.T
        z = zxbcdt[..., :D_INNER]
        xBC = zxbcdt[..., D_INNER:D_INNER + CONV_DIM]
        dt = zxbcdt[..., D_INNER + CONV_DIM:]
        dt = jax.nn.softplus(dt + dt_bias)
        xBC_t = xBC.transpose(0, 2, 1)
        xBC_t = jax.lax.conv_general_dilated(xBC_t, conv_w, window_strides=(1,), padding=[(D_CONV - 1, 0)], dimension_numbers=('NCH', 'OIH', 'NCH'), feature_group_count=CONV_DIM)
        xBC = jax.nn.silu(xBC_t.transpose(0, 2, 1) + conv_b)
        x = xBC[..., :D_INNER].reshape(b, L, HEADS, HEAD_DIM)
        Bmat = xBC[..., D_INNER:D_INNER + NGROUPS * D_STATE]
        Cmat = xBC[..., D_INNER + NGROUPS * D_STATE:]
        A = -jnp.exp(A_log)
        y = _ssd(x * dt[..., None], dt * A, Bmat, Cmat)
        y = y + D_param[None, None, :, None] * x
        y = y.reshape(b, L, D_INNER)
        y = y * jax.nn.silu(z)
        y = y * jax.lax.rsqrt(jnp.mean(y * y, axis=-1, keepdims=True) + EPS) * norm_w
        return y @ out_proj_w.T + out_proj_b

    def _L0_ffn_ref(inputs, Wr, br, W1, b1, W2, b2):
        import jax, jax.numpy as jnp
        import numpy as np
        B, T, D = inputs.shape
        E = Wr.shape[1]
        x = inputs.reshape(B * T, D)
        N = x.shape[0]
        C = N // E
        logits = x @ Wr + br
        probs = jax.nn.softmax(logits, axis=-1)
        gate = jnp.max(probs, axis=-1, keepdims=True)
        idx = jnp.argmax(probs, axis=-1)
        mask = jax.nn.one_hot(idx, E, dtype=jnp.float32)
        pos = (jnp.cumsum(mask, axis=0) * mask).astype(jnp.int32)
        mask = mask * (pos < C).astype(jnp.float32)
        mask_flat = jnp.sum(mask, axis=-1, keepdims=True)
        gate = gate * mask_flat
        combine = (gate * mask_flat * jax.nn.one_hot(idx, E, dtype=jnp.float32))[..., None] * jax.nn.one_hot(pos, C, dtype=jnp.float32)
        dispatch = combine
        expert_in = jnp.einsum('nd,nec->ecd', x, dispatch)
        h = jax.nn.relu(jnp.einsum('ecd,edf->ecf', expert_in, W1) + b1[:, None, :])
        eo = jnp.einsum('ecf,efd->ecd', h, W2) + b2[:, None, :]
        out = jnp.einsum('ecd,nec->nd', eo, combine)
        return out.reshape(B, T, D)
    x = L0_attn_a_x
    x = x + _L0_attn_a_ref(_layernorm(x, axis=-1), L0_attn_a_w_in_l, L0_attn_a_b_in_l, L0_attn_a_w_out_l, L0_attn_a_b_out_l, L0_attn_a_w_in_g, L0_attn_a_b_in_g, L0_attn_a_w_out_g, L0_attn_a_b_out_g)
    x = x + _L0_ffn_ref(_layernorm(x, axis=-1), L0_ffn_Wr, L0_ffn_br, L0_ffn_W1, L0_ffn_b1, L0_ffn_W2, L0_ffn_b2)
    x = x + _L0_attn_b_ref(_layernorm(x, axis=-1), L0_attn_b_in_proj_w, L0_attn_b_conv_w, L0_attn_b_conv_b, L0_attn_b_dt_bias, L0_attn_b_A_log, L0_attn_b_D_param, L0_attn_b_norm_w, L0_attn_b_out_proj_w, L0_attn_b_out_proj_b)
    x = x + _L0_ffn_ref(_layernorm(x, axis=-1), L0_ffn_Wr, L0_ffn_br, L0_ffn_W1, L0_ffn_b1, L0_ffn_W2, L0_ffn_b2)
    return x

_drawn_inputs = setup_inputs


def setup_inputs(seed=0):
    import zlib

    import numpy as np

    out = dict(_drawn_inputs(seed))
    spreads = {'L0_attn_a_b_in_l': (0.0, 0.8),
     'L0_attn_a_b_out_l': (0.0, 0.8),
     'L0_attn_a_b_in_g': (0.0, 0.362),
     'L0_attn_a_b_out_g': (0.0, 0.1),
     'L0_attn_b_conv_b': (0.0, 0.1),
     'L0_attn_b_norm_w': (1.0, 0.6),
     'L0_attn_b_out_proj_b': (0.0, 0.1),
     'L0_ffn_br': (0.0, 0.297),
     'L0_ffn_b1': (0.0, 0.8),
     'L0_ffn_b2': (0.0, 0.311)}
    factors = {'L0_attn_a_w_in_l': 8.0,
     'L0_attn_a_w_out_l': 8.0,
     'L0_attn_a_w_in_g': 8.0,
     'L0_ffn_W1': 8.0,
     'L0_ffn_W2': 8.0,
     'L0_attn_b_A_log': 29.776}
    for name, (base, spread) in spreads.items():
        noise = np.random.default_rng([zlib.crc32(name.encode()), seed]).standard_normal(out[name].shape)
        drawn = base * np.exp(spread * noise) if base else spread * noise
        out[name] = jnp.asarray(drawn.astype(out[name].dtype))
    for name, factor in factors.items():
        out[name] = (out[name] * factor).astype(out[name].dtype)
    return out
```

```python
from contextlib import ExitStack

import concourse.bass as bass
from concourse import mybir

F32 = mybir.dt.float32
BF16 = mybir.dt.bfloat16
U32 = mybir.dt.uint32
ALU = mybir.AluOpType
ACT = mybir.ActivationFunctionType
AX = mybir.AxisListType

P = 128
B = 8
S = 512
D = 128
T = S // P
H = 16
HD = D // H
NG = 4
NJ = H // NG
W = 64
NC = S // W
PR = B // 2
SCALE = HD ** -0.5
EPS = 1e-5
NPART = 3
PROD = NPART * NPART * HD
KA = PROD + NPART
LOADS = NPART * (1 + NPART)
STEPS = NG * T
SC = 4 * STEPS
DVE_C = (0, 3, 6)
POOL_C = (1, 2, 4, 5, 7)
E = 8
NT = B * T
CAP = B * S // E
H2 = 2
TAPS = 4
FREE = 1
R = 3


class Count:

    def __init__(self, i, a, b, eng, made=None):
        self.i, self.a, self.b, self.eng = i, a, b, eng
        self.made = {} if made is None else made

    def __add__(self, n):
        return Count(self.i, self.a, self.b + n, self.eng, self.made)

    def __sub__(self, n):
        return self + -n

    def __mul__(self, n):
        return Count(self.i, self.a * n, self.b * n, self.eng, self.made)

    __radd__, __rmul__ = __add__, __mul__

    def value(self):
        if self.a not in self.made:
            self.made[self.a] = self.eng.snap(self.i * self.a)
        return self.made[self.a] + self.b


def v(x):
    return x.value() if isinstance(x, Count) else x


def build(nc, a, out):
    ctx = ExitStack()
    with ctx:
        def sb(name, shape, dt=F32):
            return ctx.enter_context(nc.sbuf_tensor(name, shape, dt))

        def sem(name):
            return ctx.enter_context(nc.semaphore(name))

        class Chain:

            def __init__(self, eng, name):
                self.eng, self.sem, self.base, self.n = eng, sem(name), 0, 0

            def __call__(self, ins):
                self.n += 1
                ins.then_inc(self.sem, 1)

            def settle(self):
                self.eng.wait_ge(self.sem, v(self.base + self.n))

        def loop(eng, count, body, chain=None, per=0):
            if chain is not None:
                b0 = chain.base + chain.n
            with eng.Fori(0, count) as i:
                if chain is not None:
                    chain.base, chain.n = Count(i, per, b0, eng), 0
                body(i)
                if chain is not None:
                    assert chain.n == per, (chain.n, per)
            if chain is not None:
                chain.base, chain.n = 0, b0 + count * per

        xf = a["attn_a_x"]
        parts_dram = [nc.dram_tensor(f"parts_{w}", (B, NPART * HD, H, S), BF16).ap() for w in "qk"]

        ident = sb("ident", [P, P])
        identb = sb("identb", [P, P], BF16)
        wT = {k: sb(f"wT_{k}", [P, 3, P]) for k in "lg"}
        woT = {k: sb(f"woT_{k}", [P, P]) for k in "lg"}
        b_qk_l = sb("b_qk_l", [1, 2 * D])
        ones_row = sb("ones_row", [1, P])
        b_qk_g = sb("b_qk_g", [P, 2])
        b_v = {k: sb(f"b_v_{k}", [P, 1]) for k in "lg"}
        b_out_l = sb("b_out_l", [P, 1])
        bias_l = sb("bias_l", [P, 1])
        b_out_g = sb("b_out_g", [P, D])
        bias_g = sb("bias_g", [P, D])
        halfneg = sb("halfneg", [P, 64])
        eps = sb("eps", [P, T])
        x1 = sb("x1", [P, (B + 1) * T, D])
        locT = sb("locT", [P, B, S])

        WORDS = 41472
        arena = sb("arena", [P, WORDS])

        class Lay:
            def __init__(self):
                self.at = 0

            def __call__(self, shape, dt=F32, rows=P):
                n, per = 1, 2 if dt == BF16 else 1
                for x in shape:
                    n *= x
                words = -(-n // per)
                w = arena[0:rows, self.at:self.at + words]
                self.at += words
                assert self.at <= WORDS, self.at
                if dt != F32:
                    w = w.bitcast(dt)
                names = "abcd"[:len(shape)]
                if len(shape) > 1:
                    w = w.rearrange("p (" + " ".join(names) + ") -> p " + " ".join(names),
                                    **{x: y for x, y in zip(names, shape)})
                return w

        lay = Lay()
        xb = [lay([NC, D]) for p in range(2)]
        xn = [lay([NC, D]) for p in range(2)]
        xT = [lay([NC, P]) for p in range(2)]
        qkv = lay([PR, NC, 3 * D])
        prod_p = [lay([NC, D]) for p in range(2)]
        prod_d = [lay([NC, D]) for p in range(len(DVE_C))]
        sc = lay([NC, H, NC])
        sx = lay([NC, H, NC])
        pe_ = lay([NC, H, NC])
        o_l = lay([NC, D])
        oT_l = lay([NC, P])
        smax = lay([NC, H])
        ssum = lay([NC, H])
        srec = lay([NC, H])
        st6 = lay([NC, 6])
        mv = [lay([NC, 2]) for p in range(2)]
        ve = lay([NC])
        rs = [lay([NC]) for p in range(2)]
        w_nat = {k: lay([3, P]) for k in "lg"}
        wo_nat = {k: lay([P]) for k in "lg"}
        lay = Lay()
        qpk = [lay([H, S], BF16, KA) for r in range(R)]
        kpk = [lay([H, S], BF16, KA) for r in range(R)]
        va = [lay([T, H, 32]) for r in range(R)]
        eb = [lay([S]) for r in range(8)]
        xs = lay([S])
        ff = [lay([S]) for w in "qk"]
        rres = lay([S])
        parts = [lay([NPART, S], BF16) for w in "qk"]
        mx = [lay([T, H]) for r in range(R)]
        nr = lay([T, NJ])
        nm = [lay([NG, T, NPART * NJ], BF16) for r in range(R)]
        mrow = [lay([S], BF16, NPART * NJ) for g in range(2)]
        ou = [lay([S]) for g in range(2)]
        rc = lay([T, NJ])
        on = lay([T, D])
        onT = lay([S])

        lay = Lay()
        f_xn = [lay([T, D]) for p in range(2)]
        f_xT = [lay([S]) for p in range(2)]
        f_st = lay([T, 6])
        f_mv = lay([NT, 2])
        f_mv4 = lay([T, 2])
        f_ve = lay([T])
        f_rs = lay([NT])
        f_lg = lay([NT, E])
        f_m = lay([NT])
        f_ex = lay([NT, E])
        f_sum = lay([NT])
        f_gate = lay([NT])
        f_pick = lay([NT, E])
        f_one = lay([E, NT])
        f_oneb = lay([E, NT], BF16)
        f_incl = lay([E * NT])
        f_pos = lay([E, NT])
        f_at = lay([NT])
        f_e0 = lay([NT])
        f_keep = lay([NT])
        f_slot = lay([NT])
        f_si = lay([NT])
        f_gi = lay([NT])
        f_rg = lay([NT])
        f_gk = lay([NT])
        f_xg = [lay([T, D]) for p in range(2)]
        f_i4 = [lay([T], U32) for p in range(2)]
        f_g4 = [lay([T]) for p in range(2)]
        f_xe = [lay([T, D]) for p in range(2)]
        f_w = [lay([2, D]) for p in range(2)]
        f_b1 = lay([E])
        f_b2 = lay([E, D])
        f_xeT = [lay([S]) for p in range(2)]
        f_hT = [lay([S]) for p in range(2)]
        f_ye = [lay([T, D]) for p in range(2)]
        f_yg = [lay([T, D]) for p in range(2)]
        lay = Lay()
        zn = lay([2, P])
        xbn = lay([4, P])
        dtn = lay([P], F32, H2)
        on_nat = lay([2 * P])
        wz = lay([2 * P + H2])
        wx = lay([4, P])
        wo2 = lay([2, P])
        cwf = lay([4, TAPS])
        cw = lay([4, TAPS])
        cbf = lay([4])
        cb = lay([4])
        nw = lay([2])
        dtb = lay([H2])
        alog = lay([H2])
        aneg = lay([H2])
        dpar = lay([H2])
        ob = lay([D])
        after = lay([P])
        m_st = lay([T, 6])
        m_mv = lay([T, 2])
        m_ve = lay([T])
        m_rs = lay([T])
        m_xn = lay([T, D])
        m_xT = lay([S])
        m_acc = lay([4, S])
        m_th = lay([4, S])
        m_ch = [lay([4, S]) for p in range(2)]
        m_zt = lay([T, 2 * P])
        m_g = [lay([T, 2 * P]) for p in range(2)]
        m_raw = [lay([T, H2]) for p in range(2)]
        m_abs = lay([T, H2])
        m_u = lay([T, H2])
        m_pos = lay([T, H2])
        m_s = lay([T, H2])
        m_s2 = lay([T, H2])
        m_q = lay([T, H2])
        m_dt = lay([T, H2])
        m_dA = lay([T, H2])
        m_wj = lay([T, H2])
        m_xtok = lay([T, H2, P])
        m_btok = lay([T, P])
        m_L = lay([T, H2, P])
        m_erow = lay([T, H2, P])
        m_el = lay([T, H2, P])
        m_ce = lay([T, H2, P])
        m_gm = lay([T, P])
        m_m = lay([T, H2, P])
        m_xst = lay([T - 1, H2, P])
        m_S = lay([T - 1, H2, P])
        m_y1 = lay([T, H2, P])
        m_y = lay([T, 2 * P])
        m_sq = lay([2 * P])
        m_ssq = lay([T])
        m_rv = lay([T])
        m_ri = lay([T])
        m_yT = lay([2, S])
        W_IN = ([(zn[:, c], P, P) for c in range(2)] + [(xbn[:, c], P, P) for c in range(4)] + [(dtn, H2, P)]
                + [(on_nat[:, k * P:(k + 1) * P], P, P) for k in range(2)])
        W_EVAC = ([(wz[:, c * P:(c + 1) * P], c, P, P) for c in range(2)] + [(wx[:, c], 2 + c, P, P) for c in range(4)]
                  + [(wz[:, 2 * P:], 6, P, H2), (wo2[:, 0], 7, P, P), (wo2[:, 1], 0, P, P)])
        slot_x = nc.dram_tensor("slot_x", (E * CAP, D), F32).ap()
        slot_y = nc.dram_tensor("slot_y", (E * CAP, D), F32).ap()
        wr = sb("wr", [P, E])
        br = sb("br", [P, E])
        prefer = sb("prefer", [P, E])
        first_slot = sb("first_slot", [P, E])
        not_first = sb("not_first", [P, E, NT])
        upto = sb("upto", [P, P])
        uptob = sb("uptob", [P, P], BF16)
        onesb = sb("onesb", [P, P], BF16)
        zeros = sb("zeros", [P, D])

        ps = ctx.enter_context(nc.psum_tensor("ps", [P, 8, S], F32))
        ST, SS, PV, M = 0, 3, 6, 7
        ps_mb = ps[:, M, :].bitcast(BF16)

        names = ["weights_in", "residual_in", "identity_ready", "constants_ready", "bf_identity_ready", "weight_transposes",
                 "weight_evacuations", "bias_made", "x1_biased",
                 "lxb_in0", "lxb_in1", "l_mv", "l_rs", "l_xn", "l_xnT", "l_xTs", "l_proj", "l_qkv", "l_prod_pool",
                 "l_prod_dve", "l_prod_d_used", "l_shift", "l_exp", "l_acc",
                 "l_o", "l_oT", "l_oTs", "l_out", "l_loc", "l_qk_used",
                 "ones_rows", "values_ready", "dummy_ready", "s", "max", "nm", "mrow", "st", "exp", "pv", "ou", "xs", "p1",
                 "parts_q", "parts_k", "stored", "pk0", "pk1", "pk2", "mr0", "mr1", "mr2", "mr3", "rc",
                 "m_full", "m_free", "waited", "out_stored", "moe_const", "upto_ones", "slots_cleared"]
        K = {n: sem(n) for n in names}

        FN = ["mv", "rs", "xn", "xnT", "xTs", "logits", "shift", "exp", "onehot", "counts", "routed", "xg", "scat0", "scat1",
              "exp_b", "ex0", "ex1", "xe_T", "xeTs", "h", "hT", "y", "ye", "st0", "st1", "gidx", "gath0", "gath1", "x"]
        for n_ in FN:
            K["e_" + n_] = sem(f"moe_{n_}")
        ADDS = dict({n_: 8 for n_ in FN}, shift=1, exp=1, onehot=1, counts=1, routed=1, exp_b=32)
        for p in range(2):
            ADDS.update({f"scat{p}": 16 * NT // 2, f"gath{p}": 16 * NT // 2, f"ex{p}": 48 * E // 2, f"st{p}": 16 * E // 2})

        E_FREE = ("xnT", "xTs", "logits", "xeTs", "hT", "ye", "st0", "st1")

        def run(f, name):
            return ADDS[name] * f + (FREE if name in E_FREE else 0)

        MN = ["w", "wT", "wTs", "cw", "cst", "mv", "rs", "xn", "xT", "xTs", "proj", "acc", "conv", "th", "silu", "z", "zt", "zg", "abs", "u", "dA",
              "xtok", "xtoks", "btok", "btoks", "g", "gm", "L", "row", "dif", "erow", "el", "wj", "xst", "m", "ce", "P", "S", "Y",
              "y1", "y", "ssq", "ri", "yT", "yTs", "out", "x", "bias"]
        for n_ in MN:
            K["m_" + n_] = sem("mamba_" + n_)

        block = ctx.enter_context(nc.Block())

        ORDER = "bffbffbbffbfbfb"

        def mamba(eng, front, back, chain=None, per=0):
            def both(b, p):
                f, g = front(b + 1, 1 - p), back(b, p)
                for s_ in ORDER:
                    next(f if s_ == "f" else g)

            for _ in front(0, 0):
                pass

            def two(i):
                for p in range(2):
                    both(Count(i, 2, p, eng), p)
            loop(eng, B // 2 - 1, two, chain, per)
            both(B - 2, 0)
            for _ in back(B - 1, 1):
                pass


        def apart(eng):
            eng.sem_inc(K["waited"], 1)

        def free_at(c):
            return STEPS * (c + 1)

        PV0 = R * STEPS
        MAX0 = (1 + R) * SC

        def prev_use(q):
            return q - 3 if q >= 3 else max(x for x in range(SC) if x % 3 == q % 3) - SC

        TASKS = [(1, "mt3"), (2, "ot3"), (3, "aq"), (4, "tt"), (5, "mt0"), (6, "ot0"), (7, "dd"), (8, "ak"),
                 (9, "mt1"), (10, "ot1"), (11, "av"), (13, "mt2"), (14, "ot2")]
        PRO = 6 + 3

        def tasks(n_next, n_after):
            return [(n, t) for n, t in TASKS
                    if (n_next or t not in ("mt0", "mt1", "mt2")) and (n_after or t[0] != "a")]

        def m_base(b):
            if isinstance(b, int) and b == B - 1:
                return PRO + len(TASKS) * (B - 2) + len(tasks(True, False))
            if isinstance(b, int) and b == B:
                return m_base(B - 1) + len(tasks(False, False))
            return PRO + len(TASKS) * b

        def bc(t, n):
            return t.rearrange("p a (b o) -> p a b o", o=1).broadcast_to([P, t.shape[1], t.shape[2], n])

        def qk_product(eng, i, c, dst):
            q = qkv[:, bass.ds(i, 1), c, 0:D].broadcast_to([P, NC, D])
            k = qkv[:, bass.ds(i, 1), :, D:2 * D].rearrange("p o c d -> p (o c) d")
            return eng.tensor_tensor(dst, q, k, ALU.mult)

        def pv_product(eng, i, c, dst):
            vals = qkv[:, bass.ds(i, 1), :, 2 * D:3 * D].rearrange("p o c (h d) -> p (o c) h d", h=H)
            pr = pe_[:, c].rearrange("p h (c o) -> p c h o", o=1).broadcast_to([P, NC, H, HD])
            return eng.tensor_tensor(dst.rearrange("p c (h d) -> p c h d", h=H), vals, pr, ALU.mult)

        def halves(eng, half, chain=None, per=0):
            def three(i):
                for r in range(R):
                    half(Count(i, R, r, eng), r, True, True)
            loop(eng, 2, three, chain, per)
            half(6, 0, True, False)
            half(7, 1, False, False)

        @block.sync
        def _(sp):
            for s_ in ("l_acc", "l_proj", "l_xnT", "l_oT", "l_o", "l_loc", "l_xTs", "l_qkv", "ou", "m_y1", "m_yTs", "m_x", "mr0", "mr1", "mr2", "mr3", *("e_" + x for x in E_FREE)):
                sp.sem_inc(K[s_], FREE)
            n = 0
            def ld(dst, src, **how):
                nonlocal n
                sp.dma_start(dst, src, **how).then_inc(K["weights_in"], 16)
                n += 1

            def load_x(pr, p):
                for h in range(2):
                    sp.dma_start(xb[p][h * W:(h + 1) * W],
                                 xf[bass.ds(pr * 2 + h, 1)].rearrange("o (c i) d -> i (o c) d", i=W)
                                 ).then_inc(K[f"lxb_in{p}"], 16)
            for p in range(2):
                load_x(p, p)
            for k in "lg":
                ld(w_nat[k][:], a[f"attn_a_w_in_{k}"].rearrange("(c p) d -> p c d", p=P))
                ld(wo_nat[k][:], a[f"attn_a_w_out_{k}"])
                bi = a[f"attn_a_b_in_{k}"]
                ld(b_v[k][:], bi[2 * D:3 * D].rearrange("(p o) -> p o", o=1))
            ld(b_qk_l[:], a["attn_a_b_in_l"][0:2 * D].rearrange("(o d) -> o d", o=1))
            for c in range(2):
                for d in range(HD):
                    ld(b_qk_g[d * H:(d + 1) * H, c:c + 1],
                       a["attn_a_b_in_g"][c * D:(c + 1) * D].rearrange("(h d one) -> d h one", h=H, one=1)[d],
                       allow_slow_non_contiguous=True)
            ld(b_out_l[:], a["attn_a_b_out_l"].rearrange("(p o) -> p o", o=1))
            ld(b_out_g[:], a["attn_a_b_out_g"].rearrange("(o d) -> o d", o=1).broadcast_to([P, D]))
            ld(wr[:], a["ffn_Wr"])
            ld(br[:], a["ffn_br"].rearrange("(o d) -> o d", o=1).broadcast_to([P, E]))
            assert n == N_WEIGHTS, n
            sp.dma_start(x1[:, T:], xf.rearrange("b (t p) d -> p (b t) d", p=P)).then_inc(K["residual_in"], 16)
            for p in range(2):
                sp.wait_ge(K["l_xn"], v(p + 1))
                load_x(2 + p, p)

            def pack(c, r):
                for w in range(2):
                    sp.wait_ge(K["parts_" + "qk"[w]], v(c + 1))
                    sp.dma_start(parts_dram[w][bass.ds(v(c), 1)].rearrange("o (a d) h n -> (o d h) a n", a=NPART),
                                 parts[w][:]).then_inc(K["stored"], 16)
                sp.wait_ge(K["stored"], v(32 * (c + 1)))
                apart(sp)
                sp.wait_ge(K["pv"], v(free_at(c)))
                q, kk = (x[bass.ds(v(c), 1)].rearrange("o r h n -> (o r) h n") for x in parts_dram)
                for x in range(NPART):
                    sp.dma_start(qpk[r][x * NPART * HD:(x + 1) * NPART * HD], q).then_inc(K[f"pk{r}"], 16)
                    for y in range(NPART):
                        lo = (x * NPART + y) * HD
                        sp.dma_start(kpk[r][lo:lo + HD], kk[x * HD:(x + 1) * HD]).then_inc(K[f"pk{r}"], 16)

            sp.wait_ge(K["ones_rows"], R)

            def three(i):
                for r in range(R):
                    pack(Count(i, R, r, sp), r)
            loop(sp, 2, three)
            pack(6, 0)
            pack(7, 1)

            def experts_sp(f):
                sp.wait_ge(K["e_routed"], run(f, "routed") + 1)
                sp.dma_start(f_b1, a["ffn_b1"].rearrange("e d -> d e"), allow_slow_non_contiguous=True).then_inc(K["e_exp_b"], 16)
                sp.dma_start(f_b2, a["ffn_b2"].rearrange("(o e) d -> o e d", o=1).broadcast_to([P, E, D])).then_inc(K["e_exp_b"], 16)
                for p in range(2):
                    sp.wait_ge(K[f"e_scat{p}"], run(f, f"scat{p}") + 16 * NT // 2)

                def load(e, p):
                    sp.dma_start(f_xe[p], slot_x.rearrange("(e t p) d -> e p t d", t=T, p=P)[bass.ds(e, 1)].rearrange("o p t d -> p (o t) d")).then_inc(K[f"e_ex{p}"], 16)
                    for m, w in enumerate(("ffn_W1", "ffn_W2")):
                        sp.dma_start(f_w[p][:, m], a[w][bass.ds(e, 1)].rearrange("o k n -> (o k) n")).then_inc(K[f"e_ex{p}"], 16)

                def store(e, p):
                    sp.wait_ge(K["e_ye"], run(f, "ye") + e + 1)
                    sp.dma_start(slot_y.rearrange("(e t p) d -> e p t d", t=T, p=P)[bass.ds(e, 1)].rearrange("o p t d -> p (o t) d"), f_ye[p]).then_inc(K[f"e_st{p}"], 16)
                load(0, 0)
                load(1, 1)
                def two(i):
                    for p in range(2):
                        store(2 * i + p, p)
                        load(2 * i + p + 2, p)
                loop(sp, E // 2 - 1, two)
                for p in range(2):
                    store(E - 2 + p, p)
            experts_sp(0)
            sp.wait_ge(K["e_x"], NT // T)
            wi = a["attn_b_in_proj_w"]
            loads = [(zn, wi[0:2 * P].rearrange("(c p) d -> p c d", p=P), {}),
                     (xbn, wi[2 * P:6 * P].rearrange("(c p) d -> p c d", p=P), {}),
                     (dtn, wi[6 * P:6 * P + H2], {}),
                     (on_nat, a["attn_b_out_proj_w"], {}),
                     (cwf, a["attn_b_conv_w"].rearrange("(c p) o k -> p c (o k)", p=P), {}),
                     (cbf, a["attn_b_conv_b"].rearrange("(c p) -> p c", p=P), dict(allow_slow_non_contiguous=True)),
                     (nw, a["attn_b_norm_w"].rearrange("(c p) -> p c", p=P), dict(allow_slow_non_contiguous=True)),
                     (dtb, a["attn_b_dt_bias"].rearrange("(o h) -> o h", o=1).broadcast_to([P, H2]), {}),
                     (alog, a["attn_b_A_log"].rearrange("(o h) -> o h", o=1).broadcast_to([P, H2]), {}),
                     (dpar, a["attn_b_D_param"].rearrange("(o h) -> o h", o=1).broadcast_to([P, H2]), {}),
                     (ob, a["attn_b_out_proj_b"].rearrange("(o d) -> o d", o=1).broadcast_to([P, D]), {})]
            assert len(loads) == N_MAMBA
            for dst, src, how in loads:
                sp.dma_start(dst, src, **how).then_inc(K["m_w"], 16)
            experts_sp(1)
            sp.wait_ge(K["e_x"], 2 * NT // T)
            sp.dma_start(out.rearrange("b (t p) d -> p (b t) d", p=P), x1[:, T:]).then_inc(K["out_stored"], 16)
            sp.wait_ge(K["out_stored"], 16)

        @block.gpsimd
        def _(pool):
            ch = Chain(pool, "pool_chain")
            ch(nc.gpsimd.memset(ident[:], 0.0))
            ch(nc.gpsimd.memset(identb[:], 0.0))
            ch.settle()
            for t_, s_ in ((ident, "identity_ready"), (identb, "bf_identity_ready")):
                nc.gpsimd.affine_select(out=t_[:], in_=t_[:], compare_op=ALU.not_equal, fill=1.0, base=0,
                                        pattern=[[-1, P]], channel_multiplier=1).then_inc(K[s_], 1)
            pool.wait_ge(K["bf_identity_ready"], 1)
            pool.wait_ge(K["constants_ready"], 4)
            pool.wait_ge(K["upto_ones"], 2)
            for t_ in (upto, uptob):
                nc.gpsimd.affine_select(out=t_[:], in_=t_[:], compare_op=ALU.is_ge, fill=0.0, base=0,
                                        pattern=[[1, P]], channel_multiplier=-1).then_inc(K["moe_const"], 1)
            pool.wait_ge(K["moe_const"], 2)

            def rstd(i, p):
                pool.wait_ge(K["l_mv"], v(2 * i + p + 1))
                apart(pool)
                ch(nc.gpsimd.tensor_scalar(ve[:], mv[p][:, :, 1], EPS, None, ALU.add))
                ch.settle()
                nc.gpsimd.tensor_tensor(rs[p][:], ve[:], halfneg[:, 0:NC], ALU.pow).then_inc(K["l_rs"], 1)
                pool.wait_ge(K["l_rs"], v(2 * i + p + 1))
                apart(pool)
            loop(pool, 2, lambda i: [rstd(i, p) for p in range(2)], ch, 2)

            def local(i):
                pool.wait_ge(K["l_qkv"], v(NC * (i + 1) + FREE))
                apart(pool)
                u = 2 * len(POOL_C) * i
                for n, c in enumerate(POOL_C + POOL_C):
                    if n == len(POOL_C):
                        pool.wait_ge(K["l_exp"], v(i + 1))
                        apart(pool)
                    if n == 0:
                        pool.wait_ge(K["l_acc"], v(NC * i + FREE))
                        apart(pool)
                    elif 2 <= n < len(POOL_C):
                        pool.wait_ge(K["l_qk_used"], v(len(POOL_C) * i + n - 1))
                        apart(pool)
                    elif n >= len(POOL_C) + 2:
                        pool.wait_ge(K["l_acc"], v(NC * i + POOL_C[n - len(POOL_C) - 2] + 1 + FREE))
                        apart(pool)
                    make = qk_product if n < len(POOL_C) else pv_product
                    make(nc.gpsimd, i, c, prod_p[n % 2]).then_inc(K["l_prod_pool"], 1)
                    pool.wait_ge(K["l_prod_pool"], v(u + n + 1))
                    apart(pool)
            loop(pool, PR, local)

            pool.wait_ge(K["residual_in"], 16)
            pool.wait_ge(K["bias_made"], 2)
            nc.gpsimd.tensor_tensor(x1[:, T:], x1[:, T:], bias_g[:].rearrange("p (o d) -> p o d", o=1).broadcast_to([P, B * T, D]), ALU.add).then_inc(K["x1_biased"], 1)
            pool.wait_ge(K["x1_biased"], 1)

            def split(c, w):
                pool.wait_ge(K["p1"], v(2 * c + w + 1))
                ch(nc.gpsimd.tensor_tensor(rres[:], ff[w][:], parts[w][:, 0], ALU.subtract))
                ch.settle()
                apart(pool)
                ch(nc.gpsimd.tensor_copy(parts[w][:, 1], rres[:]))
                ch.settle()
                nc.gpsimd.tensor_tensor(parts[w][:, 2], rres[:], parts[w][:, 1], ALU.subtract).then_inc(K["parts_" + "qk"[w]], 1)
                pool.wait_ge(K["parts_" + "qk"[w]], v(c + 1))
                apart(pool)

            def neg_max(b, r, g):
                pool.wait_ge(K["max"], v(MAX0 + SC * b + 16 * (g + 1)))
                apart(pool)
                m = mx[r][:, :, g * NJ:(g + 1) * NJ]
                def part(x): return nm[r][:, g, :, x * NJ:(x + 1) * NJ]
                ch(nc.gpsimd.tensor_scalar(part(0), m, -1.0, None, ALU.mult))
                ch(nc.gpsimd.tensor_scalar(nr[:], m, -1.0, None, ALU.mult))
                ch.settle()
                ch(nc.gpsimd.tensor_tensor(nr[:], nr[:], part(0), ALU.subtract))
                ch.settle()
                apart(pool)
                ch(nc.gpsimd.tensor_copy(part(1), nr[:]))
                ch.settle()
                nc.gpsimd.tensor_tensor(part(2), nr[:], part(1), ALU.subtract).then_inc(K["nm"], 1)
                pool.wait_ge(K["nm"], v(NG * b + g + 1))
                apart(pool)

            for c in range(2):
                for w in range(2):
                    split(c, w)
            for g in range(NG):
                neg_max(0, 0, g)

            def half(b, r, n_next, n_after):
                for g in range(NG):
                    if n_next:
                        neg_max(b + 1, (r + 1) % R, g)
                    if n_after and g < 2:
                        split(b + 2, g)
            halves(pool, half, ch, 3 * 20)

            def experts_pool(f):
                def rstd(i):
                    pool.wait_ge(K["e_mv"], run(f, "mv") + i + 1)
                    apart(pool)
                    ch(nc.gpsimd.tensor_tensor(f_ve, f_mv[:, bass.ds(i * T, T), 1], eps[:, 0:T], ALU.add))
                    ch.settle()
                    nc.gpsimd.tensor_tensor(f_rs[:, bass.ds(i * T, T)], f_ve, halfneg[:, 0:T], ALU.pow).then_inc(K["e_rs"], 1)
                    pool.wait_ge(K["e_rs"], run(f, "rs") + i + 1)
                    apart(pool)
                loop(pool, NT // T, rstd, ch, 1)
                pool.wait_ge(K["slots_cleared"], 16)

                def scatter(i):
                    for p in range(2):
                        pool.wait_ge(K["e_xg"], run(f, "xg") + 2 * i + p + 1)
                        apart(pool)
                        for t in range(T):
                            nc.gpsimd.indirect_dma_start(
                                out=slot_x, out_offset=bass.IndirectOffsetOnAxis(ap=f_i4[p][:, t:t + 1], axis=0),
                                in_=f_xg[p][:, t], in_offset=None, bounds_check=E * CAP - 1, oob_is_err=False,
                            ).then_inc(K[f"e_scat{p}"], 16)
                loop(pool, NT // T // 2, scatter)

                for p in range(2):
                    pool.wait_ge(K[f"e_st{p}"], run(f, f"st{p}") + 16 * E // 2)

                def gather(i):
                    for p in range(2):
                        pool.wait_ge(K["e_gidx"], run(f, "gidx") + 2 * i + p + 1)
                        apart(pool)
                        for t in range(T):
                            nc.gpsimd.indirect_dma_start(
                                out=f_yg[p][:, t], out_offset=None, in_=slot_y,
                                in_offset=bass.IndirectOffsetOnAxis(ap=f_i4[p][:, t:t + 1], axis=0),
                            ).then_inc(K[f"e_gath{p}"], 16)
                loop(pool, NT // T // 2, gather)
            experts_pool(0)
            pool.wait_ge(K["m_w"], 16 * N_MAMBA)

            def front(b, p):
                pool.wait_ge(K["m_mv"], v(b + 1))
                apart(pool)
                ch(nc.gpsimd.tensor_scalar(m_ve, m_mv[:, :, 1], EPS, None, ALU.add))
                ch.settle()
                nc.gpsimd.tensor_tensor(m_rs, m_ve, halfneg[:, 0:T], ALU.pow).then_inc(K["m_rs"], 1)
                pool.wait_ge(K["m_rs"], v(b + 1))
                yield
                pool.wait_ge(K["m_xn"], v(b + 1))
                apart(pool)
                xr = x1[:, bass.ds(v(b * T + T), T), :]
                nc.gpsimd.tensor_tensor(xr, xr, ob.rearrange("p (o d) -> p o d", o=1).broadcast_to([P, T, D]), ALU.add).then_inc(K["m_bias"], 1)
                pool.wait_ge(K["m_bias"], v(b + 1))
                apart(pool)
                yield
                yield
                yield
                yield
                yield
                yield
                yield

            def back(b, p):
                yield
                yield
                pool.wait_ge(K["m_wj"], v(b + 1))
                pool.wait_ge(K["m_xtoks"], v(b + 1))
                wj = m_wj[:, 0:T - 1].rearrange("p c (h o) -> p c h o", o=1).broadcast_to([P, T - 1, H2, P])
                nc.gpsimd.tensor_tensor(m_xst, m_xtok[:, 0:T - 1], wj, ALU.mult).then_inc(K["m_xst"], 1)
                pool.wait_ge(K["m_erow"], v(b + 1))
                apart(pool)
                c = m_ch[p][:, 3, :].rearrange("p (c o n) -> p c o n", c=T, o=1).broadcast_to([P, T, H2, P])
                nc.gpsimd.tensor_tensor(m_ce, c, m_erow, ALU.mult).then_inc(K["m_ce"], 1)
                pool.wait_ge(K["m_ce"], v(b + 1))
                yield
                yield
                yield
                pool.wait_ge(K["m_ssq"], v(T * b + T))
                apart(pool)
                ch(nc.gpsimd.tensor_scalar(m_rv, m_ssq, 1.0 / (2 * P), EPS, ALU.mult, ALU.add))
                ch.settle()
                nc.gpsimd.tensor_tensor(m_ri, m_rv, halfneg[:, 0:T], ALU.pow).then_inc(K["m_ri"], 1)
                pool.wait_ge(K["m_ri"], v(b + 1))
                apart(pool)
                yield
                yield
            mamba(pool, front, back, ch, 4)
            experts_pool(1)

        @block.scalar
        def _(act):
            act.wait_ge(K["constants_ready"], 4)
            act.dma_start(slot_x.rearrange("(t p) d -> p t d", p=P), zeros[:].rearrange("p (o d) -> p o d", o=1).broadcast_to([P, NT, D])).then_inc(K["slots_cleared"], 16)
            nt = 0
            for k in "lg":
                for c in range(4):
                    act.wait_ge(K["weight_transposes"], v(nt + 1))
                    src = ps[:, nt % 4, 0:P]
                    dst = wT[k][:, c, :] if c < 3 else woT[k][:]
                    if c < 2 and k == "g":
                        src, dst = src.rearrange("p (h d) -> p d h", h=H), dst.rearrange("p (d h) -> p d h", h=H)
                    nc.scalar.activation(dst, src, ACT.Copy).then_inc(K["weight_evacuations"], 1)
                    nt += 1
            act.wait_ge(K["weights_in"], 16 * N_WEIGHTS)
            act.wait_ge(K["weight_transposes"], v(nt + 1))
            nc.scalar.activation(bias_l[:], ps[:, 4, 0:1], ACT.Identity, bias=b_out_l[:]).then_inc(K["bias_made"], 1)

            def front(i, p):
                act.wait_ge(K["l_xnT"], v(2 * i + p + 1 + FREE))
                act.wait_ge(K["l_proj"], v(NC * 2 * i + FREE))
                nc.scalar.activation(xT[p].rearrange("p c n -> p (c n)"), ps[:, 6:8, :].rearrange("p a n -> p (a n)"), ACT.Copy).then_inc(K["l_xTs"], 1)
                for c in range(NC):
                    act.wait_ge(K["l_proj"], v(NC * (2 * i + p) + c + 1 + FREE))
                    nc.scalar.activation(qkv[:, bass.ds(2 * i + p, 1), c, :].rearrange("p o d -> p (o d)"), ps[:, c % 4, 0:3 * D], ACT.Copy).then_inc(K["l_qkv"], 1)
            loop(act, 2, lambda i: [front(i, p) for p in range(2)])

            def local(i):
                act.wait_ge(K["l_shift"], v(i + 1))
                nc.scalar.activation(pe_[:], sx[:], ACT.Exp, scale=SCALE).then_inc(K["l_exp"], 1)
                act.wait_ge(K["l_oT"], v(i + 1 + FREE))
                nc.scalar.activation(oT_l.rearrange("p c n -> p (c n)"), ps[:, 6:8, :].rearrange("p a n -> p (a n)"), ACT.Copy).then_inc(K["l_oTs"], 1)
                act.wait_ge(K["l_out"], v(i + 1))
                for h in range(2):
                    nc.scalar.activation(locT[:, 4 * h:4 * h + 4, bass.ds(i * P, P)], ps[:, h, :].rearrange("p (c n) -> p c n", c=4), ACT.Identity, bias=bias_l[:]).then_inc(K["l_loc"], 1)
            act.wait_ge(K["bias_made"], 1)
            loop(act, PR, local)
            act.wait_ge(K["l_loc"], 2 * PR + FREE)

            act.sem_inc(K["exp"], SC)

            def m_wait(b, k):
                act.wait_ge(K["m_full"], v(m_base(b) + k + 1))

            def copy_x(c):
                nc.scalar.activation(xs[:], locT[:, bass.ds(v(c), 1), :].rearrange("p o n -> p (o n)"), ACT.Copy).then_inc(K["xs"], 1)

            def qk_evac(c, w):
                act.wait_ge(K["stored"], v(32 * c))
                nc.scalar.activation(ff[w][:], ps[:, M, :], ACT.Identity, bias=b_qk_g[:, w:w + 1]).then_inc(K["m_free"], 1)
                act.wait_ge(K["m_free"], v(act_now[0]))
                nc.scalar.activation(parts[w][:, 0], ff[w][:], ACT.Copy).then_inc(K["p1"], 1)

            def v_evac(c, r):
                act.wait_ge(K["pv"], v(free_at(c)))
                nc.scalar.activation(va[r][:, :, :, 0:HD], ps[:, M, :].rearrange("p (t h d) -> p t h d", t=T, h=H), ACT.Copy).then_inc(K["m_free"], 1)

            def mrow_copy(b, r, g):
                n_ = NPART * NJ
                if g >= 2:
                    act.wait_ge(K[f"mr{g - 2}"], v(16 * (b + 1) + FREE))
                else:
                    act.wait_ge(K[f"mr{g + 2}"], v(16 * b + FREE))
                nc.scalar.activation(mrow[g % 2][0:n_, :], ps_mb[0:n_, 0:S], ACT.Copy).then_inc(K["m_free"], 1)
                act.wait_ge(K["m_free"], v(act_now[0]))
                act.dma_start(qpk[r][PROD:KA, g * NJ:(g + 1) * NJ, :], mrow[g % 2][0:n_, :]).then_inc(K[f"mr{g}"], 16)

            act_now = [0]
            act.wait_ge(K["values_ready"], R)
            k = 0
            for c in range(2):
                copy_x(c)
                for t in "qkv":
                    act.wait_ge(K["m_full"], v(k + 1))
                    k += 1
                    act_now[0] = k
                    if t == "v":
                        v_evac(c, c)
                    else:
                        qk_evac(c, "qk".index(t))
            for g in range(3):
                act.wait_ge(K["m_full"], v(k + 1))
                k += 1
                act_now[0] = k
                mrow_copy(0, 0, g)

            def half(b, r, n_next, n_after):
                todo = tasks(n_next, n_after)
                at = {t: k for k, (_, t) in enumerate(todo)}

                def evac_ou(g, before):
                    act.wait_ge(K["pv"], v(PV0 + STEPS * b + 4 * (g + 1)))
                    act.wait_ge(K["m_full"], v(before))
                    nc.scalar.activation(ou[g % 2][:], ps[:, PV, :], ACT.Copy).then_inc(K["ou"], 1)

                for n in range(STEPS):
                    for j in range(NJ):
                        q = 4 * n + j
                        act.wait_ge(K["st"], v(SC * b + q + 1))
                        if j == 0:
                            act.wait_ge(K["pv"], v(PV0 + STEPS * b + n - 1))
                        nc.scalar.activation(eb[q % 8][:], ps[:, ST + q % 3, :], ACT.Exp, scale=SCALE).then_inc(K["exp"], 1)
                    if n == 4:
                        evac_ou(0, m_base(b))
                    if n == 8:
                        evac_ou(1, m_base(b) + at["ot3"] + 1)
                    if n == 12:
                        evac_ou(2, m_base(b) + at["ot0"] + 1)
                    if n == 1 and n_after:
                        copy_x(b + 2)
                    for k, (m, t) in enumerate(todo):
                        if m != n or t[:2] in ("ot", "dd"):
                            continue
                        m_wait(b, k)
                        act_now[0] = m_base(b) + k + 1
                        if t == "mt3":
                            mrow_copy(b, r, 3)
                        elif t[:2] == "mt":
                            mrow_copy(b + 1, (r + 1) % R, int(t[2]))
                        elif t in ("aq", "ak"):
                            qk_evac(b + 2, "qk".index(t[1]))
                        elif t == "av":
                            v_evac(b + 2, (r + 2) % R)
                        elif t == "tt":
                            nc.scalar.activation(onT[:], ps[:, M, :], ACT.Copy).then_inc(K["m_free"], 1)
                evac_ou(3, m_base(b) + at["ot1"] + 1)
            halves(act, half)
            m_wait(B, 1)
            nc.scalar.activation(onT[:], ps[:, M, :], ACT.Copy).then_inc(K["m_free"], 1)

            def experts_act(f):
                def front(i):
                    for p in range(2):
                        act.wait_ge(K["e_xnT"], run(f, "xnT") + 2 * i + p + 1)
                        act.wait_ge(K["e_logits"], run(f, "logits") + 2 * i)
                        nc.scalar.activation(f_xT[p], ps[:, p, :], ACT.Copy).then_inc(K["e_xTs"], 1)
                loop(act, NT // T // 2, front)
                act.wait_ge(K["e_shift"], run(f, "shift") + 1)
                nc.scalar.activation(f_ex, f_lg, ACT.Exp).then_inc(K["e_exp"], 1)
                act.wait_ge(K["e_exp_b"], run(f, "exp_b") + 32)

                def expert(i):
                    for p in range(2):
                        e = 2 * i + p
                        act.wait_ge(K["e_xe_T"], run(f, "xe_T") + e + 1)
                        nc.scalar.activation(f_xeT[p], ps[:, p, :], ACT.Copy).then_inc(K["e_xeTs"], 1)
                        act.wait_ge(K["e_h"], run(f, "h") + e + 1)
                        nc.scalar.activation(f_hT[p], ps[:, 2 + p, :], ACT.Relu, bias=f_b1[:, bass.ds(e, 1)]).then_inc(K["e_hT"], 1)
                loop(act, E // 2, expert)
            experts_act(0)
            for n, (dst, bank, rows, cols) in enumerate(W_EVAC):
                act.wait_ge(K["m_wT"], n + 1)
                if n == 0:
                    act.wait_ge(K["m_w"], 16 * N_MAMBA)
                if n >= 7:
                    nc.scalar.activation(dst, ps[0:rows, bank, 0:cols], ACT.Copy, scale=nw[:, n - 7:n - 6]).then_inc(K["m_wTs"], 1)
                else:
                    nc.scalar.activation(dst, ps[0:rows, bank, 0:cols], ACT.Copy).then_inc(K["m_wTs"], 1)
            nc.scalar.activation(aneg, alog, ACT.Exp).then_inc(K["m_cst"], 1)

            def front(b, p):
                yield
                act.wait_ge(K["m_xT"], v(b + 1))
                act.wait_ge(K["m_z"], v(T * b))
                nc.scalar.activation(m_xT, ps[:, 0, :], ACT.Copy).then_inc(K["m_xTs"], 1)
                act.wait_ge(K["m_silu"], v(4 * b))
                act.wait_ge(K["m_cw"], 2)
                yield
                for c in range(4):
                    act.wait_ge(K["m_proj"], v(4 * b + c + 1))
                    nc.scalar.activation(m_acc[:, c], ps[:, (1 + c) % 3, :], ACT.Identity, bias=cb[:, c:c + 1], scale=cw[:, c, TAPS - 1:TAPS]).then_inc(K["m_acc"], 1)
                    if c >= 1:
                        act.wait_ge(K["m_conv"], v(4 * b + c))
                        nc.scalar.activation(m_th[:, c - 1], m_acc[:, c - 1], ACT.Tanh).then_inc(K["m_th"], 1)
                    yield
                act.wait_ge(K["m_conv"], v(4 * b + 4))
                nc.scalar.activation(m_th[:, 3], m_acc[:, 3], ACT.Tanh).then_inc(K["m_th"], 1)
                for t in range(T):
                    act.wait_ge(K["m_z"], v(T * b + t + 1))
                    nc.scalar.activation(m_zt[:, t], ps[:, (5 + t) % 3, 0:2 * P], ACT.Tanh, scale=0.5).then_inc(K["m_zt"], 1)
                yield
                act.wait_ge(K["m_abs"], v(b + 1))
                nc.scalar.activation(m_u, m_abs, ACT.Exp, scale=-1.0).then_inc(K["m_u"], 1)
                yield

            def back(b, p):
                act.wait_ge(K["m_xtok"], v(b + 1))
                nc.scalar.activation(m_xtok.rearrange("p c h n -> p (c h n)"), ps[:, 3:5, :].rearrange("p a n -> p (a n)"), ACT.Copy).then_inc(K["m_xtoks"], 1)
                act.wait_ge(K["m_btok"], v(b + 1))
                nc.scalar.activation(m_btok.rearrange("p c n -> p (c n)"), ps[:, 5, :], ACT.Copy).then_inc(K["m_btoks"], 1)
                yield
                yield
                act.wait_ge(K["m_dif"], v(b + 1))
                nc.scalar.activation(m_el.rearrange("p c h n -> p (c h n)"), ps[:, 5:7, :].rearrange("p a n -> p (a n)"), ACT.Exp).then_inc(K["m_el"], 1)
                act.wait_ge(K["m_row"], v(b + 1))
                nc.scalar.activation(m_erow.rearrange("p c h n -> p (c h n)"), ps[:, 3:5, :].rearrange("p a n -> p (a n)"), ACT.Exp).then_inc(K["m_erow"], 1)
                yield
                yield
                yield
                act.wait_ge(K["m_y"], v(b + 1))
                for t in range(T):
                    nc.scalar.activation(m_sq, m_y[:, t], ACT.Square, accum_out=m_ssq[:, t:t + 1]).then_inc(K["m_ssq"], 1)
                    act.wait_ge(K["m_ssq"], v(T * b + t + 1))
                act.wait_ge(K["m_yT"], v(b + 1))
                nc.scalar.activation(m_yT.rearrange("p a n -> p (a n)"), ps[:, 5:7, :].rearrange("p a n -> p (a n)"), ACT.Copy).then_inc(K["m_yTs"], 1)
                yield
                yield
            mamba(act, front, back)
            experts_act(1)

        @block.vector
        def _(dve):
            ch = Chain(dve, "dve_chain")
            for t_ in (upto, uptob):
                nc.vector.memset(t_[:], 1.0).then_inc(K["upto_ones"], 1)
            nc.vector.memset(zeros[:], 0.0).then_inc(K["constants_ready"], 1)
            nc.vector.memset(halfneg[:], -0.5).then_inc(K["constants_ready"], 1)
            nc.vector.memset(ones_row[:], 1.0).then_inc(K["constants_ready"], 1)
            nc.vector.memset(eps[:], EPS).then_inc(K["constants_ready"], 1)

            dve.wait_ge(K["moe_const"], 2)
            ch(nc.vector.memset(onesb[:], 1.0))
            ch(nc.vector.memset(not_first[:], 1.0))
            ch.settle()
            ch(nc.vector.memset(not_first[:, :, 0:1], 0.0))
            for e in range(E):
                nc.vector.memset(prefer[:, e:e + 1], float(E - e)).then_inc(K["moe_const"], 1)
                nc.vector.memset(first_slot[:, e:e + 1], float(e * CAP)).then_inc(K["moe_const"], 1)

            def stats(i, p):
                dve.wait_ge(K[f"lxb_in{p}"], v(32 * (i + 1)))
                for c in range(NC):
                    ch(nc.vector.bn_stats(st6[:, c], xb[p][:, c]))
                ch.settle()
                apart(dve)
                for c in range(NC):
                    last = nc.vector.bn_aggr(mv[p][:, c], st6[:, c])
                    if c < NC - 1:
                        ch(last)
                last.then_inc(K["l_mv"], 1)
                dve.wait_ge(K["l_rs"], v(2 * i + p + 1))
                dve.wait_ge(K["l_xnT"], v(2 * i + FREE))
                for c in range(NC):
                    last = nc.vector.tensor_scalar(xn[p][:, c], xb[p][:, c], mv[p][:, c, 0:1], rs[p][:, c:c + 1], ALU.subtract, ALU.mult)
                    if c < NC - 1:
                        ch(last)
                last.then_inc(K["l_xn"], 1)
                dve.wait_ge(K["l_xn"], v(2 * i + p + 1))
            loop(dve, 2, lambda i: [stats(i, p) for p in range(2)], ch, 2 * (3 * NC - 2))
            dve.wait_ge(K["weights_in"], 16 * N_WEIGHTS)
            dve.wait_ge(K["weight_transposes"], 10)
            nc.vector.tensor_tensor(bias_g[:], ps[:, 5, 0:D], b_out_g[:], ALU.add).then_inc(K["bias_made"], 1)

            def local(i):
                dve.wait_ge(K["l_qkv"], v(NC * (i + 1) + FREE))
                dve.wait_ge(K["l_acc"], v(NC * i + FREE))
                np_, nd = 0, 0
                for c in range(NC):
                    if c in DVE_C:
                        src = prod_d[nd]
                        ch(qk_product(nc.vector, i, c, src))
                        ch.settle()
                        nd += 1
                    else:
                        src = prod_p[np_ % 2]
                        np_ += 1
                        dve.wait_ge(K["l_prod_pool"], v(2 * len(POOL_C) * i + np_))
                    last = nc.vector.tensor_reduce(sc[:, c].rearrange("p h c -> p c h"), src.rearrange("p c (h d) -> p c h d", h=H), AX.X, ALU.add)
                    if c in DVE_C:
                        ch(last)
                    else:
                        last.then_inc(K["l_qk_used"], 1)
                ch.settle()
                dve.wait_ge(K["l_qk_used"], v(len(POOL_C) * (i + 1)))
                ch(nc.vector.tensor_reduce(smax[:], sc[:], AX.X, ALU.max))
                ch.settle()
                nc.vector.tensor_tensor(sx[:], sc[:], bc(smax, NC), ALU.subtract).then_inc(K["l_shift"], 1)
                dve.wait_ge(K["l_exp"], v(i + 1))
                for n, c in enumerate(DVE_C):
                    pv_product(nc.vector, i, c, prod_d[n]).then_inc(K["l_prod_dve"], 1)
                ch(nc.vector.tensor_reduce(ssum[:], pe_[:], AX.X, ALU.add))
                ch.settle()
                ch(nc.vector.reciprocal(srec[:], ssum[:]))
                ch.settle()
                dve.wait_ge(K["l_acc"], v(NC * (i + 1) + FREE))
                dve.wait_ge(K["l_oT"], v(i + FREE))
                nc.vector.tensor_tensor(o_l.rearrange("p c (h d) -> p c h d", h=H), ps[:, 4:6, :].rearrange("p a (c h d) -> p (a c) h d", h=H, d=HD), bc(srec, HD), ALU.mult).then_inc(K["l_o"], 1)
            loop(dve, PR, local, ch, 3 + 3 + 1 + 2)

            dve.sem_inc(K["max"], MAX0)
            dve.wait_ge(K["l_loc"], 2 * PR + FREE)
            for r in range(R):
                nc.vector.memset(kpk[r][64:KA], 1.0).then_inc(K["ones_rows"], 1)
                ch(nc.vector.memset(va[r][:], 0.0))
                ch.settle()
                nc.vector.memset(va[r][:, :, :, HD:HD + 1], 1.0).then_inc(K["values_ready"], 1)
            nc.vector.memset(ou[1][:], 1.0).then_inc(K["dummy_ready"], 1)
            nc.vector.memset(on[:], 1.0).then_inc(K["dummy_ready"], 1)
            nc.vector.memset(x1[:, 0:T], 0.0).then_inc(K["dummy_ready"], 1)
            dve.wait_ge(K["dummy_ready"], 3)
            dve.wait_ge(K["x1_biased"], 1)

            def maxes(b, r, n):
                for s in range(4 * n, 4 * n + 4):
                    g, qt, j = s // 16, s // 4 % 4, s % 4
                    dve.wait_ge(K["s"], v(SC * b + s + 1))
                    nc.vector.tensor_reduce(mx[r][:, qt, g * NJ + j:g * NJ + j + 1], ps[:, SS + s % 3, :], AX.X, ALU.max).then_inc(K["max"], 1)

            def normalise(b, k, g, seen):
                dve.wait_ge(K["m_full"], v(m_base(b) + k + 1))
                o = ps[:, M, :].rearrange("p (t j c) -> p t j c", t=T, j=NJ)
                nc.vector.reciprocal(rc.rearrange("p t (j o) -> p t j o", o=1), o[:, :, :, HD:HD + 1]).then_inc(K["rc"], 1)
                dve.wait_ge(K["rc"], v(NG * b + seen))
                nc.vector.tensor_tensor(on[:, :, g * NJ * HD:(g + 1) * NJ * HD].rearrange("p t (j d) -> p t j d", j=NJ), o[:, :, :, 0:HD], bc(rc, HD), ALU.mult).then_inc(K["m_free"], 1)
                dve.wait_ge(K["m_free"], v(m_base(b) + k + 1))

            def residual(b, k, s0):
                dve.wait_ge(K["m_full"], v(m_base(b) + k + 1))
                xd = x1[:, bass.ds(v(s0 * T), T), :]
                nc.vector.tensor_tensor(xd, ps[:, M, :].rearrange("p (t d) -> p t d", t=T), xd, ALU.add).then_inc(K["m_free"], 1)

            for n in range(STEPS):
                maxes(0, 0, n)

            def half(b, r, n_next, n_after):
                seen = 0
                todo = tasks(n_next, n_after)
                for n in range(STEPS):
                    if n_next:
                        maxes(b + 1, (r + 1) % R, n)
                    for k, (m, t) in enumerate(todo):
                        if m != n:
                            continue
                        if t[:2] == "ot":
                            seen += 1
                            normalise(b, k, int(t[2]), seen)
                        elif t == "dd":
                            residual(b, k, b)
            halves(dve, half)
            normalise(B, 0, 3, 1)
            residual(B, 2, B)
            dve.wait_ge(K["m_free"], v(m_base(B) + 3))
            dve.wait_ge(K["moe_const"], 18)

            def experts_dve(f):
                def stats(i):
                    for p in range(2):
                        g = 2 * i + p
                        for t in range(T):
                            ch(nc.vector.bn_stats(f_st[:, t], x1[:, bass.ds(T + g * T + t, 1), :].rearrange("p o d -> p (o d)")))
                        ch.settle()
                        apart(dve)
                        for t in range(T):
                            ch(nc.vector.bn_aggr(f_mv4[:, t], f_st[:, t]))
                        ch.settle()
                        nc.vector.tensor_copy(f_mv[:, bass.ds(g * T, T), :], f_mv4).then_inc(K["e_mv"], 1)
                        dve.wait_ge(K["e_rs"], run(f, "rs") + g + 1)
                        dve.wait_ge(K["e_xnT"], run(f, "xnT") + 2 * i)
                        for t in range(T):
                            last = nc.vector.tensor_scalar(f_xn[p][:, t], x1[:, bass.ds(T + g * T + t, 1), :].rearrange("p o d -> p (o d)"),
                                                           f_mv[:, bass.ds(g * T + t, 1), 0], f_rs[:, bass.ds(g * T + t, 1)], ALU.subtract, ALU.mult)
                            if t < T - 1:
                                ch(last)
                        last.then_inc(K["e_xn"], 1)
                loop(dve, NT // T // 2, stats, ch, 2 * (3 * T - 1))

                def te(x):
                    return x.rearrange("p e t -> p t e")

                def over_e(x):
                    return x.rearrange("p (t o) -> p t o", o=1).broadcast_to([P, NT, E])

                def over_t(x):
                    return x[:, :].rearrange("p (o e) -> p o e", o=1).broadcast_to([P, NT, E])

                def do(ins):
                    ch(ins)
                    ch.settle()
                dve.wait_ge(K["e_logits"], run(f, "logits") + NT // T)
                do(nc.vector.tensor_tensor(f_lg, ps[:, 4, 0:NT * E].rearrange("p (t e) -> p t e", e=E), over_t(br), ALU.add))
                do(nc.vector.tensor_reduce(f_m, f_lg, AX.X, ALU.max))
                nc.vector.tensor_tensor(f_lg, f_lg, over_e(f_m), ALU.subtract).then_inc(K["e_shift"], 1)
                dve.wait_ge(K["e_shift"], run(f, "shift") + 1)
                do(nc.vector.tensor_scalar(f_pick, f_lg, 0.0, None, ALU.is_equal))
                do(nc.vector.tensor_tensor(f_pick, f_pick, over_t(prefer), ALU.mult))
                do(nc.vector.tensor_reduce(f_m, f_pick, AX.X, ALU.max))
                do(nc.vector.tensor_tensor(te(f_one), f_pick, over_e(f_m), ALU.is_equal))
                nc.vector.tensor_copy(f_oneb, f_one).then_inc(K["e_onehot"], 1)
                dve.wait_ge(K["e_exp"], run(f, "exp") + 1)
                do(nc.vector.tensor_reduce(f_sum, f_ex, AX.X, ALU.add))
                do(nc.vector.reciprocal(f_gate, f_sum))
                ch(nc.vector.tensor_tensor(f_rg, f_rs, f_gate, ALU.mult))
                dve.wait_ge(K["e_counts"], run(f, "counts") + 1)
                do(nc.vector.tensor_tensor_scan(f_incl, not_first[:].rearrange("p e t -> p (e t)"), ps[:, 6, 0:E * NT], 0.0, ALU.mult, ALU.add))
                pos = f_pos.rearrange("p e t -> p (e t)")
                do(nc.vector.tensor_tensor(pos, ps[:, 5, 0:E * NT], f_incl, ALU.add))
                do(nc.vector.scalar_tensor_tensor(pos, ps[:, 6, 0:E * NT], -1.0, pos, ALU.mult, ALU.add))
                do(nc.vector.tensor_tensor(f_pos, f_pos, f_one, ALU.mult))
                do(nc.vector.tensor_reduce(f_at, te(f_pos), AX.X, ALU.add))
                do(nc.vector.tensor_tensor(te(f_pos), te(f_one), over_t(first_slot), ALU.mult))
                do(nc.vector.tensor_reduce(f_e0, te(f_pos), AX.X, ALU.add))
                do(nc.vector.tensor_scalar(f_keep, f_at, float(CAP), None, ALU.is_lt))
                do(nc.vector.tensor_tensor(f_gk, f_gate, f_keep, ALU.mult))
                do(nc.vector.tensor_tensor(f_slot, f_at, f_keep, ALU.mult))
                do(nc.vector.tensor_tensor(f_gi, f_e0, f_slot, ALU.add))
                do(nc.vector.tensor_scalar(f_si, f_keep, -float(2 * E * CAP), float(2 * E * CAP), ALU.mult, ALU.add))
                nc.vector.tensor_tensor(f_si, f_si, f_gi, ALU.add).then_inc(K["e_routed"], 1)
                dve.wait_ge(K["e_routed"], run(f, "routed") + 1)

                first = 0

                def rows(i):
                    for p in range(2):
                        g = 2 * i + p
                        if i is not first:
                            dve.wait_ge(K[f"e_scat{p}"], run(f, f"scat{p}") + 16 * T * i)
                        for t in range(T):
                            ch(nc.vector.tensor_scalar(f_xg[p][:, t], x1[:, bass.ds(T + g * T + t, 1), :].rearrange("p o d -> p (o d)"),
                                                       f_mv[:, bass.ds(g * T + t, 1), 0], f_rg[:, bass.ds(g * T + t, 1)], ALU.subtract, ALU.mult))
                        ch.settle()
                        nc.vector.tensor_copy(f_i4[p], f_si[:, bass.ds(g * T, T)]).then_inc(K["e_xg"], 1)
                rows(first)
                loop(dve, NT // T // 2 - 1, lambda i: rows(i + 1), ch, 2 * T)

                dve.wait_ge(K["e_exp_b"], run(f, "exp_b") + 32)

                def expert(i):
                    for p in range(2):
                        e = 2 * i + p
                        dve.wait_ge(K["e_y"], run(f, "y") + e + 1)
                        dve.wait_ge(K[f"e_st{p}"], run(f, f"st{p}") + 16 * i)
                        nc.vector.tensor_tensor(f_ye[p], ps[:, 4 + p, :].rearrange("p (t d) -> p t d", t=T),
                                                f_b2[:, bass.ds(e, 1), :].broadcast_to([P, T, D]), ALU.add).then_inc(K["e_ye"], 1)
                loop(dve, E // 2, expert)

                for p in range(2):
                    dve.wait_ge(K[f"e_scat{p}"], run(f, f"scat{p}") + 16 * NT // 2)

                def index(g, p):
                    nc.vector.tensor_copy(f_i4[p], f_gi[:, bass.ds(g * T, T)]).then_inc(K["e_gidx"], 1)

                def add(i, p):
                    g = 2 * i + p
                    dve.wait_ge(K[f"e_gath{p}"], run(f, f"gath{p}") + 16 * T * (i + 1))
                    for t in range(T):
                        xr = x1[:, bass.ds(T + g * T + t, 1), :].rearrange("p o d -> p (o d)")
                        last = nc.vector.scalar_tensor_tensor(xr, f_yg[p][:, t], f_gk[:, bass.ds(g * T + t, 1)], xr, ALU.mult, ALU.add)
                        if t < T - 1:
                            ch(last)
                    last.then_inc(K["e_x"], 1)
                    dve.wait_ge(K["e_x"], run(f, "x") + g + 1)
                    ch.settle()
                index(0, 0)
                index(1, 1)

                def back(i):
                    for p in range(2):
                        add(i, p)
                        index(2 * i + p + 2, p)
                loop(dve, NT // T // 2 - 1, back, ch, 2 * (T - 1))
                for p in range(2):
                    add(NT // T // 2 - 1, p)
            experts_dve(0)
            dve.wait_ge(K["m_w"], 16 * N_MAMBA)
            nc.vector.tensor_scalar(cw, cwf, 0.5, None, ALU.mult).then_inc(K["m_cw"], 1)
            nc.vector.tensor_scalar(cb, cbf, 0.5, None, ALU.mult).then_inc(K["m_cw"], 1)
            dve.wait_ge(K["m_cw"], 2)
            dve.wait_ge(K["m_cst"], 1)
            ch(nc.vector.tensor_scalar(aneg, aneg, -1.0, None, ALU.mult))
            ch(nc.vector.tensor_scalar(after, upto[:], -1.0, 1.0, ALU.mult, ALU.add))
            ch.settle()

            def do(ins):
                ch(ins)
                ch.settle()

            def front(b, p):
                for t in range(T):
                    ch(nc.vector.bn_stats(m_st[:, t], x1[:, bass.ds(v(b * T + (T + t)), 1), :].rearrange("p o d -> p (o d)")))
                ch.settle()
                apart(dve)
                for t in range(T):
                    last = nc.vector.bn_aggr(m_mv[:, t], m_st[:, t])
                    if t < T - 1:
                        ch(last)
                last.then_inc(K["m_mv"], 1)
                yield
                dve.wait_ge(K["m_rs"], v(b + 1))
                dve.wait_ge(K["m_xT"], v(b))
                for t in range(T):
                    last = nc.vector.tensor_scalar(m_xn[:, t], x1[:, bass.ds(v(b * T + (T + t)), 1), :].rearrange("p o d -> p (o d)"),
                                                   m_mv[:, t, 0:1], m_rs[:, t:t + 1], ALU.subtract, ALU.mult)
                    if t < T - 1:
                        ch(last)
                last.then_inc(K["m_xn"], 1)
                yield

                def conv(c):
                    dve.wait_ge(K["m_acc"], v(4 * b + c + 1))
                    for k in range(TAPS - 2, -1, -1):
                        j = TAPS - 1 - k
                        last = nc.vector.scalar_tensor_tensor(m_acc[:, c, j:], ps[:, (1 + c) % 3, 0:S - j], cw[:, c, k:k + 1], m_acc[:, c, j:], ALU.mult, ALU.add)
                        if k:
                            ch(last)
                            ch.settle()
                    last.then_inc(K["m_conv"], 1)

                def silu(c):
                    dve.wait_ge(K["m_th"], v(4 * b + c + 1))
                    nc.vector.scalar_tensor_tensor(m_ch[p][:, c], m_th[:, c], 1.0, m_acc[:, c], ALU.add, ALU.mult).then_inc(K["m_silu"], 1)
                for c in range(4):
                    conv(c)
                    if c:
                        silu(c - 1)
                    yield
                silu(3)
                for t in range(T):
                    dve.wait_ge(K["m_zt"], v(T * b + t + 1))
                    z = ps[:, (5 + t) % 3, :]
                    ch(nc.vector.tensor_tensor(m_raw[p][:, t], z[:, 2 * P:2 * P + H2], dtb, ALU.add))
                    nc.vector.scalar_tensor_tensor(m_g[p][:, t], m_zt[:, t], 1.0, z[:, 0:2 * P], ALU.add, ALU.mult).then_inc(K["m_zg"], 1)
                ch.settle()
                yield
                do(nc.vector.tensor_scalar(m_abs, m_raw[p], -1.0, None, ALU.mult))
                nc.vector.tensor_tensor(m_abs, m_abs, m_raw[p], ALU.max).then_inc(K["m_abs"], 1)
                ch(nc.vector.tensor_scalar(m_pos, m_raw[p], 0.0, None, ALU.max))
                dve.wait_ge(K["m_u"], v(b + 1))
                do(nc.vector.tensor_scalar(m_s, m_u, 2.0, None, ALU.add))
                do(nc.vector.reciprocal(m_s, m_s))
                do(nc.vector.tensor_tensor(m_s, m_s, m_u, ALU.mult))
                do(nc.vector.tensor_tensor(m_s2, m_s, m_s, ALU.mult))
                do(nc.vector.tensor_scalar(m_q, m_s2, 1.0 / 17, None, ALU.mult))
                for d in (15, 13, 11, 9, 7, 5, 3):
                    do(nc.vector.scalar_tensor_tensor(m_q, m_q, 1.0 / d, m_s2, ALU.add, ALU.mult))
                do(nc.vector.scalar_tensor_tensor(m_q, m_q, 1.0, m_s, ALU.add, ALU.mult))
                do(nc.vector.scalar_tensor_tensor(m_dt, m_q, 2.0, m_pos, ALU.mult, ALU.add))
                nc.vector.tensor_tensor(m_dA, m_dt, aneg.rearrange("p (o h) -> p o h", o=1).broadcast_to([P, T, H2]), ALU.mult).then_inc(K["m_dA"], 1)
                dve.wait_ge(K["m_dA"], v(b + 1))
                nc.vector.tensor_tensor(m_L, after.rearrange("p (a o n) -> p a o n", a=1, o=1).broadcast_to([P, T, H2, P]),
                                        m_dA.rearrange("p c (h o) -> p c h o", o=1).broadcast_to([P, T, H2, P]), ALU.mult).then_inc(K["m_L"], 1)
                yield

            def back(b, p):
                yield
                dve.wait_ge(K["m_g"], v(b + 1))
                nc.vector.tensor_tensor(m_gm, ps[:, 6, :].rearrange("p (c n) -> p c n", c=T), upto[:].rearrange("p (o n) -> p o n", o=1).broadcast_to([P, T, P]), ALU.mult).then_inc(K["m_gm"], 1)
                yield
                dve.wait_ge(K["m_el"], v(b + 1))
                nc.vector.tensor_tensor(m_wj, m_dt, m_el[:, :, :, P - 1], ALU.mult).then_inc(K["m_wj"], 1)
                dve.wait_ge(K["m_gm"], v(b + 1))
                for c in range(T):
                    for h in range(H2):
                        last = nc.vector.scalar_tensor_tensor(m_m[:, c, h], m_el[:, c, h], m_dt[:, c, h:h + 1], m_gm[:, c], ALU.mult, ALU.mult)
                        if (c, h) != (T - 1, H2 - 1):
                            ch(last)
                last.then_inc(K["m_m"], 1)
                yield
                dve.wait_ge(K["m_P"], v(b + 1))
                dve.wait_ge(K["m_erow"], v(b + 1))
                do(nc.vector.tensor_copy(m_S[:, 0].rearrange("p h n -> p (h n)"), ps[:, 5, 0:2 * P]))
                for c, part in ((1, ps[:, 5, 2 * P:4 * P]), (2, ps[:, 7, 2 * P:4 * P])):
                    for h in range(H2):
                        last = nc.vector.scalar_tensor_tensor(m_S[:, c, h], m_S[:, c - 1, h], m_erow[:, c, h, P - 1:P], part[:, h * P:(h + 1) * P], ALU.mult, ALU.add)
                        if (c, h) != (2, H2 - 1):
                            ch(last)
                    if c == 1:
                        ch.settle()
                last.then_inc(K["m_S"], 1)
                yield
                dve.wait_ge(K["m_Y"], v(b + 1))
                y = ps[:, 3:5, :].rearrange("p a (c h n) -> p (a c) h n", h=H2, n=P)
                for h in range(H2):
                    nc.vector.scalar_tensor_tensor(m_y1[:, :, h], m_xtok[:, :, h], dpar[:, h:h + 1], y[:, :, h], ALU.mult, ALU.add).then_inc(K["m_y1"], 1)
                dve.wait_ge(K["m_y1"], v(2 * b + 2 + FREE))
                nc.vector.scalar_tensor_tensor(m_y.rearrange("p c n -> p (c n)"), m_g[p].rearrange("p c n -> p (c n)"), 0.5, m_y1.rearrange("p c h n -> p (c h n)"), ALU.mult, ALU.mult).then_inc(K["m_y"], 1)
                yield
                yield
                dve.wait_ge(K["m_out"], v(b + 1))
                dve.wait_ge(K["m_ri"], v(b + 1))
                dve.wait_ge(K["m_bias"], v(b + 1))
                for t in range(T):
                    xr = x1[:, bass.ds(v(b * T + (T + t)), 1), :].rearrange("p o d -> p (o d)")
                    last = nc.vector.scalar_tensor_tensor(xr, ps[:, 7, t * P:(t + 1) * P], m_ri[:, t:t + 1], xr, ALU.mult, ALU.add)
                    if t < T - 1:
                        ch(last)
                last.then_inc(K["m_x"], 1)
                yield
            mamba(dve, front, back, ch, 104)
            dve.wait_ge(K["m_x"], B + FREE)
            experts_dve(1)

        @block.tensor
        def _(pe):
            pe.wait_ge(K["weights_in"], 16 * N_WEIGHTS)
            pe.wait_ge(K["identity_ready"], 1)
            pe.wait_ge(K["bf_identity_ready"], 1)
            pe.wait_ge(K["constants_ready"], 4)
            nt = 0
            for k in "lg":
                for src in [w_nat[k][:, c, :] for c in range(3)] + [wo_nat[k][:]]:
                    if nt >= 4:
                        pe.wait_ge(K["weight_evacuations"], v(nt - 3))
                    nc.tensor.transpose(ps[:, nt % 4, 0:P], src, ident[:]).then_inc(K["weight_transposes"], 1)
                    nt += 1
            pe.wait_ge(K["weight_evacuations"], v(nt))
            nc.tensor.matmul(ps[:, 4, 0:1], woT["l"][:], b_v["l"][:], start=True, stop=True).then_inc(K["weight_transposes"], 1)
            nc.tensor.matmul(ps[:, 5, 0:D], b_v["g"][:].broadcast_to([P, P]), woT["g"][:], start=True, stop=True).then_inc(K["weight_transposes"], 1)

            def front(i, p):
                pe.wait_ge(K["l_xn"], v(2 * i + p + 1))
                pe.wait_ge(K["l_xTs"], v(2 * i + p + FREE))
                for c in range(NC):
                    last = nc.tensor.transpose(ps[:, 6 + c // 4, c % 4 * P:(c % 4 + 1) * P], xn[p][:, c], ident[:])
                last.then_inc(K["l_xnT"], 1)
                pe.wait_ge(K["l_xTs"], v(2 * i + p + 1 + FREE))
                for c in range(NC):
                    if c >= 4:
                        pe.wait_ge(K["l_qkv"], v(NC * (2 * i + p) + c - 3 + FREE))
                    elif c == 0:
                        pe.wait_ge(K["l_qkv"], v(NC * (2 * i + p) + FREE))
                    nc.tensor.matmul(ps[:, c % 4, 0:3 * D], xT[p][:, c], wT["l"][:].rearrange("p c d -> p (c d)"), start=True, stop=False)
                    nc.tensor.matmul(ps[:, c % 4, 0:2 * D], ones_row[:], b_qk_l[:], start=False, stop=True).then_inc(K["l_proj"], 1)
            loop(pe, 2, lambda i: [front(i, p) for p in range(2)])
            pe.wait_ge(K["l_qkv"], NC * PR + FREE)

            def local(i):
                np_, nd = 0, 0
                pe.wait_ge(K["l_o"], v(i + FREE))
                for c in range(NC):
                    if c in DVE_C:
                        nd += 1
                        src = prod_d[nd - 1]
                        pe.wait_ge(K["l_prod_dve"], v(len(DVE_C) * i + nd))
                    else:
                        src = prod_p[(len(POOL_C) + np_) % 2]
                        np_ += 1
                        pe.wait_ge(K["l_prod_pool"], v(len(POOL_C) * (2 * i + 1) + np_))
                    for x in range(NC):
                        last = nc.tensor.matmul(ps[:, 4 + c // 4, c % 4 * P:(c % 4 + 1) * P], ident[:], src[:, x], start=x == 0, stop=x == NC - 1)
                    last.then_inc(K["l_acc"], 1)
                pe.wait_ge(K["l_o"], v(i + 1 + FREE))
                for c in range(NC):
                    last = nc.tensor.transpose(ps[:, 6 + c // 4, c % 4 * P:(c % 4 + 1) * P], o_l[:, c], ident[:])
                last.then_inc(K["l_oT"], 1)
                pe.wait_ge(K["l_oTs"], v(i + 1))
                pe.wait_ge(K["l_loc"], v(2 * i + FREE))
                for h in range(2):
                    last = nc.tensor.matmul(ps[:, h, :], woT["l"][:], oT_l[:, 4 * h:4 * h + 4, :].rearrange("p c n -> p (c n)"), start=True, stop=True)
                last.then_inc(K["l_out"], 1)
            loop(pe, PR, local)

            pe.wait_ge(K["l_loc"], 2 * PR + FREE)
            pe.sem_inc(K["pv"], PV0)

            def project(c, w):
                pe.wait_ge(K["xs"], v(c + 1))
                if w < 2:
                    nc.tensor.matmul(ps[:, M, :], wT["g"][:, w, :], xs[:], start=True, stop=True).then_inc(K["m_full"], 1)
                else:
                    for t in range(T):
                        last = nc.tensor.matmul(ps[:, M, t * P:(t + 1) * P], xs[:, t * P:(t + 1) * P], wT["g"][:, 2, :], start=True, stop=True)
                    last.then_inc(K["m_full"], 1)

            def max_transposes(b, r, g):
                pe.wait_ge(K["nm"], v(NG * b + g + 1))
                for t in range(T):
                    last = nc.tensor.transpose(ps_mb[0:NPART * NJ, t * P:(t + 1) * P], nm[r][:, g, t], identb[:])
                last.then_inc(K["m_full"], 1)

            def out_transposes(b, g):
                pe.wait_ge(K["ou"], v(NG * b + g + 1 + FREE))
                for t in range(T):
                    last = nc.tensor.transpose(ps[:, M, t * P:(t + 1) * P], ou[g % 2][:, t * P:(t + 1) * P], ident[:])
                last.then_inc(K["m_full"], 1)

            def on_transposes():
                for t in range(T):
                    last = nc.tensor.transpose(ps[:, M, t * P:(t + 1) * P], on[:, t], ident[:])
                last.then_inc(K["m_full"], 1)

            def out_projection():
                for t in range(T):
                    last = nc.tensor.matmul(ps[:, M, t * P:(t + 1) * P], onT[:, t * P:(t + 1) * P], woT["g"][:], start=True, stop=True)
                last.then_inc(K["m_full"], 1)

            def scores(b, r, s):
                g, qt, j = s // 16, s // 4 % 4, s % 4
                h = g * NJ + j
                pe.wait_ge(K["max"], v(MAX0 + SC * b + prev_use(s) + 1))
                nc.tensor.matmul(ps[:, SS + s % 3, :], qpk[r][0:PROD, h, qt * P:(qt + 1) * P], kpk[r][0:PROD, h, :], start=True, stop=True).then_inc(K["s"], 1)

            def scores_t(b, r, q):
                g, kt, j = q // 16, q // 4 % 4, q % 4
                h = g * NJ + j
                if q % 16 == 0:
                    pe.wait_ge(K[f"mr{g}"], v(16 * (b + 1) + FREE))
                pe.wait_ge(K["exp"], v(SC + SC * b + prev_use(q) + 1))
                nc.tensor.matmul(ps[:, ST + q % 3, :], kpk[r][:, h, kt * P:(kt + 1) * P], qpk[r][:, h, :], start=True, stop=True).then_inc(K["st"], 1)

            def pv(b, r, n):
                g, kt = n // 4, n % 4
                if kt == 0:
                    pe.wait_ge(K["ou"], v(NG * b + g + FREE))
                pe.wait_ge(K["exp"], v(SC + SC * b + 4 * (n + 1)))
                for j in range(NJ):
                    last = nc.tensor.matmul(ps[32 * j:32 * j + 32, PV, :], va[r][:, kt, g * NJ + j, :], eb[(4 * n + j) % 8][:], start=kt == 0, stop=kt == 3, tile_position=(0, 32 * j))
                last.then_inc(K["pv"], 1)

            k = 0
            for c in range(2):
                for w in range(3):
                    pe.wait_ge(K["m_free"], v(k))
                    project(c, w)
                    k += 1
            pe.wait_ge(K["pk0"], 16 * LOADS)
            for s in range(SC):
                scores(0, 0, s)
            for g in range(3):
                pe.wait_ge(K["m_free"], v(k))
                max_transposes(0, 0, g)
                k += 1
            pe.wait_ge(K["dummy_ready"], 3)

            def half(b, r, n_next, n_after, i):
                todo = tasks(n_next, n_after)
                r1, r2 = (r + 1) % R, (r + 2) % R
                for n in range(STEPS):
                    if n == 0 and n_next:
                        pe.wait_ge(K[f"pk{r1}"], v(16 * LOADS * (i + 1 + (1 if r == R - 1 else 0))))
                    for j in range(NJ):
                        scores_t(b, r, 4 * n + j)
                        if n_next:
                            scores(b + 1, r1, 4 * n + j)
                        if j == 1 and n > 0:
                            pv(b, r, n - 1)
                    for k, (m, t) in enumerate(todo):
                        if m != n:
                            continue
                        pe.wait_ge(K["m_free"], v(m_base(b) + k))
                        if t == "mt3":
                            max_transposes(b, r, 3)
                        elif t[:2] == "mt":
                            max_transposes(b + 1, r1, int(t[2]))
                        elif t == "ot3":
                            out_transposes(b - 1, 3)
                        elif t[:2] == "ot":
                            out_transposes(b, int(t[2]))
                        elif t == "tt":
                            on_transposes()
                        elif t == "dd":
                            out_projection()
                        else:
                            project(b + 2, "qkv".index(t[1]))
                pv(b, r, STEPS - 1)

            def three(i):
                for r in range(R):
                    half(Count(i, R, r, pe), r, True, True, i)
            loop(pe, 2, three)
            half(6, 0, True, False, 2)
            half(7, 1, False, False, 2)
            for k, f in enumerate((lambda: out_transposes(B - 1, 3), on_transposes, out_projection)):
                pe.wait_ge(K["m_free"], v(m_base(B) + k))
                f()

            def experts_pe(f):
                def front(i):
                    for p in range(2):
                        g = 2 * i + p
                        pe.wait_ge(K["e_xn"], run(f, "xn") + g + 1)
                        pe.wait_ge(K["e_xTs"], run(f, "xTs") + 2 * i)
                        for t in range(T):
                            last = nc.tensor.transpose(ps[:, p, t * P:(t + 1) * P], f_xn[p][:, t], ident[:])
                        last.then_inc(K["e_xnT"], 1)
                        pe.wait_ge(K["e_xTs"], run(f, "xTs") + g + 1)
                        for t in range(T):
                            last = nc.tensor.matmul(ps[:, 4, bass.ds((g * T + t) * E, E)], f_xT[p][:, t * P:(t + 1) * P], wr[:], start=True, stop=True)
                        last.then_inc(K["e_logits"], 1)
                loop(pe, NT // T // 2, front)
                pe.wait_ge(K["e_onehot"], run(f, "onehot") + 1)
                one = f_oneb.rearrange("p e t -> p (e t)")
                nc.tensor.matmul(ps[:, 5, 0:E * NT], uptob[:], one, start=True, stop=True)
                nc.tensor.matmul(ps[:, 6, 0:E * NT], onesb[:], one, start=True, stop=True).then_inc(K["e_counts"], 1)
                pe.wait_ge(K["e_routed"], run(f, "routed") + 1)

                def expert(i):
                    for p in range(2):
                        e = 2 * i + p
                        pe.wait_ge(K[f"e_ex{p}"], run(f, f"ex{p}") + 48 * (i + 1))
                        pe.wait_ge(K["e_xeTs"], run(f, "xeTs") + 2 * i)
                        for t in range(T):
                            last = nc.tensor.transpose(ps[:, p, t * P:(t + 1) * P], f_xe[p][:, t], ident[:])
                        last.then_inc(K["e_xe_T"], 1)
                        pe.wait_ge(K["e_xeTs"], run(f, "xeTs") + e + 1)
                        pe.wait_ge(K["e_hT"], run(f, "hT") + 2 * i)
                        nc.tensor.matmul(ps[:, 2 + p, :], f_w[p][:, 0], f_xeT[p], start=True, stop=True).then_inc(K["e_h"], 1)
                        pe.wait_ge(K["e_hT"], run(f, "hT") + e + 1)
                        pe.wait_ge(K["e_ye"], run(f, "ye") + 2 * i)
                        for t in range(T):
                            last = nc.tensor.matmul(ps[:, 4 + p, t * P:(t + 1) * P], f_hT[p][:, t * P:(t + 1) * P], f_w[p][:, 1], start=True, stop=True)
                        last.then_inc(K["e_y"], 1)
                loop(pe, E // 2, expert)
            experts_pe(0)
            pe.wait_ge(K["m_w"], 16 * N_MAMBA)
            for n, (src, rows, cols) in enumerate(W_IN):
                nc.tensor.transpose(ps[0:cols, n % 8, 0:rows] if n < 8 else ps[0:cols, 0, 0:rows], src, ident[0:rows, 0:rows])\
                    .then_inc(K["m_wT"], 1)
                if n == 7:
                    pe.wait_ge(K["m_wTs"], 1)
            pe.wait_ge(K["m_wTs"], len(W_IN))

            def front(b, p):
                yield
                pe.wait_ge(K["m_xn"], v(b + 1))
                pe.wait_ge(K["m_zg"], v(T * b))
                for t in range(T):
                    last = nc.tensor.transpose(ps[:, 0, t * P:(t + 1) * P], m_xn[:, t], ident[:])
                last.then_inc(K["m_xT"], 1)
                pe.wait_ge(K["m_xTs"], v(b + 1))

                def project(c):
                    nc.tensor.matmul(ps[:, (1 + c) % 3, :], wx[:, c], m_xT, start=True, stop=True).then_inc(K["m_proj"], 1)

                def project_z(t):
                    nc.tensor.matmul(ps[:, (5 + t) % 3, 0:2 * P + H2], m_xT[:, t * P:(t + 1) * P], wz, start=True, stop=True).then_inc(K["m_z"], 1)
                for c in range(3):
                    project(c)
                yield
                pe.wait_ge(K["m_conv"], v(4 * b + 1))
                project(3)
                yield
                for t in range(T):
                    if t < 3:
                        pe.wait_ge(K["m_conv"], v(4 * b + 2 + t))
                    else:
                        pe.wait_ge(K["m_zg"], v(T * b + 1))
                    project_z(t)
                    if t < 3:
                        yield
                yield
                yield

            def back(b, p):
                def at(c, h):
                    return ps[:, 3 + c // 2, (c % 2 * 2 + h) * P:(c % 2 * 2 + h + 1) * P]
                pe.wait_ge(K["m_silu"], v(4 * b + 4))
                pe.wait_ge(K["m_y1"], v(2 * b + FREE))
                for c in range(T):
                    for h in range(H2):
                        last = nc.tensor.transpose(at(c, h), m_ch[p][:, h, c * P:(c + 1) * P], ident[:])
                last.then_inc(K["m_xtok"], 1)
                pe.wait_ge(K["m_yTs"], v(b + FREE))
                for c in range(T):
                    last = nc.tensor.transpose(ps[:, 5, c * P:(c + 1) * P], m_ch[p][:, 2, c * P:(c + 1) * P], ident[:])
                last.then_inc(K["m_btok"], 1)
                for c in range(T):
                    last = nc.tensor.matmul(ps[:, 6, c * P:(c + 1) * P], m_ch[p][:, 2, c * P:(c + 1) * P], m_ch[p][:, 3, c * P:(c + 1) * P], start=True, stop=True)
                last.then_inc(K["m_g"], 1)
                yield
                pe.wait_ge(K["m_L"], v(b + 1))
                pe.wait_ge(K["m_btoks"], v(b + 1))
                pe.wait_ge(K["m_gm"], v(b + 1))
                for c in range(T):
                    for h in range(H2):
                        last = nc.tensor.matmul(ps[:, 5 + c // 2, (c % 2 * 2 + h) * P:(c % 2 * 2 + h + 1) * P], m_L[:, c, h], upto[:], start=True, stop=True)
                last.then_inc(K["m_dif"], 1)
                pe.wait_ge(K["m_xtoks"], v(b + 1))
                for c in range(T):
                    for h in range(H2):
                        last = nc.tensor.matmul(at(c, h), m_dA[:, c, h:h + 1].broadcast_to([P, P]), upto[:], start=True, stop=True)
                last.then_inc(K["m_row"], 1)
                yield
                pe.wait_ge(K["m_el"], v(b + 1))
                pe.wait_ge(K["m_x"], v(b + FREE))
                pe.wait_ge(K["m_xst"], v(b + 1))
                for c, dst in enumerate((ps[:, 5, 0:2 * P], ps[:, 5, 2 * P:4 * P], ps[:, 7, 2 * P:4 * P])):
                    last = nc.tensor.matmul(dst, m_btok[:, c], m_xst[:, c].rearrange("p h n -> p (h n)"), start=True, stop=True)
                last.then_inc(K["m_P"], 1)
                yield
                pe.wait_ge(K["m_m"], v(b + 1))
                pe.wait_ge(K["m_erow"], v(b + 1))
                pe.wait_ge(K["m_S"], v(b + 1))
                pe.wait_ge(K["m_ce"], v(b + 1))
                for c in range(T):
                    for h in range(H2):
                        last = nc.tensor.matmul(at(c, h), m_m[:, c, h], m_xtok[:, c, h], start=True, stop=c == 0)
                        if c:
                            last = nc.tensor.matmul(at(c, h), m_ce[:, c, h], m_S[:, c - 1, h], start=False, stop=True)
                last.then_inc(K["m_Y"], 1)
                yield
                yield
                pe.wait_ge(K["m_y"], v(b + 1))
                pe.wait_ge(K["m_gm"], v(b + 1))
                for t in range(T):
                    for k in range(2):
                        last = nc.tensor.transpose(ps[:, 5 + k, t * P:(t + 1) * P], m_y[:, t, k * P:(k + 1) * P], ident[:])
                last.then_inc(K["m_yT"], 1)
                pe.wait_ge(K["m_yTs"], v(b + 1 + FREE))
                for t in range(T):
                    for k in range(2):
                        last = nc.tensor.matmul(ps[:, 7, t * P:(t + 1) * P], m_yT[:, k, t * P:(t + 1) * P], wo2[:, k], start=k == 0, stop=k == 1)
                last.then_inc(K["m_out"], 1)
                yield
                yield
            mamba(pe, front, back)
            experts_pe(1)


N_WEIGHTS = 2 * 3 + 1 + 2 * HD + 2 + 2
N_MAMBA = 11
_INS = (["attn_a_x"] + [f"attn_a_{w}_{k}" for k in "lg" for w in ("w_in", "b_in", "w_out", "b_out")]
        + [f"ffn_{w}" for w in ("Wr", "br", "W1", "b1", "W2", "b2")]
        + [f"attn_b_{w}" for w in ("in_proj_w", "conv_w", "conv_b", "dt_bias", "A_log", "D_param", "norm_w",
                                   "out_proj_w", "out_proj_b")])


def kernel(**inputs):
    import numpy as np
    import concourse.bacc as bacc
    from concourse.bass_utils import run_bass_kernel_spmd

    nc = bacc.Bacc("TRN2", target_bir_lowering=False, num_devices=1)
    arrays, args = {}, {}
    for n in _INS:
        arrays["in_" + n] = np.ascontiguousarray(inputs["L0_" + n])
        args[n] = nc.dram_tensor("in_" + n, arrays["in_" + n].shape, F32, kind="ExternalInput").ap()
    out = nc.dram_tensor("out_0", (B, S, D), F32, kind="ExternalOutput").ap()
    build(nc, args, out)
    r = run_bass_kernel_spmd(nc, [arrays], core_ids=[0])
    return r.results[0]["out_0"]
```

```python
from contextlib import ExitStack

import concourse.bass as bass
from concourse import mybir

F32 = mybir.dt.float32
BF16 = mybir.dt.bfloat16
U32 = mybir.dt.uint32
ALU = mybir.AluOpType
ACT = mybir.ActivationFunctionType
AX = mybir.AxisListType

P = 128
B = 8
S = 512
D = 128
T = S // P
H = 16
HD = D // H
NG = 4
NJ = H // NG
W = 64
NC = S // W
PR = B // 2
SCALE = HD ** -0.5
EPS = 1e-5
NPART = 3
PROD = NPART * NPART * HD
KA = PROD + NPART
LOADS = NPART * (1 + NPART)
STEPS = NG * T
SC = 4 * STEPS
DVE_QK, POOL_QK = (0, 3, 6), (1, 2, 4, 5, 7)
DVE_PV, POOL_PV = (0, 2, 4, 6), (1, 3, 5, 7)
E = 8
EQ = 4
NT = B * T
CAP = B * S // E
H2 = 2
TAPS = 4
FREE = 1
R = 3


class Count:

    def __init__(self, i, a, b, eng, made=None):
        self.i, self.a, self.b, self.eng = i, a, b, eng
        self.made = {} if made is None else made

    def __add__(self, n):
        return Count(self.i, self.a, self.b + n, self.eng, self.made)

    def __sub__(self, n):
        return self + -n

    def __mul__(self, n):
        return Count(self.i, self.a * n, self.b * n, self.eng, self.made)

    __radd__, __rmul__ = __add__, __mul__

    def value(self):
        if self.a not in self.made:
            self.made[self.a] = self.eng.snap(self.i * self.a)
        return self.made[self.a] + self.b


def v(x):
    return x.value() if isinstance(x, Count) else x


def at_start(i):
    return isinstance(i, int) and i == 0


def build(nc, a, out):
    ctx = ExitStack()
    with ctx:
        def sb(name, shape, dt=F32):
            return ctx.enter_context(nc.sbuf_tensor(name, shape, dt))

        def sem(name):
            return ctx.enter_context(nc.semaphore(name))

        class Chain:

            def __init__(self, eng, name):
                self.eng, self.sem, self.base, self.n = eng, sem(name), 0, 0

            def __call__(self, ins):
                self.n += 1
                ins.then_inc(self.sem, 1)

            def settle(self):
                self.eng.wait_ge(self.sem, v(self.base + self.n))

        def loop(eng, count, body, chain=None, per=0):
            if chain is not None:
                b0 = chain.base + chain.n
            with eng.Fori(0, count) as i:
                if chain is not None:
                    chain.base, chain.n = Count(i, per, b0, eng), 0
                body(i)
                if chain is not None:
                    assert chain.n == per, (chain.n, per)
            if chain is not None:
                chain.base, chain.n = 0, b0 + count * per

        xf = a["attn_a_x"]
        parts_dram = [nc.dram_tensor(f"parts_{w}", (B, NPART * HD, H, S), BF16).ap() for w in "qk"]

        ident = sb("ident", [P, P])
        identb = sb("identb", [P, P], BF16)
        wT = {k: sb(f"wT_{k}", [P, 3, P]) for k in "lg"}
        woT = {k: sb(f"woT_{k}", [P, P]) for k in "lg"}
        b_qk_l = sb("b_qk_l", [1, 2 * D])
        ones_row = sb("ones_row", [1, P])
        b_qk_g = sb("b_qk_g", [P, 2])
        b_v = {k: sb(f"b_v_{k}", [P, 1]) for k in "lg"}
        b_out_l = sb("b_out_l", [P, 1])
        bias_l = sb("bias_l", [P, 1])
        b_out_g = sb("b_out_g", [P, D])
        bias_g = sb("bias_g", [P, D])
        halfneg = sb("halfneg", [P, 64])
        eps = sb("eps", [P, T])
        x1 = sb("x1", [P, (B + 1) * T, D])
        locT = sb("locT", [P, B, S])

        WORDS = 41536
        arena = sb("arena", [P, WORDS])

        class Lay:
            def __init__(self):
                self.at = 0

            def __call__(self, shape, dt=F32, rows=P):
                n, per = 1, 2 if dt == BF16 else 1
                for x in shape:
                    n *= x
                words = -(-n // per)
                w = arena[0:rows, self.at:self.at + words]
                self.at += words
                assert self.at <= WORDS, self.at
                if dt != F32:
                    w = w.bitcast(dt)
                names = "abcd"[:len(shape)]
                if len(shape) > 1:
                    w = w.rearrange("p (" + " ".join(names) + ") -> p " + " ".join(names),
                                    **{x: y for x, y in zip(names, shape)})
                return w

        lay = Lay()
        xb = [lay([NC, D]) for p in range(2)]
        xn = [lay([NC, D]) for p in range(2)]
        xT = [lay([NC, P]) for p in range(2)]
        qkv = lay([PR, NC, 3 * D])
        prod_p = [lay([NC, D]) for p in range(2)]
        prod_d = [lay([NC, D]) for p in range(len(DVE_PV) - 1)] + [xT[0]]
        qk_d, qk_p = xn, xb
        sc = lay([NC, H, NC])
        sx = lay([NC, H, NC])
        pe_ = lay([NC, H, NC])
        o_l = lay([NC, D])
        oT_l = lay([NC, P])
        smax = lay([NC, H])
        ssum = lay([NC, H])
        srec = lay([NC, H])
        st6 = lay([NC, 6])
        mv = [lay([NC, 2]) for p in range(2)]
        ve = lay([NC])
        rs = [lay([NC]) for p in range(2)]
        w_all = lay([8, P])
        w_nat = {k: w_all[:, 4 * n:4 * n + 3] for n, k in enumerate("lg")}
        wo_nat = {k: w_all[:, 4 * n + 3] for n, k in enumerate("lg")}
        prod_p = prod_p + [w_all, xT[1]]
        top = lay.at
        va = [lay([T, H, 32]) for r in range(R)]
        ou = [lay([S]) for g in range(2)]
        on = lay([T, D])
        xs = lay([S])
        ff = [lay([S]) for w in "qk"]
        rres = lay([S])
        parts = [lay([NPART, S], BF16) for w in "qk"]
        nr = lay([T, NJ])
        rc = lay([T, NJ])
        lay = Lay()
        qpk = [lay([H, S], BF16, KA) for r in range(R)]
        kpk = [lay([H, S], BF16, KA) for r in range(R)]
        eb = [lay([S]) for r in range(8)]
        mx = [lay([T, H]) for r in range(R)]
        nm = [lay([NG, T, NPART * NJ], BF16) for r in range(R)]
        mrow = [lay([S], BF16, NPART * NJ) for g in range(2)]
        onT = lay([S])
        assert lay.at <= top

        lay = Lay()
        f_gk = lay([NT])
        f_yg = [lay([T, D]) for p in range(2)]
        f_xn = [lay([T, D]) for p in range(2)]
        f_xT = [lay([S]) for p in range(2)]
        f_st = lay([T, 6])
        f_mv = lay([NT, 2])
        f_mv4 = lay([T, 2])
        f_ve = lay([T])
        f_rs = lay([NT])
        f_lg = lay([NT, E])
        f_m = lay([NT])
        f_ex = lay([NT, E])
        f_sum = lay([NT])
        f_gate = lay([NT])
        f_pick = lay([NT, E])
        f_one = lay([E, NT])
        f_oneb = lay([E, NT], BF16)
        f_incl = lay([E * NT])
        f_pos = lay([E, NT])
        f_at = lay([NT])
        f_e0 = lay([NT])
        f_keep = lay([NT])
        f_slot = lay([NT])
        f_si = lay([NT])
        f_gi = lay([NT])
        f_i4 = [lay([T], U32) for p in range(2)]
        f_none = lay([T])
        f_back = [lay([T], U32) for q in range(EQ)]
        f_rg = lay([NT])
        f_xg = [lay([T, D + 1]) for p in range(2)]
        f_xe = [lay([T, D + 1]) for q in range(EQ)]
        f_w = [lay([2, D]) for q in range(EQ)]
        f_b1 = lay([E])
        f_b2 = lay([E, D])
        f_xeT = [lay([S]) for p in range(2)]
        f_hT = [lay([S]) for p in range(2)]
        f_ye = [lay([T, D]) for p in range(2)] + f_xn
        zn = lay([2, P])
        xbn = lay([4, P])
        dtn = lay([P], F32, H2)
        on_nat = lay([2 * P])
        wz = lay([2 * P + H2])
        wx = lay([4, P])
        wo2 = lay([2, P])
        cwf = lay([4, TAPS])
        cw = lay([4, TAPS])
        cbf = lay([4])
        cb = lay([4])
        nw = lay([2])
        dtb = lay([H2])
        alog = lay([H2])
        aneg = lay([H2])
        dpar = lay([H2])
        ob = lay([D])
        after = lay([P])
        m_st = lay([T, 6])
        m_mv = lay([T, 2])
        m_ve = lay([T])
        m_rs = lay([T])
        m_xn = lay([T, D])
        m_xT = lay([S])
        m_acc = lay([4, S])
        m_th = lay([4, S])
        m_ch = [lay([4, S]) for p in range(2)]
        m_zt = lay([T, 2 * P])
        m_g = [lay([T, 2 * P]) for p in range(2)]
        m_raw = [lay([T, H2]) for p in range(2)]
        m_abs = lay([T, H2])
        m_u = lay([T, H2])
        m_pos = lay([T, H2])
        m_s = lay([T, H2])
        m_s2 = lay([T, H2])
        m_q = lay([T, H2])
        m_dt = lay([T, H2])
        m_dA = lay([T, H2])
        m_xdt = lay([T, H2, P])
        m_xtok = lay([T, H2, P])
        m_btok = lay([T, P])
        m_L = lay([T, H2, P])
        m_erow = lay([T, H2, P])
        m_el = lay([T, H2, P])
        m_ce = lay([T, H2, P])
        m_gm = lay([T, P])
        m_m = lay([T, H2, P])
        m_xst = lay([T - 1, H2, P])
        m_S = lay([T - 1, H2, P])
        m_y1 = lay([T, H2, P])
        m_y = lay([T, 2 * P])
        m_sq = lay([2 * P])
        m_ssq = lay([T])
        m_rv = lay([T])
        m_ri = lay([T])
        m_yT = lay([2, S])
        W_IN = ([(zn[:, c], P, P) for c in range(2)] + [(xbn[:, c], P, P) for c in range(4)] + [(dtn, H2, P)]
                + [(on_nat[:, k * P:(k + 1) * P], P, P) for k in range(2)])
        W_EVAC = ([(wz[:, c * P:(c + 1) * P], c, P, P) for c in range(2)] + [(wx[:, c], 2 + c, P, P) for c in range(4)]
                  + [(wz[:, 2 * P:], 6, P, H2), (wo2[:, 0], 7, P, P), (wo2[:, 1], 0, P, P)])
        slot_x = nc.dram_tensor("slot_x", (E * CAP, D + 1), F32).ap()
        token_y = nc.dram_tensor("token_y", (B * S, D), F32).ap()
        wr = sb("wr", [P, E])
        br = sb("br", [P, E])
        prefer = sb("prefer", [P, E])
        first_slot = sb("first_slot", [P, E])
        not_first = sb("not_first", [P, E, NT])
        upto = sb("upto", [P, P])
        uptob = sb("uptob", [P, P], BF16)
        onesb = sb("onesb", [P, P], BF16)
        zeros = sb("zeros", [P, D + 1])
        number = sb("number", [P, NT])

        ps = ctx.enter_context(nc.psum_tensor("ps", [P, 8, S], F32))
        ST, SS, PV, M = 0, 3, 6, 7
        ps_mb = ps[:, M, :].bitcast(BF16)

        names = ["weights_in", "residual_in", "identity_ready", "constants_ready", "bf_identity_ready", "weight_transposes",
                 "weight_evacuations", "bias_made", "x1_biased",
                 "lxb_in0", "lxb_in1", "l_mv", "l_rs", "l_xn", "l_xnT", "l_xTs", "l_proj", "l_qkv", "l_prod_pool", "l_prod_qk",
                 "l_prod_dve", "l_shift", "l_exp", "l_acc",
                 "l_o", "l_oT", "l_oTs", "l_out", "l_loc", "l_qk_used",
                 "ones_rows", "ones_made", "values_ready", "dummy_ready", "s", "max", "nm", "st", "exp", "pv", "ou", "xs", "p1",
                 "parts_q", "parts_k", "stored", "pk0", "pk1", "pk2", "mr0", "mr1", "mr2", "mr3", "rc",
                 "m_full", "m_free", "waited", "out_stored", "moe_const", "upto_ones", "numbers_ready", "slots_cleared", "y_cleared"]
        K = {n: sem(n) for n in names}

        FN = ["mv", "rs", "xn", "xnT", "xTs", "logits", "shift", "exp", "onehot", "counts", "routed", "xg", "scat0", "scat1",
              "exp_b", "ex0", "ex1", "ex2", "ex3", "xe_T", "xeTs", "h", "hT", "y", "ye", "st0", "st1", "st2", "st3", "gath0", "gath1", "x"]
        for n_ in FN:
            K["e_" + n_] = sem(f"moe_{n_}")
        ADDS = dict({n_: 8 for n_ in FN}, shift=1, exp=1, onehot=1, counts=1, routed=1, exp_b=32)
        for p in range(2):
            ADDS.update({f"scat{p}": 16 * NT // 2, f"gath{p}": 16 * B // 2})

        for q in range(EQ):
            ADDS.update({f"ex{q}": 48 * E // EQ, f"st{q}": 16 * NT // EQ})
        E_FREE = ("xnT", "xTs", "logits", "xeTs", "h", "hT", "ye")

        def run(f, name):
            return ADDS[name] * f + (FREE if name in E_FREE else 0)

        MN = ["w", "wT", "wTs", "cw", "cst", "mv", "rs", "xn", "xT", "xTs", "proj", "acc", "conv", "th", "silu", "z", "zt", "zg", "abs", "u", "dA",
              "xtok", "xtoks", "btok", "btoks", "g", "gm", "L", "row", "dif", "erow", "el", "xdt", "xst", "m", "ce", "P", "S", "Y",
              "y1", "y", "ssq", "ri", "yT", "yTs", "out", "x", "bias"]
        for n_ in MN:
            K["m_" + n_] = sem("mamba_" + n_)

        block = ctx.enter_context(nc.Block())

        ORDER = "bffbffbbffbfbfb"

        def mamba(eng, front, back, chain=None, per=0):
            def both(b, p):
                f, g = front(b + 1, 1 - p), back(b, p)
                for s_ in ORDER:
                    next(f if s_ == "f" else g)

            for _ in front(0, 0):
                pass

            both(0, 0)

            def two(i):
                for p in range(2):
                    both(Count(i, 2, p + 1, eng), 1 - p)
            loop(eng, B // 2 - 2, two, chain, per)
            both(B - 3, 1)
            both(B - 2, 0)
            for _ in back(B - 1, 1):
                pass


        def apart(eng):
            eng.sem_inc(K["waited"], 1)

        def free_at(c):
            return STEPS * (c + 1)

        PV0 = R * STEPS
        MAX0 = (1 + R) * SC

        def prev_use(q):
            return q - 3 if q >= 3 else max(x for x in range(SC) if x % 3 == q % 3) - SC

        TASKS = [(1, "mt3"), (2, "ot3"), (3, "aq"), (4, "tt"), (5, "mt0"), (6, "ot0"), (7, "dd"), (8, "ak"),
                 (9, "mt1"), (10, "ot1"), (11, "av"), (13, "mt2"), (14, "ot2")]
        PRO = 6 + 3

        def tasks(n_next, n_after):
            return [(n, t) for n, t in TASKS
                    if (n_next or t not in ("mt0", "mt1", "mt2")) and (n_after or t[0] != "a")]

        def m_base(b):
            if isinstance(b, int) and b == B - 1:
                return PRO + len(TASKS) * (B - 2) + len(tasks(True, False))
            if isinstance(b, int) and b == B:
                return m_base(B - 1) + len(tasks(False, False))
            return PRO + len(TASKS) * b

        def bc(t, n):
            return t.rearrange("p a (b o) -> p a b o", o=1).broadcast_to([P, t.shape[1], t.shape[2], n])

        def qk_product(eng, i, c, dst):
            q = qkv[:, bass.ds(i, 1), c, 0:D].broadcast_to([P, NC, D])
            k = qkv[:, bass.ds(i, 1), :, D:2 * D].rearrange("p o c d -> p (o c) d")
            return eng.tensor_tensor(dst, q, k, ALU.mult)

        def pv_product(eng, i, c, dst):
            vals = qkv[:, bass.ds(i, 1), :, 2 * D:3 * D].rearrange("p o c (h d) -> p (o c) h d", h=H)
            pr = pe_[:, c].rearrange("p h (c o) -> p c h o", o=1).broadcast_to([P, NC, H, HD])
            return eng.tensor_tensor(dst.rearrange("p c (h d) -> p c h d", h=H), vals, pr, ALU.mult)

        def halves(eng, half, chain=None, per=0):
            def three(i):
                for r in range(R):
                    half(Count(i, R, r, eng), r, True, True)
            loop(eng, 2, three, chain, per)
            half(6, 0, True, False)
            half(7, 1, False, False)

        @block.sync
        def _(sp):
            for s_ in ("l_acc", "l_proj", "l_xnT", "l_oT", "l_o", "l_loc", "l_xTs", "l_qkv", "ou", "m_y1", "m_yTs", "m_x", "mr0", "mr1", "mr2", "mr3", *("e_" + x for x in E_FREE)):
                sp.sem_inc(K[s_], FREE)
            n = 0
            def ld(dst, src, **how):
                nonlocal n
                sp.dma_start(dst, src, **how).then_inc(K["weights_in"], 16)
                n += 1

            def load_x(pr, p):
                for h in range(2):
                    sp.dma_start(xb[p][h * W:(h + 1) * W],
                                 xf[bass.ds(pr * 2 + h, 1)].rearrange("o (c i) d -> i (o c) d", i=W)
                                 ).then_inc(K[f"lxb_in{p}"], 16)
            for p in range(2):
                load_x(p, p)
            for k in "lg":
                ld(w_nat[k][:], a[f"attn_a_w_in_{k}"].rearrange("(c p) d -> p c d", p=P))
                ld(wo_nat[k][:], a[f"attn_a_w_out_{k}"])
                bi = a[f"attn_a_b_in_{k}"]
                ld(b_v[k][:], bi[2 * D:3 * D].rearrange("(p o) -> p o", o=1))
            ld(b_qk_l[:], a["attn_a_b_in_l"][0:2 * D].rearrange("(o d) -> o d", o=1))
            for c in range(2):
                for d in range(HD):
                    ld(b_qk_g[d * H:(d + 1) * H, c:c + 1],
                       a["attn_a_b_in_g"][c * D:(c + 1) * D].rearrange("(h d one) -> d h one", h=H, one=1)[d],
                       allow_slow_non_contiguous=True)
            ld(b_out_l[:], a["attn_a_b_out_l"].rearrange("(p o) -> p o", o=1))
            ld(b_out_g[:], a["attn_a_b_out_g"].rearrange("(o d) -> o d", o=1).broadcast_to([P, D]))
            ld(wr[:], a["ffn_Wr"])
            ld(br[:], a["ffn_br"].rearrange("(o d) -> o d", o=1).broadcast_to([P, E]))
            assert n == N_WEIGHTS, n
            sp.dma_start(x1[:, T:], xf.rearrange("b (t p) d -> p (b t) d", p=P)).then_inc(K["residual_in"], 16)
            for p in range(2):
                sp.wait_ge(K["l_xn"], v(p + 1))
                load_x(2 + p, p)

            def pack(c, r):
                for w in range(2):
                    sp.wait_ge(K["parts_" + "qk"[w]], v(c + 1))
                    sp.dma_start(parts_dram[w][bass.ds(v(c), 1)].rearrange("o (a d) h n -> (o d h) a n", a=NPART),
                                 parts[w][:]).then_inc(K["stored"], 16)
                sp.wait_ge(K["stored"], v(32 * (c + 1)))
                apart(sp)
                sp.wait_ge(K["pv"], v(free_at(c)))
                q, kk = (x[bass.ds(v(c), 1)].rearrange("o r h n -> (o r) h n") for x in parts_dram)
                for x in range(NPART):
                    sp.dma_start(qpk[r][x * NPART * HD:(x + 1) * NPART * HD], q).then_inc(K[f"pk{r}"], 16)
                    for y in range(NPART):
                        lo = (x * NPART + y) * HD
                        sp.dma_start(kpk[r][lo:lo + HD], kk[x * HD:(x + 1) * HD]).then_inc(K[f"pk{r}"], 16)

            sp.wait_ge(K["l_loc"], 2 * PR + FREE)
            sp.wait_ge(K["ones_made"], 1)
            for r in range(R):
                sp.dma_start(kpk[r][PROD:KA], onesb[0:NPART, :].rearrange("p (o n) -> p o n", o=1).broadcast_to([NPART, H * S // P, P])
                             ).then_inc(K["ones_rows"], 16)

            def three(i):
                for r in range(R):
                    pack(Count(i, R, r, sp), r)
            loop(sp, 2, three)
            pack(6, 0)
            pack(7, 1)

            def setup_mamba():
                wi = a["attn_b_in_proj_w"]
                loads = [(zn, wi[0:2 * P].rearrange("(c p) d -> p c d", p=P), {}),
                         (xbn, wi[2 * P:6 * P].rearrange("(c p) d -> p c d", p=P), {}),
                         (dtn, wi[6 * P:6 * P + H2], {}),
                         (on_nat, a["attn_b_out_proj_w"], {}),
                         (cwf, a["attn_b_conv_w"].rearrange("(c p) o k -> p c (o k)", p=P), {}),
                         (cbf, a["attn_b_conv_b"].rearrange("(c p) -> p c", p=P), dict(allow_slow_non_contiguous=True)),
                         (nw, a["attn_b_norm_w"].rearrange("(c p) -> p c", p=P), dict(allow_slow_non_contiguous=True)),
                         (dtb, a["attn_b_dt_bias"].rearrange("(o h) -> o h", o=1).broadcast_to([P, H2]), {}),
                         (alog, a["attn_b_A_log"].rearrange("(o h) -> o h", o=1).broadcast_to([P, H2]), {}),
                         (dpar, a["attn_b_D_param"].rearrange("(o h) -> o h", o=1).broadcast_to([P, H2]), {}),
                         (ob, a["attn_b_out_proj_b"].rearrange("(o d) -> o d", o=1).broadcast_to([P, D]), {})]
                assert len(loads) == N_MAMBA
                for dst, src, how in loads:
                    sp.dma_start(dst, src, **how).then_inc(K["m_w"], 16)

            def experts_sp(f):
                def load_w(e, q):
                    for m, w in enumerate(("ffn_W1", "ffn_W2")):
                        sp.dma_start(f_w[q][:, m], a[w][e]).then_inc(K[f"e_ex{q}"], 16)

                def load(e, q):
                    sp.dma_start(f_xe[q], slot_x[e * CAP:(e + 1) * CAP].rearrange("(t p) d -> p t d", p=P)).then_inc(K[f"e_ex{q}"], 16)

                sp.wait_ge(K["e_routed"], run(f, "routed") + 1)
                sp.dma_start(f_b1, a["ffn_b1"].rearrange("e d -> d e"), allow_slow_non_contiguous=True).then_inc(K["e_exp_b"], 16)
                sp.dma_start(f_b2, a["ffn_b2"].rearrange("(o e) d -> o e d", o=1).broadcast_to([P, E, D])).then_inc(K["e_exp_b"], 16)
                for e in range(EQ):
                    load_w(e, e)
                if f == 0:
                    setup_mamba()
                for p in range(2):
                    sp.wait_ge(K[f"e_scat{p}"], run(f, f"scat{p}") + 16 * NT // 2)
                for e in range(EQ):
                    load(e, e)
                for e in range(EQ):
                    sp.wait_ge(K["e_ye"], run(f, "ye") + e + 1)
                    load_w(e + EQ, e)
                    load(e + EQ, e)

            def load_y(f, g, p):
                sp.dma_start(f_yg[p], token_y.rearrange("(g t p) d -> g p t d", t=T, p=P)[bass.ds(g, 1)].rearrange("o p t d -> p (o t) d")).then_inc(K[f"e_gath{p}"], 16)

            def load_ys(f):
                for q in range(EQ):
                    sp.wait_ge(K[f"e_st{q}"], run(f, f"st{q}") + 16 * NT // EQ)
                for p in range(2):
                    load_y(f, p, p)

                def two(i):
                    for p in range(2):
                        sp.wait_ge(K["e_x"], run(f, "x") + 2 * i + p + 1)
                        load_y(f, 2 * i + p + 2, p)
                return two

            experts_sp(0)
            two = load_ys(0)
            loop(sp, B // 2 - 1, two)
            experts_sp(1)
            two = load_ys(1)

            def store_out(b):
                sp.wait_ge(K["e_x"], B + b + 1)
                sp.dma_start(out[bass.ds(b, 1)].rearrange("o (t p) d -> p (o t) d", p=P), x1[:, bass.ds(T + b * T, T)]).then_inc(K["out_stored"], 16)

            def last(i):
                two(i)
                for p in range(2):
                    store_out(2 * i + p)
            loop(sp, B // 2 - 1, last)
            for p in range(2):
                store_out(B - 2 + p)
            sp.wait_ge(K["out_stored"], 16 * B)

        @block.gpsimd
        def _(pool):
            ch = Chain(pool, "pool_chain")
            nc.gpsimd.iota(number[:], [[P, NT]], base=1, channel_multiplier=1, allow_small_or_imprecise_dtypes=True).then_inc(K["numbers_ready"], 1)
            ch(nc.gpsimd.memset(ident[:], 0.0))
            ch(nc.gpsimd.memset(identb[:], 0.0))
            ch.settle()
            for t_, s_ in ((ident, "identity_ready"), (identb, "bf_identity_ready")):
                nc.gpsimd.affine_select(out=t_[:], in_=t_[:], compare_op=ALU.not_equal, fill=1.0, base=0,
                                        pattern=[[-1, P]], channel_multiplier=1).then_inc(K[s_], 1)
            pool.wait_ge(K["bf_identity_ready"], 1)
            pool.wait_ge(K["constants_ready"], 4)
            pool.wait_ge(K["upto_ones"], 2)
            for t_ in (upto, uptob):
                nc.gpsimd.affine_select(out=t_[:], in_=t_[:], compare_op=ALU.is_ge, fill=0.0, base=0,
                                        pattern=[[1, P]], channel_multiplier=-1).then_inc(K["moe_const"], 1)
            pool.wait_ge(K["moe_const"], 2)

            for r in range(R):
                ch(nc.gpsimd.memset(va[r][:], 0.0))
            ch.settle()
            for r in range(R):
                nc.gpsimd.memset(va[r][:, :, :, HD:HD + 1], 1.0).then_inc(K["values_ready"], 1)
            pool.wait_ge(K["values_ready"], R)

            def rstd(i, p):
                pool.wait_ge(K["l_mv"], v(2 * i + p + 1))
                apart(pool)
                ch(nc.gpsimd.tensor_scalar(ve[:], mv[p][:, :, 1], EPS, None, ALU.add))
                ch.settle()
                nc.gpsimd.tensor_tensor(rs[p][:], ve[:], halfneg[:, 0:NC], ALU.pow).then_inc(K["l_rs"], 1)
                pool.wait_ge(K["l_rs"], v(2 * i + p + 1))
                apart(pool)
            loop(pool, 2, lambda i: [rstd(i, p) for p in range(2)], ch, 2)

            def local_qk(i):
                pool.wait_ge(K["l_qkv"], v(NC * (i + 1) + FREE))
                for n, c in enumerate(POOL_QK):
                    if n >= 2:
                        pool.wait_ge(K["l_qk_used"], v(len(POOL_QK) * i + n - 1))
                    elif not at_start(i):
                        pool.wait_ge(K["l_qk_used"], v(len(POOL_QK) * i))
                    apart(pool)
                    qk_product(nc.gpsimd, i, c, qk_p[n % 2]).then_inc(K["l_prod_qk"], 1)
                    pool.wait_ge(K["l_prod_qk"], v(len(POOL_QK) * i + n + 1))
                apart(pool)

            def local_pv(i):
                pool.wait_ge(K["l_exp"], v(i + 1))
                pool.wait_ge(K["l_acc"], v(NC * i + FREE))
                apart(pool)
                for n, c in enumerate(POOL_PV):
                    if n == len(POOL_PV) - 1:
                        pool.wait_ge(K["l_qkv"], NC * PR + FREE)
                    pv_product(nc.gpsimd, i, c, prod_p[n]).then_inc(K["l_prod_pool"], 1)
                pool.wait_ge(K["l_prod_pool"], v(len(POOL_PV) * (i + 1)))
                apart(pool)

            pool.wait_ge(K["l_xn"], PR)
            local_qk(0)

            def local(i):
                local_pv(i)
                local_qk(i + 1)
            loop(pool, PR - 1, local)
            local_pv(PR - 1)

            pool.wait_ge(K["residual_in"], 16)
            pool.wait_ge(K["bias_made"], 2)
            nc.gpsimd.tensor_tensor(x1[:, T:], x1[:, T:], bias_g[:].rearrange("p (o d) -> p o d", o=1).broadcast_to([P, B * T, D]), ALU.add).then_inc(K["x1_biased"], 1)
            pool.wait_ge(K["x1_biased"], 1)

            def split(c, w):
                pool.wait_ge(K["p1"], v(2 * c + w + 1))
                ch(nc.gpsimd.tensor_tensor(rres[:], ff[w][:], parts[w][:, 0], ALU.subtract))
                ch.settle()
                apart(pool)
                ch(nc.gpsimd.tensor_copy(parts[w][:, 1], rres[:]))
                ch.settle()
                nc.gpsimd.tensor_tensor(parts[w][:, 2], rres[:], parts[w][:, 1], ALU.subtract).then_inc(K["parts_" + "qk"[w]], 1)
                pool.wait_ge(K["parts_" + "qk"[w]], v(c + 1))
                apart(pool)

            def neg_max(b, r, g):
                pool.wait_ge(K["max"], v(MAX0 + SC * b + 16 * (g + 1)))
                apart(pool)
                m = mx[r][:, :, g * NJ:(g + 1) * NJ]
                def part(x): return nm[r][:, g, :, x * NJ:(x + 1) * NJ]
                ch(nc.gpsimd.tensor_scalar(part(0), m, -1.0, None, ALU.mult))
                ch(nc.gpsimd.tensor_scalar(nr[:], m, -1.0, None, ALU.mult))
                ch.settle()
                ch(nc.gpsimd.tensor_tensor(nr[:], nr[:], part(0), ALU.subtract))
                ch.settle()
                apart(pool)
                ch(nc.gpsimd.tensor_copy(part(1), nr[:]))
                ch.settle()
                nc.gpsimd.tensor_tensor(part(2), nr[:], part(1), ALU.subtract).then_inc(K["nm"], 1)
                pool.wait_ge(K["nm"], v(NG * b + g + 1))
                apart(pool)

            for c in range(2):
                split(c, 0)
            for g in range(NG):
                neg_max(0, 0, g)

            def half(b, r, n_next, n_after):
                for g in range(NG):
                    if n_next:
                        neg_max(b + 1, (r + 1) % R, g)
                    if n_after and g < 2:
                        split(b + 2, g)
            halves(pool, half, ch, 3 * 20)

            def experts_pool(f):
                def rstd(i):
                    pool.wait_ge(K["e_mv"], run(f, "mv") + i + 1)
                    apart(pool)
                    ch(nc.gpsimd.tensor_tensor(f_ve, f_mv[:, bass.ds(i * T, T), 1], eps[:, 0:T], ALU.add))
                    ch.settle()
                    nc.gpsimd.tensor_tensor(f_rs[:, bass.ds(i * T, T)], f_ve, halfneg[:, 0:T], ALU.pow).then_inc(K["e_rs"], 1)
                    pool.wait_ge(K["e_rs"], run(f, "rs") + i + 1)
                    apart(pool)
                loop(pool, NT // T, rstd, ch, 1)
                pool.wait_ge(K["slots_cleared"], 16 * (f + 1))

                def scatter(i):
                    for p in range(2):
                        pool.wait_ge(K["e_xg"], run(f, "xg") + 2 * i + p + 1)
                        apart(pool)
                        for t in range(T):
                            nc.gpsimd.indirect_dma_start(
                                out=slot_x, out_offset=bass.IndirectOffsetOnAxis(ap=f_i4[p][:, t:t + 1], axis=0),
                                in_=f_xg[p][:, t], in_offset=None, bounds_check=E * CAP - 1, oob_is_err=False,
                            ).then_inc(K[f"e_scat{p}"], 16)
                loop(pool, NT // T // 2, scatter)

                pool.wait_ge(K["y_cleared"], 16)

                def scatter_y(i):
                    for q in range(EQ):
                        pool.wait_ge(K["e_ye"], run(f, "ye") + EQ * i + q + 1)
                        apart(pool)
                        for t in range(T):
                            nc.gpsimd.indirect_dma_start(
                                out=token_y, out_offset=bass.IndirectOffsetOnAxis(ap=f_back[q][:, t:t + 1], axis=0),
                                in_=f_ye[q][:, t], in_offset=None, bounds_check=B * S - 1, oob_is_err=False,
                            ).then_inc(K[f"e_st{q}"], 16)
                loop(pool, E // EQ, scatter_y)
            experts_pool(0)
            def add_experts(g, p):
                pool.wait_ge(K[f"e_gath{p}"], v(8 * (g - p) + 16))
                apart(pool)
                gate = f_gk[:, bass.ds(v(g * T), T)].rearrange("p (t o) -> p t o", o=1).broadcast_to([P, T, D])
                ch(nc.gpsimd.tensor_tensor(f_yg[p], f_yg[p], gate, ALU.mult))
                ch.settle()
                apart(pool)
                xr = x1[:, bass.ds(v(g * T + T), T), :]
                nc.gpsimd.tensor_tensor(xr, xr, f_yg[p], ALU.add).then_inc(K["e_x"], 1)
                pool.wait_ge(K["e_x"], v(g + 1))
                apart(pool)

            pool.wait_ge(K["e_routed"], 1)
            add_experts(0, 0)
            pool.wait_ge(K["m_w"], 16 * N_MAMBA)

            def front(b, p):
                pool.wait_ge(K["m_mv"], v(b + 1))
                apart(pool)
                ch(nc.gpsimd.tensor_scalar(m_ve, m_mv[:, :, 1], EPS, None, ALU.add))
                ch.settle()
                nc.gpsimd.tensor_tensor(m_rs, m_ve, halfneg[:, 0:T], ALU.pow).then_inc(K["m_rs"], 1)
                pool.wait_ge(K["m_rs"], v(b + 1))
                if not (isinstance(b, int) and b == B - 1):
                    add_experts(b + 1, 1 - p)
                yield
                pool.wait_ge(K["m_xn"], v(b + 1))
                apart(pool)
                xr = x1[:, bass.ds(v(b * T + T), T), :]
                nc.gpsimd.tensor_tensor(xr, xr, ob.rearrange("p (o d) -> p o d", o=1).broadcast_to([P, T, D]), ALU.add).then_inc(K["m_bias"], 1)
                pool.wait_ge(K["m_bias"], v(b + 1))
                apart(pool)
                yield
                yield
                yield
                yield
                yield
                yield
                yield

            def per_n(x):
                return x.rearrange("p c (h o) -> p c h o", o=1).broadcast_to([P, T, H2, P])

            def back(b, p):
                pool.wait_ge(K["m_dA"], v(b + 1))
                nc.gpsimd.tensor_tensor(m_L, after.rearrange("p (a o n) -> p a o n", a=1, o=1).broadcast_to([P, T, H2, P]),
                                        per_n(m_dA), ALU.mult).then_inc(K["m_L"], 1)
                yield
                pool.wait_ge(K["m_xtoks"], v(b + 1))
                nc.gpsimd.tensor_tensor(m_xdt, m_xtok, per_n(m_dt), ALU.mult).then_inc(K["m_xdt"], 1)
                pool.wait_ge(K["m_xdt"], v(b + 1))
                yield
                pool.wait_ge(K["m_el"], v(b + 1))
                nc.gpsimd.tensor_tensor(m_xst, m_xdt[:, 0:T - 1], m_el[:, 0:T - 1, :, P - 1:P].broadcast_to([P, T - 1, H2, P]), ALU.mult).then_inc(K["m_xst"], 1)
                pool.wait_ge(K["m_erow"], v(b + 1))
                apart(pool)
                c = m_ch[p][:, 3, :].rearrange("p (c o n) -> p c o n", c=T, o=1).broadcast_to([P, T, H2, P])
                nc.gpsimd.tensor_tensor(m_ce, c, m_erow, ALU.mult).then_inc(K["m_ce"], 1)
                pool.wait_ge(K["m_ce"], v(b + 1))
                yield
                yield
                yield
                pool.wait_ge(K["m_ssq"], v(T * b + T))
                apart(pool)
                ch(nc.gpsimd.tensor_scalar(m_rv, m_ssq, 1.0 / (2 * P), EPS, ALU.mult, ALU.add))
                ch.settle()
                nc.gpsimd.tensor_tensor(m_ri, m_rv, halfneg[:, 0:T], ALU.pow).then_inc(K["m_ri"], 1)
                pool.wait_ge(K["m_ri"], v(b + 1))
                apart(pool)
                yield
                yield
            mamba(pool, front, back, ch, 6)
            experts_pool(1)

        @block.scalar
        def _(act):
            act.wait_ge(K["constants_ready"], 4)

            def clear_slots():
                act.dma_start(slot_x.rearrange("(t p) d -> p t d", p=P), zeros[:].rearrange("p (o d) -> p o d", o=1).broadcast_to([P, NT, D + 1])).then_inc(K["slots_cleared"], 16)
            clear_slots()
            def copy_xT(g, p):
                act.wait_ge(K["l_xnT"], v(g + 1 + FREE))
                if not at_start(g):
                    act.wait_ge(K["l_proj"], v(NC * (g - 1) + FREE))
                nc.scalar.activation(xT[p].rearrange("p c n -> p (c n)"), ps[:, 6:8, :].rearrange("p a n -> p (a n)"), ACT.Copy).then_inc(K["l_xTs"], 1)

            def evacuate(g, some=range(NC)):
                for c in some:
                    act.wait_ge(K["l_proj"], v(NC * g + c + 1 + FREE))
                    nc.scalar.activation(qkv[:, bass.ds(g, 1), c, :].rearrange("p o d -> p (o d)"), ps[:, c % 4, 0:3 * D], ACT.Copy).then_inc(K["l_qkv"], 1)

            copy_xT(0, 0)
            nt = 0
            for k in "lg":
                for c in range(4):
                    act.wait_ge(K["weight_transposes"], nt + 1)
                    src = ps[:, nt % 4, 0:P]
                    dst = wT[k][:, c, :] if c < 3 else woT[k][:]
                    if c < 2 and k == "g":
                        src, dst = src.rearrange("p (h d) -> p d h", h=H), dst.rearrange("p (d h) -> p d h", h=H)
                    nc.scalar.activation(dst, src, ACT.Copy).then_inc(K["weight_evacuations"], 1)
                    nt += 1
            act.wait_ge(K["weights_in"], 16 * N_WEIGHTS)
            act.wait_ge(K["weight_transposes"], nt + 1)
            nc.scalar.activation(bias_l[:], ps[:, 4, 0:1], ACT.Identity, bias=b_out_l[:]).then_inc(K["bias_made"], 1)

            copy_xT(1, 1)
            evacuate(0)

            def two(i):
                for p in range(2):
                    copy_xT(2 * i + 2 + p, p)
                    evacuate(2 * i + 1 + p)
            loop(act, PR // 2 - 1, two)

            def local_exp(i):
                act.wait_ge(K["l_shift"], v(i + 1))
                nc.scalar.activation(pe_[:], sx[:], ACT.Exp, scale=SCALE).then_inc(K["l_exp"], 1)

            def local_out(i):
                act.wait_ge(K["l_oT"], v(i + 1 + FREE))
                nc.scalar.activation(oT_l.rearrange("p c n -> p (c n)"), ps[:, 6:8, :].rearrange("p a n -> p (a n)"), ACT.Copy).then_inc(K["l_oTs"], 1)
                act.wait_ge(K["l_out"], v(i + 1))
                for h in range(2):
                    nc.scalar.activation(locT[:, 4 * h:4 * h + 4, bass.ds(i * P, P)], ps[:, h, :].rearrange("p (c n) -> p c n", c=4), ACT.Identity, bias=bias_l[:]).then_inc(K["l_loc"], 1)
            evacuate(PR - 1, range(NC // 2))
            local_exp(0)
            evacuate(PR - 1, range(NC // 2, NC))
            act.dma_start(token_y.rearrange("(t p) d -> p t d", p=P), zeros[:, 0:D].rearrange("p (o d) -> p o d", o=1).broadcast_to([P, NT, D])).then_inc(K["y_cleared"], 16)
            act.wait_ge(K["bias_made"], 1)

            def local(i):
                act.wait_ge(K["l_prod_pool"], v(len(POOL_PV) * (i + 1)))
                local_exp(i + 1)
                local_out(i)
            loop(act, PR - 1, local)
            local_out(PR - 1)
            act.wait_ge(K["l_loc"], 2 * PR + FREE)

            act.sem_inc(K["exp"], SC)

            def m_wait(b, k):
                act.wait_ge(K["m_full"], v(m_base(b) + k + 1))

            def copy_x(c):
                nc.scalar.activation(xs[:], locT[:, bass.ds(v(c), 1), :].rearrange("p o n -> p (o n)"), ACT.Copy).then_inc(K["xs"], 1)

            def qk_evac(c, w):
                act.wait_ge(K["stored"], v(32 * c))
                nc.scalar.activation(ff[w][:], ps[:, M, :], ACT.Identity, bias=b_qk_g[:, w:w + 1]).then_inc(K["m_free"], 1)
                act.wait_ge(K["m_free"], v(act_now[0]))
                nc.scalar.activation(parts[w][:, 0], ff[w][:], ACT.Copy).then_inc(K["p1"], 1)

            def v_evac(c, r):
                act.wait_ge(K["pv"], v(free_at(c)))
                nc.scalar.activation(va[r][:, :, :, 0:HD], ps[:, M, :].rearrange("p (t h d) -> p t h d", t=T, h=H), ACT.Copy).then_inc(K["m_free"], 1)

            def mrow_copy(b, r, g):
                n_ = NPART * NJ
                if g >= 2:
                    act.wait_ge(K[f"mr{g - 2}"], v(16 * (b + 1) + FREE))
                else:
                    act.wait_ge(K[f"mr{g + 2}"], v(16 * b + FREE))
                nc.scalar.activation(mrow[g % 2][0:n_, :], ps_mb[0:n_, 0:S], ACT.Copy).then_inc(K["m_free"], 1)
                act.wait_ge(K["m_free"], v(act_now[0]))
                act.dma_start(qpk[r][PROD:KA, g * NJ:(g + 1) * NJ, :], mrow[g % 2][0:n_, :]).then_inc(K[f"mr{g}"], 16)

            act_now = [0]
            act.wait_ge(K["values_ready"], R)
            k = 0
            for c in range(2):
                copy_x(c)
                for t in "qkv":
                    act.wait_ge(K["m_full"], v(k + 1))
                    k += 1
                    act_now[0] = k
                    if t == "v":
                        v_evac(c, c)
                    else:
                        qk_evac(c, "qk".index(t))
            for g in range(3):
                act.wait_ge(K["m_full"], v(k + 1))
                k += 1
                act_now[0] = k
                mrow_copy(0, 0, g)

            def half(b, r, n_next, n_after):
                todo = tasks(n_next, n_after)
                at = {t: k for k, (_, t) in enumerate(todo)}

                def evac_ou(g, before):
                    act.wait_ge(K["pv"], v(PV0 + STEPS * b + 4 * (g + 1)))
                    act.wait_ge(K["m_full"], v(before))
                    nc.scalar.activation(ou[g % 2][:], ps[:, PV, :], ACT.Copy).then_inc(K["ou"], 1)

                for n in range(STEPS):
                    for j in range(NJ):
                        q = 4 * n + j
                        act.wait_ge(K["st"], v(SC * b + q + 1))
                        if j == 0:
                            act.wait_ge(K["pv"], v(PV0 + STEPS * b + n - 1))
                        nc.scalar.activation(eb[q % 8][:], ps[:, ST + q % 3, :], ACT.Exp, scale=SCALE).then_inc(K["exp"], 1)
                    if n == 4:
                        evac_ou(0, m_base(b))
                    if n == 8:
                        evac_ou(1, m_base(b) + at["ot3"] + 1)
                    if n == 12:
                        evac_ou(2, m_base(b) + at["ot0"] + 1)
                    if n == 1 and n_after:
                        copy_x(b + 2)
                    for k, (m, t) in enumerate(todo):
                        if m != n or t[:2] in ("ot", "dd"):
                            continue
                        m_wait(b, k)
                        act_now[0] = m_base(b) + k + 1
                        if t == "mt3":
                            mrow_copy(b, r, 3)
                        elif t[:2] == "mt":
                            mrow_copy(b + 1, (r + 1) % R, int(t[2]))
                        elif t in ("aq", "ak"):
                            qk_evac(b + 2, "qk".index(t[1]))
                        elif t == "av":
                            v_evac(b + 2, (r + 2) % R)
                        elif t == "tt":
                            nc.scalar.activation(onT[:], ps[:, M, :], ACT.Copy).then_inc(K["m_free"], 1)
                evac_ou(3, m_base(b) + at["ot1"] + 1)
            halves(act, half)
            m_wait(B, 1)
            nc.scalar.activation(onT[:], ps[:, M, :], ACT.Copy).then_inc(K["m_free"], 1)

            def setup_mamba():
                for n, (dst, bank, rows, cols) in enumerate(W_EVAC):
                    act.wait_ge(K["m_wT"], n + 1)
                    if n == 0:
                        act.wait_ge(K["m_w"], 16 * N_MAMBA)
                    if n >= 7:
                        nc.scalar.activation(dst, ps[0:rows, bank, 0:cols], ACT.Copy, scale=nw[:, n - 7:n - 6]).then_inc(K["m_wTs"], 1)
                    else:
                        nc.scalar.activation(dst, ps[0:rows, bank, 0:cols], ACT.Copy).then_inc(K["m_wTs"], 1)
                nc.scalar.activation(aneg, alog, ACT.Exp).then_inc(K["m_cst"], 1)

            def experts_act(f):
                def front(i):
                    for p in range(2):
                        act.wait_ge(K["e_xnT"], run(f, "xnT") + 2 * i + p + 1)
                        act.wait_ge(K["e_logits"], run(f, "logits") + 2 * i)
                        nc.scalar.activation(f_xT[p], ps[:, p, :], ACT.Copy).then_inc(K["e_xTs"], 1)
                loop(act, NT // T // 2, front)
                act.wait_ge(K["e_shift"], run(f, "shift") + 1)
                nc.scalar.activation(f_ex, f_lg, ACT.Exp).then_inc(K["e_exp"], 1)
                if f == 0:
                    setup_mamba()
                act.wait_ge(K["e_exp_b"], run(f, "exp_b") + 32)

                def expert(i):
                    for p in range(2):
                        e = 2 * i + p
                        act.wait_ge(K["e_xe_T"], run(f, "xe_T") + e + 1)
                        act.wait_ge(K["e_h"], run(f, "h") + 2 * i)
                        nc.scalar.activation(f_xeT[p], ps[:, p, :], ACT.Copy).then_inc(K["e_xeTs"], 1)
                        act.wait_ge(K["e_h"], run(f, "h") + e + 1)
                        nc.scalar.activation(f_hT[p], ps[:, 2 + p, :], ACT.Relu, bias=f_b1[:, bass.ds(e, 1)]).then_inc(K["e_hT"], 1)
                loop(act, E // 2, expert)
            experts_act(0)
            for q in range(EQ):
                act.wait_ge(K[f"e_ex{q}"], run(1, f"ex{q}"))
            clear_slots()

            def front(b, p):
                yield
                act.wait_ge(K["m_xT"], v(b + 1))
                act.wait_ge(K["m_z"], v(T * b))
                nc.scalar.activation(m_xT, ps[:, 0, :], ACT.Copy).then_inc(K["m_xTs"], 1)
                act.wait_ge(K["m_silu"], v(4 * b))
                act.wait_ge(K["m_cw"], 2)
                yield
                for c in range(4):
                    act.wait_ge(K["m_proj"], v(4 * b + c + 1))
                    nc.scalar.activation(m_acc[:, c], ps[:, (1 + c) % 3, :], ACT.Identity, bias=cb[:, c:c + 1], scale=cw[:, c, TAPS - 1:TAPS]).then_inc(K["m_acc"], 1)
                    if c >= 1:
                        act.wait_ge(K["m_conv"], v(4 * b + c))
                        nc.scalar.activation(m_th[:, c - 1], m_acc[:, c - 1], ACT.Tanh).then_inc(K["m_th"], 1)
                    yield
                act.wait_ge(K["m_conv"], v(4 * b + 4))
                nc.scalar.activation(m_th[:, 3], m_acc[:, 3], ACT.Tanh).then_inc(K["m_th"], 1)
                for t in range(T):
                    act.wait_ge(K["m_z"], v(T * b + t + 1))
                    nc.scalar.activation(m_zt[:, t], ps[:, (5 + t) % 3, 0:2 * P], ACT.Tanh, scale=0.5).then_inc(K["m_zt"], 1)
                act.wait_ge(K["m_abs"], v(b + 1))
                nc.scalar.activation(m_u, m_abs, ACT.Exp, scale=-1.0).then_inc(K["m_u"], 1)
                yield
                yield

            def back(b, p):
                act.wait_ge(K["m_xtok"], v(b + 1))
                nc.scalar.activation(m_xtok.rearrange("p c h n -> p (c h n)"), ps[:, 3:5, :].rearrange("p a n -> p (a n)"), ACT.Copy).then_inc(K["m_xtoks"], 1)
                act.wait_ge(K["m_btok"], v(b + 1))
                nc.scalar.activation(m_btok.rearrange("p c n -> p (c n)"), ps[:, 5, :], ACT.Copy).then_inc(K["m_btoks"], 1)
                yield
                yield
                act.wait_ge(K["m_dif"], v(b + 1))
                nc.scalar.activation(m_el.rearrange("p c h n -> p (c h n)"), ps[:, 5:7, :].rearrange("p a n -> p (a n)"), ACT.Exp).then_inc(K["m_el"], 1)
                act.wait_ge(K["m_row"], v(b + 1))
                nc.scalar.activation(m_erow.rearrange("p c h n -> p (c h n)"), ps[:, 3:5, :].rearrange("p a n -> p (a n)"), ACT.Exp).then_inc(K["m_erow"], 1)
                yield
                yield
                yield
                act.wait_ge(K["m_y"], v(b + 1))
                for t in range(T):
                    nc.scalar.activation(m_sq, m_y[:, t], ACT.Square, accum_out=m_ssq[:, t:t + 1]).then_inc(K["m_ssq"], 1)
                    act.wait_ge(K["m_ssq"], v(T * b + t + 1))
                act.wait_ge(K["m_yT"], v(b + 1))
                nc.scalar.activation(m_yT.rearrange("p a n -> p (a n)"), ps[:, 5:7, :].rearrange("p a n -> p (a n)"), ACT.Copy).then_inc(K["m_yTs"], 1)
                yield
                yield
            mamba(act, front, back)
            experts_act(1)

        @block.vector
        def _(dve):
            ch = Chain(dve, "dve_chain")
            for t_ in (upto, uptob):
                nc.vector.memset(t_[:], 1.0).then_inc(K["upto_ones"], 1)
            nc.vector.memset(zeros[:], 0.0).then_inc(K["constants_ready"], 1)
            nc.vector.memset(halfneg[:], -0.5).then_inc(K["constants_ready"], 1)
            nc.vector.memset(ones_row[:], 1.0).then_inc(K["constants_ready"], 1)
            nc.vector.memset(eps[:], EPS).then_inc(K["constants_ready"], 1)

            dve.wait_ge(K["moe_const"], 2)
            nc.vector.memset(onesb[:], 1.0).then_inc(K["ones_made"], 1)
            ch(nc.vector.memset(not_first[:], 1.0))
            ch.settle()
            ch(nc.vector.memset(not_first[:, :, 0:1], 0.0))
            for e in range(E):
                nc.vector.memset(prefer[:, e:e + 1], float(E - e)).then_inc(K["moe_const"], 1)
                nc.vector.memset(first_slot[:, e:e + 1], float(e * CAP)).then_inc(K["moe_const"], 1)

            def stats(i, p):
                dve.wait_ge(K[f"lxb_in{p}"], v(32 * (i + 1)))
                for c in range(NC):
                    ch(nc.vector.bn_stats(st6[:, c], xb[p][:, c]))
                ch.settle()
                apart(dve)
                for c in range(NC):
                    last = nc.vector.bn_aggr(mv[p][:, c], st6[:, c])
                    if c < NC - 1:
                        ch(last)
                last.then_inc(K["l_mv"], 1)
                dve.wait_ge(K["l_rs"], v(2 * i + p + 1))
                dve.wait_ge(K["l_xnT"], v(2 * i + FREE))
                for c in range(NC):
                    last = nc.vector.tensor_scalar(xn[p][:, c], xb[p][:, c], mv[p][:, c, 0:1], rs[p][:, c:c + 1], ALU.subtract, ALU.mult)
                    if c < NC - 1:
                        ch(last)
                last.then_inc(K["l_xn"], 1)
                dve.wait_ge(K["l_xn"], v(2 * i + p + 1))
            loop(dve, 2, lambda i: [stats(i, p) for p in range(2)], ch, 2 * (3 * NC - 2))
            nc.vector.memset(ou[1][:], 1.0).then_inc(K["dummy_ready"], 1)
            nc.vector.memset(on[:], 1.0).then_inc(K["dummy_ready"], 1)
            nc.vector.memset(x1[:, 0:T], 0.0).then_inc(K["dummy_ready"], 1)
            dve.wait_ge(K["weights_in"], 16 * N_WEIGHTS)
            dve.wait_ge(K["weight_transposes"], 10)
            nc.vector.tensor_tensor(bias_g[:], ps[:, 5, 0:D], b_out_g[:], ALU.add).then_inc(K["bias_made"], 1)

            def reduce_product(i, c, src):
                return nc.vector.tensor_reduce(sc[:, c].rearrange("p h c -> p c h"), src.rearrange("p c (h d) -> p c h d", h=H), AX.X, ALU.add)

            def own_qk(i, some, held):
                for n in some:
                    c = DVE_QK[n]
                    ch(qk_product(nc.vector, i, c, held[n % 2]))
                    ch.settle()
                    ch(reduce_product(i, c, held[n % 2]))

            def pool_qk(i, some):
                for n in some:
                    dve.wait_ge(K["l_prod_qk"], v(len(POOL_QK) * i + n + 1))
                    reduce_product(i, POOL_QK[n], qk_p[n % 2]).then_inc(K["l_qk_used"], 1)

            def first_qk(i, held):
                dve.wait_ge(K["l_qkv"], v(NC * (i + 1) + FREE))
                own_qk(i, range(2), held)
                pool_qk(i, range(2))
                own_qk(i, range(2, len(DVE_QK)), held)

            def shift(i):
                ch.settle()
                dve.wait_ge(K["l_qk_used"], v(len(POOL_QK) * (i + 1)))
                ch(nc.vector.tensor_reduce(smax[:], sc[:], AX.X, ALU.max))
                ch.settle()
                nc.vector.tensor_tensor(sx[:], sc[:], bc(smax, NC), ALU.subtract).then_inc(K["l_shift"], 1)

            def own_pv(i):
                dve.wait_ge(K["l_exp"], v(i + 1))
                for n, c in enumerate(DVE_PV):
                    pv_product(nc.vector, i, c, prod_d[n]).then_inc(K["l_prod_dve"], 1)
                ch(nc.vector.tensor_reduce(ssum[:], pe_[:], AX.X, ALU.add))
                ch.settle()
                ch(nc.vector.reciprocal(srec[:], ssum[:]))
                ch.settle()

            def normalise_l(i):
                dve.wait_ge(K["l_acc"], v(NC * (i + 1) + FREE))
                dve.wait_ge(K["l_oT"], v(i + FREE))
                nc.vector.tensor_tensor(o_l.rearrange("p c (h d) -> p c h d", h=H), ps[:, 4:6, :].rearrange("p a (c h d) -> p (a c) h d", h=H, d=HD), bc(srec, HD), ALU.mult).then_inc(K["l_o"], 1)

            n_qk = len(POOL_QK)
            dve.wait_ge(K["l_xn"], PR)
            first_qk(0, prod_d)
            pool_qk(0, range(2, n_qk))
            shift(0)
            dve.wait_ge(K["l_xnT"], PR + FREE)
            dve.wait_ge(K["l_qkv"], NC * (PR - 1) + FREE)

            def local(i):
                own_pv(i)
                first_qk(i + 1, qk_d)
                pool_qk(i + 1, range(2, n_qk - 1))
                normalise_l(i)
                pool_qk(i + 1, range(n_qk - 1, n_qk))
                shift(i + 1)
            loop(dve, PR - 1, local, ch, 2 * len(DVE_QK) + 1 + 2)
            own_pv(PR - 1)
            normalise_l(PR - 1)

            dve.sem_inc(K["max"], MAX0)
            dve.wait_ge(K["l_loc"], 2 * PR + FREE)
            dve.wait_ge(K["dummy_ready"], 3)
            dve.wait_ge(K["x1_biased"], 1)

            def maxes(b, r, n):
                for s in range(4 * n, 4 * n + 4):
                    g, qt, j = s // 16, s // 4 % 4, s % 4
                    dve.wait_ge(K["s"], v(SC * b + s + 1))
                    nc.vector.tensor_reduce(mx[r][:, qt, g * NJ + j:g * NJ + j + 1], ps[:, SS + s % 3, :], AX.X, ALU.max).then_inc(K["max"], 1)

            def normalise(b, k, g, seen):
                dve.wait_ge(K["m_full"], v(m_base(b) + k + 1))
                o = ps[:, M, :].rearrange("p (t j c) -> p t j c", t=T, j=NJ)
                nc.vector.reciprocal(rc.rearrange("p t (j o) -> p t j o", o=1), o[:, :, :, HD:HD + 1]).then_inc(K["rc"], 1)
                dve.wait_ge(K["rc"], v(NG * b + seen))
                nc.vector.tensor_tensor(on[:, :, g * NJ * HD:(g + 1) * NJ * HD].rearrange("p t (j d) -> p t j d", j=NJ), o[:, :, :, 0:HD], bc(rc, HD), ALU.mult).then_inc(K["m_free"], 1)
                dve.wait_ge(K["m_free"], v(m_base(b) + k + 1))

            def residual(b, k, s0):
                dve.wait_ge(K["m_full"], v(m_base(b) + k + 1))
                xd = x1[:, bass.ds(v(s0 * T), T), :]
                nc.vector.tensor_tensor(xd, ps[:, M, :].rearrange("p (t d) -> p t d", t=T), xd, ALU.add).then_inc(K["m_free"], 1)

            for c in range(2):
                dve.wait_ge(K["p1"], 2 * c + 2)
                ch(nc.vector.tensor_tensor(eb[0], ff[1][:], parts[1][:, 0], ALU.subtract))
                ch.settle()
                ch(nc.vector.tensor_copy(parts[1][:, 1], eb[0]))
                ch.settle()
                nc.vector.tensor_tensor(parts[1][:, 2], eb[0], parts[1][:, 1], ALU.subtract).then_inc(K["parts_k"], 1)
                dve.wait_ge(K["parts_k"], c + 1)
            for n in range(STEPS):
                maxes(0, 0, n)

            def half(b, r, n_next, n_after):
                seen = 0
                todo = tasks(n_next, n_after)
                for n in range(STEPS):
                    if n_next:
                        maxes(b + 1, (r + 1) % R, n)
                    for k, (m, t) in enumerate(todo):
                        if m != n:
                            continue
                        if t[:2] == "ot":
                            seen += 1
                            normalise(b, k, int(t[2]), seen)
                        elif t == "dd":
                            residual(b, k, b)
            halves(dve, half)
            normalise(B, 0, 3, 1)
            residual(B, 2, B)
            dve.wait_ge(K["m_free"], v(m_base(B) + 3))
            dve.wait_ge(K["moe_const"], 18)
            dve.wait_ge(K["numbers_ready"], 1)

            def setup_mamba():
                dve.wait_ge(K["m_w"], 16 * N_MAMBA)
                nc.vector.tensor_scalar(cw, cwf, 0.5, None, ALU.mult).then_inc(K["m_cw"], 1)
                nc.vector.tensor_scalar(cb, cbf, 0.5, None, ALU.mult).then_inc(K["m_cw"], 1)
                dve.wait_ge(K["m_cw"], 2)
                dve.wait_ge(K["m_cst"], 1)
                ch(nc.vector.tensor_scalar(aneg, aneg, -1.0, None, ALU.mult))
                ch(nc.vector.tensor_scalar(after, upto[:], -1.0, 1.0, ALU.mult, ALU.add))
                ch.settle()

            def experts_dve(f):
                def row(g, t):
                    return x1[:, bass.ds(T + g * T + t, 1), :].rearrange("p o d -> p (o d)")

                def stats(g):
                    for t in range(T):
                        ch(nc.vector.bn_stats(f_st[:, t], row(g, t)))
                    ch.settle()
                    apart(dve)
                    for t in range(T):
                        ch(nc.vector.bn_aggr(f_mv4[:, t], f_st[:, t]))
                    ch.settle()
                    nc.vector.tensor_copy(f_mv[:, bass.ds(g * T, T), :], f_mv4).then_inc(K["e_mv"], 1)

                def normalised(g, p):
                    dve.wait_ge(K["e_rs"], run(f, "rs") + g + 1)
                    dve.wait_ge(K["e_xnT"], run(f, "xnT") + g - p)
                    for t in range(T):
                        last = nc.vector.tensor_scalar(f_xn[p][:, t], row(g, t),
                                                       f_mv[:, bass.ds(g * T + t, 1), 0], f_rs[:, bass.ds(g * T + t, 1)], ALU.subtract, ALU.mult)
                        if t < T - 1:
                            ch(last)
                    last.then_inc(K["e_xn"], 1)

                stats(0)

                def two(i):
                    for p in range(2):
                        stats(2 * i + p + 1)
                        normalised(2 * i + p, p)
                loop(dve, (NT // T) // 2 - 1, two, ch, 2 * (3 * T - 1))
                stats((NT // T) - 1)
                normalised((NT // T) - 2, 0)
                normalised((NT // T) - 1, 1)

                def te(x):
                    return x.rearrange("p e t -> p t e")

                def over_e(x):
                    return x.rearrange("p (t o) -> p t o", o=1).broadcast_to([P, NT, E])

                def over_t(x):
                    return x[:, :].rearrange("p (o e) -> p o e", o=1).broadcast_to([P, NT, E])

                def do(ins):
                    ch(ins)
                    ch.settle()
                dve.wait_ge(K["e_logits"], run(f, "logits") + NT // T)
                do(nc.vector.tensor_tensor(f_lg, ps[:, 4, 0:NT * E].rearrange("p (t e) -> p t e", e=E), over_t(br), ALU.add))
                do(nc.vector.tensor_reduce(f_m, f_lg, AX.X, ALU.max))
                nc.vector.tensor_tensor(f_lg, f_lg, over_e(f_m), ALU.subtract).then_inc(K["e_shift"], 1)
                dve.wait_ge(K["e_shift"], run(f, "shift") + 1)
                do(nc.vector.tensor_scalar(f_pick, f_lg, 0.0, None, ALU.is_equal))
                do(nc.vector.tensor_tensor(f_pick, f_pick, over_t(prefer), ALU.mult))
                do(nc.vector.tensor_reduce(f_m, f_pick, AX.X, ALU.max))
                do(nc.vector.tensor_tensor(te(f_one), f_pick, over_e(f_m), ALU.is_equal))
                nc.vector.tensor_copy(f_oneb, f_one).then_inc(K["e_onehot"], 1)
                dve.wait_ge(K["e_exp"], run(f, "exp") + 1)
                do(nc.vector.tensor_reduce(f_sum, f_ex, AX.X, ALU.add))
                do(nc.vector.reciprocal(f_gate, f_sum))
                ch(nc.vector.tensor_tensor(f_rg, f_rs, f_gate, ALU.mult))
                dve.wait_ge(K["e_counts"], run(f, "counts") + 1)
                do(nc.vector.tensor_tensor_scan(f_incl, not_first[:].rearrange("p e t -> p (e t)"), ps[:, 6, 0:E * NT], 0.0, ALU.mult, ALU.add))
                pos = f_pos.rearrange("p e t -> p (e t)")
                do(nc.vector.tensor_tensor(pos, ps[:, 5, 0:E * NT], f_incl, ALU.add))
                do(nc.vector.scalar_tensor_tensor(pos, ps[:, 6, 0:E * NT], -1.0, pos, ALU.mult, ALU.add))
                do(nc.vector.tensor_tensor(f_pos, f_pos, f_one, ALU.mult))
                do(nc.vector.tensor_reduce(f_at, te(f_pos), AX.X, ALU.add))
                do(nc.vector.tensor_tensor(te(f_pos), te(f_one), over_t(first_slot), ALU.mult))
                do(nc.vector.tensor_reduce(f_e0, te(f_pos), AX.X, ALU.add))
                do(nc.vector.tensor_scalar(f_keep, f_at, float(CAP), None, ALU.is_lt))
                do(nc.vector.tensor_tensor(f_gk, f_gate, f_keep, ALU.mult))
                do(nc.vector.tensor_tensor(f_slot, f_at, f_keep, ALU.mult))
                do(nc.vector.tensor_tensor(f_gi, f_e0, f_slot, ALU.add))
                do(nc.vector.tensor_scalar(f_si, f_keep, -float(2 * E * CAP), float(2 * E * CAP), ALU.mult, ALU.add))
                nc.vector.tensor_tensor(f_si, f_si, f_gi, ALU.add).then_inc(K["e_routed"], 1)
                dve.wait_ge(K["e_routed"], run(f, "routed") + 1)


                def rows(i):
                    for p in range(2):
                        g = 2 * i + p
                        if not at_start(i):
                            dve.wait_ge(K[f"e_scat{p}"], run(f, f"scat{p}") + 16 * T * i)
                        for t in range(T):
                            ch(nc.vector.tensor_scalar(f_xg[p][:, t, 0:D], x1[:, bass.ds(T + g * T + t, 1), :].rearrange("p o d -> p (o d)"),
                                                       f_mv[:, bass.ds(g * T + t, 1), 0], f_rg[:, bass.ds(g * T + t, 1)], ALU.subtract, ALU.mult))
                        ch(nc.vector.tensor_copy(f_xg[p][:, :, D], number[:, bass.ds(g * T, T)]))
                        ch.settle()
                        nc.vector.tensor_copy(f_i4[p], f_si[:, bass.ds(g * T, T)]).then_inc(K["e_xg"], 1)
                rows(0)
                loop(dve, NT // T // 2 - 1, lambda i: rows(i + 1), ch, 2 * (T + 1))

                if f == 0:
                    setup_mamba()
                dve.wait_ge(K["e_exp_b"], run(f, "exp_b") + 32)

                for e in range(E):
                    p, q = e % 2, e % EQ
                    if e >= EQ:
                        dve.wait_ge(K[f"e_st{q}"], run(f, f"st{q}") + 16 * T * (e // EQ))
                    dve.wait_ge(K[f"e_ex{q}"], run(f, f"ex{q}") + 48 * (e // EQ + 1))
                    numbers = f_xe[q][:, :, D]
                    ch(nc.vector.tensor_scalar(f_none, numbers, 0.0, float(2 * B * S), ALU.is_equal, ALU.mult))
                    ch.settle()
                    ch(nc.vector.scalar_tensor_tensor(f_back[q], numbers, -1.0, f_none, ALU.add, ALU.add))
                    dve.wait_ge(K["e_y"], run(f, "y") + e + 1)
                    ch.settle()
                    nc.vector.tensor_tensor(f_ye[q], ps[:, 4 + p, :].rearrange("p (t d) -> p t d", t=T),
                                            f_b2[:, e:e + 1, :].broadcast_to([P, T, D]), ALU.add).then_inc(K["e_ye"], 1)


            def add_experts(f, g, p):
                dve.wait_ge(K[f"e_gath{p}"], v(run(f, f"gath{p}") + 8 * (g - p) + 16))
                for t in range(T):
                    xr = x1[:, bass.ds(v(T + g * T + t), 1), :].rearrange("p o d -> p (o d)")
                    last = nc.vector.scalar_tensor_tensor(xr, f_yg[p][:, t], f_gk[:, bass.ds(v(g * T + t), 1)], xr, ALU.mult, ALU.add)
                    if t < T - 1:
                        ch(last)
                last.then_inc(K["e_x"], 1)
                dve.wait_ge(K["e_x"], v(run(f, "x") + g + 1))
            experts_dve(0)

            def do(ins):
                ch(ins)
                ch.settle()

            def front(b, p):
                dve.wait_ge(K["e_x"], v(b + 1))
                for t in range(T):
                    ch(nc.vector.bn_stats(m_st[:, t], x1[:, bass.ds(v(b * T + (T + t)), 1), :].rearrange("p o d -> p (o d)")))
                ch.settle()
                apart(dve)
                for t in range(T):
                    last = nc.vector.bn_aggr(m_mv[:, t], m_st[:, t])
                    if t < T - 1:
                        ch(last)
                last.then_inc(K["m_mv"], 1)
                yield
                dve.wait_ge(K["m_rs"], v(b + 1))
                dve.wait_ge(K["m_xT"], v(b))
                for t in range(T):
                    last = nc.vector.tensor_scalar(m_xn[:, t], x1[:, bass.ds(v(b * T + (T + t)), 1), :].rearrange("p o d -> p (o d)"),
                                                   m_mv[:, t, 0:1], m_rs[:, t:t + 1], ALU.subtract, ALU.mult)
                    if t < T - 1:
                        ch(last)
                last.then_inc(K["m_xn"], 1)
                yield

                def conv(c):
                    dve.wait_ge(K["m_acc"], v(4 * b + c + 1))
                    for k in range(TAPS - 2, -1, -1):
                        j = TAPS - 1 - k
                        last = nc.vector.scalar_tensor_tensor(m_acc[:, c, j:], ps[:, (1 + c) % 3, 0:S - j], cw[:, c, k:k + 1], m_acc[:, c, j:], ALU.mult, ALU.add)
                        if k:
                            ch(last)
                            ch.settle()
                    last.then_inc(K["m_conv"], 1)

                def silu(c):
                    dve.wait_ge(K["m_th"], v(4 * b + c + 1))
                    nc.vector.scalar_tensor_tensor(m_ch[p][:, c], m_th[:, c], 1.0, m_acc[:, c], ALU.add, ALU.mult).then_inc(K["m_silu"], 1)
                for c in range(4):
                    conv(c)
                    if c:
                        silu(c - 1)
                    yield
                silu(3)
                for t in range(T):
                    dve.wait_ge(K["m_zt"], v(T * b + t + 1))
                    z = ps[:, (5 + t) % 3, :]
                    ch(nc.vector.tensor_tensor(m_raw[p][:, t], z[:, 2 * P:2 * P + H2], dtb, ALU.add))
                    nc.vector.scalar_tensor_tensor(m_g[p][:, t], m_zt[:, t], 1.0, z[:, 0:2 * P], ALU.add, ALU.mult).then_inc(K["m_zg"], 1)
                ch.settle()
                do(nc.vector.tensor_scalar(m_abs, m_raw[p], -1.0, None, ALU.mult))
                nc.vector.tensor_tensor(m_abs, m_abs, m_raw[p], ALU.max).then_inc(K["m_abs"], 1)
                ch(nc.vector.tensor_scalar(m_pos, m_raw[p], 0.0, None, ALU.max))
                yield
                dve.wait_ge(K["m_u"], v(b + 1))
                do(nc.vector.tensor_scalar(m_s, m_u, 2.0, None, ALU.add))
                do(nc.vector.reciprocal(m_s, m_s))
                do(nc.vector.tensor_tensor(m_s, m_s, m_u, ALU.mult))
                do(nc.vector.tensor_tensor(m_s2, m_s, m_s, ALU.mult))
                do(nc.vector.tensor_scalar(m_q, m_s2, 1.0 / 17, None, ALU.mult))
                for d in (15, 13, 11, 9, 7, 5, 3):
                    do(nc.vector.scalar_tensor_tensor(m_q, m_q, 1.0 / d, m_s2, ALU.add, ALU.mult))
                do(nc.vector.scalar_tensor_tensor(m_q, m_q, 1.0, m_s, ALU.add, ALU.mult))
                do(nc.vector.scalar_tensor_tensor(m_dt, m_q, 2.0, m_pos, ALU.mult, ALU.add))
                nc.vector.tensor_tensor(m_dA, m_dt, aneg.rearrange("p (o h) -> p o h", o=1).broadcast_to([P, T, H2]), ALU.mult).then_inc(K["m_dA"], 1)
                yield


            def residual_m(b):
                dve.wait_ge(K["m_out"], v(b + 1))
                dve.wait_ge(K["m_ri"], v(b + 1))
                dve.wait_ge(K["m_bias"], v(b + 1))
                for t in range(T):
                    xr = x1[:, bass.ds(v(b * T + (T + t)), 1), :].rearrange("p o d -> p (o d)")
                    last = nc.vector.scalar_tensor_tensor(xr, ps[:, 7, t * P:(t + 1) * P], m_ri[:, t:t + 1], xr, ALU.mult, ALU.add)
                    if t < T - 1:
                        ch(last)
                last.then_inc(K["m_x"], 1)

            def back(b, p):
                yield
                if not at_start(b):
                    residual_m(b - 1)
                dve.wait_ge(K["m_g"], v(b + 1))
                nc.vector.tensor_tensor(m_gm, ps[:, 6, :].rearrange("p (c n) -> p c n", c=T), upto[:].rearrange("p (o n) -> p o n", o=1).broadcast_to([P, T, P]), ALU.mult).then_inc(K["m_gm"], 1)
                yield
                dve.wait_ge(K["m_el"], v(b + 1))
                dve.wait_ge(K["m_gm"], v(b + 1))
                nc.vector.tensor_tensor(m_m, m_el, m_gm.rearrange("p c (o n) -> p c o n", o=1).broadcast_to([P, T, H2, P]), ALU.mult).then_inc(K["m_m"], 1)
                yield
                dve.wait_ge(K["m_P"], v(b + 1))
                dve.wait_ge(K["m_erow"], v(b + 1))
                do(nc.vector.tensor_copy(m_S[:, 0].rearrange("p h n -> p (h n)"), ps[:, 5, 0:2 * P]))
                for c, part in ((1, ps[:, 5, 2 * P:4 * P]), (2, ps[:, 7, 2 * P:4 * P])):
                    for h in range(H2):
                        last = nc.vector.scalar_tensor_tensor(m_S[:, c, h], m_S[:, c - 1, h], m_erow[:, c, h, P - 1:P], part[:, h * P:(h + 1) * P], ALU.mult, ALU.add)
                        if (c, h) != (2, H2 - 1):
                            ch(last)
                    if c == 1:
                        ch.settle()
                last.then_inc(K["m_S"], 1)
                yield
                dve.wait_ge(K["m_Y"], v(b + 1))
                y = ps[:, 3:5, :].rearrange("p a (c h n) -> p (a c) h n", h=H2, n=P)
                for h in range(H2):
                    nc.vector.scalar_tensor_tensor(m_y1[:, :, h], m_xtok[:, :, h], dpar[:, h:h + 1], y[:, :, h], ALU.mult, ALU.add).then_inc(K["m_y1"], 1)
                dve.wait_ge(K["m_y1"], v(2 * b + 2 + FREE))
                nc.vector.scalar_tensor_tensor(m_y.rearrange("p c n -> p (c n)"), m_g[p].rearrange("p c n -> p (c n)"), 0.5, m_y1.rearrange("p c h n -> p (c h n)"), ALU.mult, ALU.mult).then_inc(K["m_y"], 1)
                yield
                yield
                yield
            mamba(dve, front, back, ch, 90)
            residual_m(B - 1)
            dve.wait_ge(K["m_x"], B + FREE)
            experts_dve(1)

            def back(i):
                for p in range(2):
                    add_experts(1, 2 * i + p, p)
            loop(dve, B // 2, back, ch, 2 * (T - 1))

        @block.tensor
        def _(pe):
            def transposes_x(g, p):
                pe.wait_ge(K["l_xn"], v(g + 1))
                if not at_start(g):
                    pe.wait_ge(K["l_xTs"], v(g + FREE))
                for c in range(NC):
                    last = nc.tensor.transpose(ps[:, 6 + c // 4, c % 4 * P:(c % 4 + 1) * P], xn[p][:, c], ident[:])
                last.then_inc(K["l_xnT"], 1)

            def project_l(g, p):
                pe.wait_ge(K["l_xTs"], v(g + 1 + FREE))
                for c in range(NC):
                    if c >= 4:
                        pe.wait_ge(K["l_qkv"], v(NC * g + c - 3 + FREE))
                    elif c == 0:
                        pe.wait_ge(K["l_qkv"], v(NC * g + FREE))
                    nc.tensor.matmul(ps[:, c % 4, 0:3 * D], xT[p][:, c], wT["l"][:].rearrange("p c d -> p (c d)"), start=True, stop=False)
                    nc.tensor.matmul(ps[:, c % 4, 0:2 * D], ones_row[:], b_qk_l[:], start=False, stop=True).then_inc(K["l_proj"], 1)

            pe.wait_ge(K["identity_ready"], 1)
            transposes_x(0, 0)
            pe.wait_ge(K["weights_in"], 16 * N_WEIGHTS)
            pe.wait_ge(K["bf_identity_ready"], 1)
            pe.wait_ge(K["constants_ready"], 4)
            nt = 0
            for k in "lg":
                for src in [w_nat[k][:, c, :] for c in range(3)] + [wo_nat[k][:]]:
                    if nt >= 4:
                        pe.wait_ge(K["weight_evacuations"], nt - 3)
                    nc.tensor.transpose(ps[:, nt % 4, 0:P], src, ident[:]).then_inc(K["weight_transposes"], 1)
                    nt += 1
            pe.wait_ge(K["weight_evacuations"], nt)
            nc.tensor.matmul(ps[:, 4, 0:1], woT["l"][:], b_v["l"][:], start=True, stop=True).then_inc(K["weight_transposes"], 1)
            nc.tensor.matmul(ps[:, 5, 0:D], b_v["g"][:].broadcast_to([P, P]), woT["g"][:], start=True, stop=True).then_inc(K["weight_transposes"], 1)

            transposes_x(1, 1)
            project_l(0, 0)

            def two(i):
                for p in range(2):
                    transposes_x(2 * i + 2 + p, p)
                    project_l(2 * i + 1 + p, 1 - p)
            loop(pe, PR // 2 - 1, two)
            project_l(PR - 1, 1)
            pe.wait_ge(K["l_qkv"], NC * PR + FREE)

            def local(i):
                pe.wait_ge(K["l_o"], v(i + FREE))
                for c in range(NC):
                    if c in DVE_PV:
                        n = DVE_PV.index(c)
                        src = prod_d[n]
                        pe.wait_ge(K["l_prod_dve"], v(len(DVE_PV) * i + n + 1))
                    else:
                        n = POOL_PV.index(c)
                        src = prod_p[n]
                        pe.wait_ge(K["l_prod_pool"], v(len(POOL_PV) * i + n + 1))
                    for x in range(NC):
                        last = nc.tensor.matmul(ps[:, 4 + c // 4, c % 4 * P:(c % 4 + 1) * P], ident[:], src[:, x], start=x == 0, stop=x == NC - 1)
                    last.then_inc(K["l_acc"], 1)
                pe.wait_ge(K["l_o"], v(i + 1 + FREE))
                for c in range(NC):
                    last = nc.tensor.transpose(ps[:, 6 + c // 4, c % 4 * P:(c % 4 + 1) * P], o_l[:, c], ident[:])
                last.then_inc(K["l_oT"], 1)
                pe.wait_ge(K["l_oTs"], v(i + 1))
                pe.wait_ge(K["l_loc"], v(2 * i + FREE))
                for h in range(2):
                    last = nc.tensor.matmul(ps[:, h, :], woT["l"][:], oT_l[:, 4 * h:4 * h + 4, :].rearrange("p c n -> p (c n)"), start=True, stop=True)
                last.then_inc(K["l_out"], 1)
            loop(pe, PR, local)

            pe.wait_ge(K["l_loc"], 2 * PR + FREE)
            pe.sem_inc(K["pv"], PV0)

            def project(c, w):
                pe.wait_ge(K["xs"], v(c + 1))
                if w < 2:
                    nc.tensor.matmul(ps[:, M, :], wT["g"][:, w, :], xs[:], start=True, stop=True).then_inc(K["m_full"], 1)
                else:
                    for t in range(T):
                        last = nc.tensor.matmul(ps[:, M, t * P:(t + 1) * P], xs[:, t * P:(t + 1) * P], wT["g"][:, 2, :], start=True, stop=True)
                    last.then_inc(K["m_full"], 1)

            def max_transposes(b, r, g):
                pe.wait_ge(K["nm"], v(NG * b + g + 1))
                for t in range(T):
                    last = nc.tensor.transpose(ps_mb[0:NPART * NJ, t * P:(t + 1) * P], nm[r][:, g, t], identb[:])
                last.then_inc(K["m_full"], 1)

            def out_transposes(b, g):
                pe.wait_ge(K["ou"], v(NG * b + g + 1 + FREE))
                for t in range(T):
                    last = nc.tensor.transpose(ps[:, M, t * P:(t + 1) * P], ou[g % 2][:, t * P:(t + 1) * P], ident[:])
                last.then_inc(K["m_full"], 1)

            def on_transposes():
                for t in range(T):
                    last = nc.tensor.transpose(ps[:, M, t * P:(t + 1) * P], on[:, t], ident[:])
                last.then_inc(K["m_full"], 1)

            def out_projection():
                for t in range(T):
                    last = nc.tensor.matmul(ps[:, M, t * P:(t + 1) * P], onT[:, t * P:(t + 1) * P], woT["g"][:], start=True, stop=True)
                last.then_inc(K["m_full"], 1)

            def scores(b, r, s):
                g, qt, j = s // 16, s // 4 % 4, s % 4
                h = g * NJ + j
                pe.wait_ge(K["max"], v(MAX0 + SC * b + prev_use(s) + 1))
                nc.tensor.matmul(ps[:, SS + s % 3, :], qpk[r][0:PROD, h, qt * P:(qt + 1) * P], kpk[r][0:PROD, h, :], start=True, stop=True).then_inc(K["s"], 1)

            def scores_t(b, r, q):
                g, kt, j = q // 16, q // 4 % 4, q % 4
                h = g * NJ + j
                if q % 16 == 0:
                    pe.wait_ge(K[f"mr{g}"], v(16 * (b + 1) + FREE))
                pe.wait_ge(K["exp"], v(SC + SC * b + prev_use(q) + 1))
                nc.tensor.matmul(ps[:, ST + q % 3, :], kpk[r][:, h, kt * P:(kt + 1) * P], qpk[r][:, h, :], start=True, stop=True).then_inc(K["st"], 1)

            def pv(b, r, n):
                g, kt = n // 4, n % 4
                if kt == 0:
                    pe.wait_ge(K["ou"], v(NG * b + g + FREE))
                pe.wait_ge(K["exp"], v(SC + SC * b + 4 * (n + 1)))
                for j in range(NJ):
                    last = nc.tensor.matmul(ps[32 * j:32 * j + 32, PV, :], va[r][:, kt, g * NJ + j, :], eb[(4 * n + j) % 8][:], start=kt == 0, stop=kt == 3, tile_position=(0, 32 * j))
                last.then_inc(K["pv"], 1)

            k = 0
            for c in range(2):
                for w in range(3):
                    pe.wait_ge(K["m_free"], v(k))
                    project(c, w)
                    k += 1
            pe.wait_ge(K["pk0"], 16 * LOADS)
            for s in range(SC):
                scores(0, 0, s)
            for g in range(3):
                pe.wait_ge(K["m_free"], v(k))
                max_transposes(0, 0, g)
                k += 1
            pe.wait_ge(K["dummy_ready"], 3)
            pe.wait_ge(K["ones_rows"], 16 * R)

            def half(b, r, n_next, n_after, i):
                todo = tasks(n_next, n_after)
                r1 = (r + 1) % R
                for n in range(STEPS):
                    if n == 0 and n_next:
                        pe.wait_ge(K[f"pk{r1}"], v(16 * LOADS * (i + 1 + (1 if r == R - 1 else 0))))
                    for j in range(NJ):
                        scores_t(b, r, 4 * n + j)
                        if n_next:
                            scores(b + 1, r1, 4 * n + j)
                        if j == 1 and n > 0:
                            pv(b, r, n - 1)
                    for k, (m, t) in enumerate(todo):
                        if m != n:
                            continue
                        pe.wait_ge(K["m_free"], v(m_base(b) + k))
                        if t == "mt3":
                            max_transposes(b, r, 3)
                        elif t[:2] == "mt":
                            max_transposes(b + 1, r1, int(t[2]))
                        elif t == "ot3":
                            out_transposes(b - 1, 3)
                        elif t[:2] == "ot":
                            out_transposes(b, int(t[2]))
                        elif t == "tt":
                            on_transposes()
                        elif t == "dd":
                            out_projection()
                        else:
                            project(b + 2, "qkv".index(t[1]))
                pv(b, r, STEPS - 1)

            def three(i):
                for r in range(R):
                    half(Count(i, R, r, pe), r, True, True, i)
            loop(pe, 2, three)
            half(6, 0, True, False, 2)
            half(7, 1, False, False, 2)
            for k, f in enumerate((lambda: out_transposes(B - 1, 3), on_transposes, out_projection)):
                pe.wait_ge(K["m_free"], v(m_base(B) + k))
                f()

            def setup_mamba():
                pe.wait_ge(K["m_w"], 16 * N_MAMBA)
                for n, (src, rows, cols) in enumerate(W_IN):
                    nc.tensor.transpose(ps[0:cols, n % 8, 0:rows] if n < 8 else ps[0:cols, 0, 0:rows], src, ident[0:rows, 0:rows])\
                        .then_inc(K["m_wT"], 1)
                    if n == 7:
                        pe.wait_ge(K["m_wTs"], 1)
                pe.wait_ge(K["m_wTs"], len(W_IN))

            def experts_pe(f):
                def transposes(g, p):
                    pe.wait_ge(K["e_xn"], run(f, "xn") + g + 1)
                    pe.wait_ge(K["e_xTs"], run(f, "xTs") + g - p)
                    for t in range(T):
                        last = nc.tensor.transpose(ps[:, p, t * P:(t + 1) * P], f_xn[p][:, t], ident[:])
                    last.then_inc(K["e_xnT"], 1)

                def logits(g, p):
                    pe.wait_ge(K["e_xTs"], run(f, "xTs") + g + 1)
                    for t in range(T):
                        last = nc.tensor.matmul(ps[:, 4, bass.ds((g * T + t) * E, E)], f_xT[p][:, t * P:(t + 1) * P], wr[:], start=True, stop=True)
                    last.then_inc(K["e_logits"], 1)

                transposes(0, 0)

                def two(i):
                    for p in range(2):
                        transposes(2 * i + p + 1, 1 - p)
                        logits(2 * i + p, p)
                loop(pe, NT // T // 2 - 1, two)
                transposes(NT // T - 1, 1)
                logits(NT // T - 2, 0)
                logits(NT // T - 1, 1)
                pe.wait_ge(K["e_onehot"], run(f, "onehot") + 1)
                one = f_oneb.rearrange("p e t -> p (e t)")
                nc.tensor.matmul(ps[:, 5, 0:E * NT], uptob[:], one, start=True, stop=True)
                nc.tensor.matmul(ps[:, 6, 0:E * NT], onesb[:], one, start=True, stop=True).then_inc(K["e_counts"], 1)
                pe.wait_ge(K["e_routed"], run(f, "routed") + 1)
                if f == 0:
                    setup_mamba()

                def transposes_e(e, q):
                    pe.wait_ge(K[f"e_ex{q}"], run(f, f"ex{q}") + 48 * (e // EQ + 1))
                    pe.wait_ge(K["e_xeTs"], run(f, "xeTs") + e - e % 2)
                    for t in range(T):
                        last = nc.tensor.transpose(ps[:, e % 2, t * P:(t + 1) * P], f_xe[q][:, t, 0:D], ident[:])
                    last.then_inc(K["e_xe_T"], 1)

                def hidden(e, q):
                    pe.wait_ge(K["e_xeTs"], run(f, "xeTs") + e + 1)
                    pe.wait_ge(K["e_hT"], run(f, "hT") + e - e % 2)
                    nc.tensor.matmul(ps[:, 2 + e % 2, :], f_w[q][:, 0], f_xeT[e % 2], start=True, stop=True).then_inc(K["e_h"], 1)

                def outputs(e, q):
                    pe.wait_ge(K["e_hT"], run(f, "hT") + e + 1)
                    pe.wait_ge(K["e_ye"], run(f, "ye") + e - e % 2)
                    for t in range(T):
                        last = nc.tensor.matmul(ps[:, 4 + e % 2, t * P:(t + 1) * P], f_hT[e % 2][:, t * P:(t + 1) * P], f_w[q][:, 1], start=True, stop=True)
                    last.then_inc(K["e_y"], 1)

                for e in range(E + 2):
                    if e < E:
                        transposes_e(e, e % EQ)
                    if 1 <= e <= E:
                        hidden(e - 1, (e - 1) % EQ)
                    if e >= 2:
                        outputs(e - 2, (e - 2) % EQ)
            experts_pe(0)

            def front(b, p):
                yield
                pe.wait_ge(K["m_xn"], v(b + 1))
                pe.wait_ge(K["m_zg"], v(T * b))
                for t in range(T):
                    last = nc.tensor.transpose(ps[:, 0, t * P:(t + 1) * P], m_xn[:, t], ident[:])
                last.then_inc(K["m_xT"], 1)
                pe.wait_ge(K["m_xTs"], v(b + 1))

                def project(c):
                    nc.tensor.matmul(ps[:, (1 + c) % 3, :], wx[:, c], m_xT, start=True, stop=True).then_inc(K["m_proj"], 1)

                def project_z(t):
                    nc.tensor.matmul(ps[:, (5 + t) % 3, 0:2 * P + H2], m_xT[:, t * P:(t + 1) * P], wz, start=True, stop=True).then_inc(K["m_z"], 1)
                for c in range(3):
                    project(c)
                yield
                pe.wait_ge(K["m_conv"], v(4 * b + 1))
                project(3)
                yield
                for t in range(T):
                    if t < 3:
                        pe.wait_ge(K["m_conv"], v(4 * b + 2 + t))
                    else:
                        pe.wait_ge(K["m_zg"], v(T * b + 1))
                    project_z(t)
                    if t < 3:
                        yield
                yield
                yield

            def back(b, p):
                def at(c, h):
                    return ps[:, 3 + c // 2, (c % 2 * 2 + h) * P:(c % 2 * 2 + h + 1) * P]
                pe.wait_ge(K["m_silu"], v(4 * b + 4))
                pe.wait_ge(K["m_y1"], v(2 * b + FREE))
                for c in range(T):
                    for h in range(H2):
                        last = nc.tensor.transpose(at(c, h), m_ch[p][:, h, c * P:(c + 1) * P], ident[:])
                last.then_inc(K["m_xtok"], 1)
                pe.wait_ge(K["m_yTs"], v(b + FREE))
                for c in range(T):
                    last = nc.tensor.transpose(ps[:, 5, c * P:(c + 1) * P], m_ch[p][:, 2, c * P:(c + 1) * P], ident[:])
                last.then_inc(K["m_btok"], 1)
                for c in range(T):
                    last = nc.tensor.matmul(ps[:, 6, c * P:(c + 1) * P], m_ch[p][:, 2, c * P:(c + 1) * P], m_ch[p][:, 3, c * P:(c + 1) * P], start=True, stop=True)
                last.then_inc(K["m_g"], 1)
                yield
                pe.wait_ge(K["m_L"], v(b + 1))
                pe.wait_ge(K["m_btoks"], v(b + 1))
                pe.wait_ge(K["m_gm"], v(b + 1))
                for c in range(T):
                    for h in range(H2):
                        last = nc.tensor.matmul(ps[:, 5 + c // 2, (c % 2 * 2 + h) * P:(c % 2 * 2 + h + 1) * P], m_L[:, c, h], upto[:], start=True, stop=True)
                last.then_inc(K["m_dif"], 1)
                pe.wait_ge(K["m_xtoks"], v(b + 1))
                for c in range(T):
                    for h in range(H2):
                        last = nc.tensor.matmul(at(c, h), m_dA[:, c, h:h + 1].broadcast_to([P, P]), upto[:], start=True, stop=True)
                last.then_inc(K["m_row"], 1)
                yield
                pe.wait_ge(K["m_el"], v(b + 1))
                pe.wait_ge(K["m_x"], v(b + FREE))
                pe.wait_ge(K["m_xst"], v(b + 1))
                for c, dst in enumerate((ps[:, 5, 0:2 * P], ps[:, 5, 2 * P:4 * P], ps[:, 7, 2 * P:4 * P])):
                    last = nc.tensor.matmul(dst, m_btok[:, c], m_xst[:, c].rearrange("p h n -> p (h n)"), start=True, stop=True)
                last.then_inc(K["m_P"], 1)
                yield
                pe.wait_ge(K["m_m"], v(b + 1))
                pe.wait_ge(K["m_xdt"], v(b + 1))
                pe.wait_ge(K["m_erow"], v(b + 1))
                pe.wait_ge(K["m_S"], v(b + 1))
                pe.wait_ge(K["m_ce"], v(b + 1))
                for c in range(T):
                    for h in range(H2):
                        last = nc.tensor.matmul(at(c, h), m_m[:, c, h], m_xdt[:, c, h], start=True, stop=c == 0)
                        if c:
                            last = nc.tensor.matmul(at(c, h), m_ce[:, c, h], m_S[:, c - 1, h], start=False, stop=True)
                last.then_inc(K["m_Y"], 1)
                yield
                yield
                pe.wait_ge(K["m_y"], v(b + 1))
                pe.wait_ge(K["m_gm"], v(b + 1))
                for t in range(T):
                    for k in range(2):
                        last = nc.tensor.transpose(ps[:, 5 + k, t * P:(t + 1) * P], m_y[:, t, k * P:(k + 1) * P], ident[:])
                last.then_inc(K["m_yT"], 1)
                pe.wait_ge(K["m_yTs"], v(b + 1 + FREE))
                for t in range(T):
                    for k in range(2):
                        last = nc.tensor.matmul(ps[:, 7, t * P:(t + 1) * P], m_yT[:, k, t * P:(t + 1) * P], wo2[:, k], start=k == 0, stop=k == 1)
                last.then_inc(K["m_out"], 1)
                yield
                yield
            mamba(pe, front, back)
            experts_pe(1)


N_WEIGHTS = 2 * 3 + 1 + 2 * HD + 2 + 2
N_MAMBA = 11
_INS = (["attn_a_x"] + [f"attn_a_{w}_{k}" for k in "lg" for w in ("w_in", "b_in", "w_out", "b_out")]
        + [f"ffn_{w}" for w in ("Wr", "br", "W1", "b1", "W2", "b2")]
        + [f"attn_b_{w}" for w in ("in_proj_w", "conv_w", "conv_b", "dt_bias", "A_log", "D_param", "norm_w",
                                   "out_proj_w", "out_proj_b")])


def kernel(**inputs):
    import numpy as np
    import concourse.bacc as bacc
    from concourse.bass_utils import run_bass_kernel_spmd

    nc = bacc.Bacc("TRN2", target_bir_lowering=False, num_devices=1)
    arrays, args = {}, {}
    for n in _INS:
        arrays["in_" + n] = np.ascontiguousarray(inputs["L0_" + n])
        args[n] = nc.dram_tensor("in_" + n, arrays["in_" + n].shape, F32, kind="ExternalInput").ap()
    out = nc.dram_tensor("out_0", (B, S, D), F32, kind="ExternalOutput").ap()
    build(nc, args, out)
    r = run_bass_kernel_spmd(nc, [arrays], core_ids=[0])
    return r.results[0]["out_0"]
```
